# Optimizing a Trainium2 kernel written in Bass

```python
import numpy as np
import jax
import jax.numpy as jnp

def _softmax(x, axis=-1):
    return jax.nn.softmax(x, axis=axis)

def _gelu(x):
    return jax.nn.gelu(x, approximate=True)

def _silu(x):
    return jax.nn.silu(x)

def _sigmoid(x):
    return jax.nn.sigmoid(x)

def _layernorm(x, axis=-1, eps=1e-05):
    m = jnp.mean(x, axis=axis, keepdims=True)
    v = jnp.var(x, axis=axis, keepdims=True)
    return (x - m) / jnp.sqrt(v + eps)

def _scatter_add(tgt, idx, src, axis=0):
    return tgt.at[idx].add(src)

def _segment_sum(src, seg, n):
    return jax.ops.segment_sum(src, seg, n)
kernel_name = 'mk_seq_postln_d2_jaxref_r8_98fd07'

def setup_inputs(seed: int=0):
    np.random.seed(seed)
    _w = jnp.asarray

    def _L0_attn_setup():
        import jax, jax.numpy as jnp
        import numpy as np
        B, S, D = (1, 256, 512)
        H = 32
        QL = 192
        KVL = 64
        DN = 128
        DR = 64
        DV = 128
        BASE = 10000.0
        FACTOR = 40.0
        BFAST, BSLOW = (32.0, 1.0)
        OLD_CTX = 4096.0
        MSCALE = 1.0

        def _yarn_inv_freq():
            freqs = 1.0 / BASE ** (jnp.arange(0, DR, 2, dtype=jnp.float32) / DR)
            wavelengths = 2.0 * jnp.pi / freqs
            ramp = jnp.clip((wavelengths / OLD_CTX - BSLOW) / (BFAST - BSLOW), 0.0, 1.0)
            scale = 1.0 - ramp + ramp * FACTOR
            return (freqs / scale, MSCALE)

        def _apply_rope(x, inv_freq, mscale):
            seq = x.shape[-2]
            pos = jnp.arange(seq, dtype=jnp.float32)
            f = jnp.concatenate([pos[:, None] * inv_freq[None, :]] * 2, axis=-1)
            cos = jnp.cos(f) * mscale
            sin = jnp.sin(f) * mscale
            half = DR // 2
            x1, x2 = (x[..., :half], x[..., half:])
            c1, c2 = (cos[:, :half], cos[:, half:])
            s2 = sin[:, half:]
            return jnp.concatenate([x1 * c1 - x2 * s2, x1 * s2 + x2 * c2], axis=-1)
        key = jax.random.key(seed)
        ks = jax.random.split(key, 10)

        def glorot(k, shape):
            lim = np.sqrt(6.0 / (shape[0] + shape[1])).astype(np.float32)
            return jax.random.uniform(k, shape, jnp.float32, -lim, lim)
        return {'hidden_states': jax.random.normal(ks[0], (B, S, D), jnp.float32), 'w_q_down': glorot(ks[1], (D, QL)), 'w_q_up_nope': glorot(ks[2], (QL, H * DN)), 'w_q_up_rope': glorot(ks[3], (QL, H * DR)), 'w_kv_down': glorot(ks[4], (D, KVL)), 'w_k_rope': glorot(ks[5], (D, DR)), 'w_uk': glorot(ks[6], (H * DN, KVL)), 'w_uv': glorot(ks[7], (H * DV, KVL)), 'w_out': glorot(ks[8], (H * DV, D))}
    _L0_attn_in = _L0_attn_setup()

    def _L0_ffn_setup():
        import jax, jax.numpy as jnp
        import numpy as np
        RANKS = (8, 16, 32, 64)
        TOPK = 1
        SCALING = 1.0 / 4
        key = jax.random.key(seed)
        ks = jax.random.split(key, 7)
        D_IN, D_OUT, MAX_R, N_RANKS = (512, 512, 64, len(RANKS))
        B_, S_ = (4, 256)
        return {'hidden_states': jax.random.normal(ks[0], (B_, S_, D_IN), jnp.float32), 'W': jax.random.normal(ks[1], (D_OUT, D_IN), jnp.float32) * 0.02, 'b': jax.random.normal(ks[2], (D_OUT,), jnp.float32) * 0.02, 'A': jax.random.normal(ks[3], (MAX_R, D_IN), jnp.float32) * 0.02, 'B': jnp.zeros((D_OUT, MAX_R), jnp.float32) + jax.random.normal(ks[4], (D_OUT, MAX_R), jnp.float32) * 0.02, 'gate_w': jax.random.normal(ks[5], (N_RANKS, D_IN), jnp.float32) * 0.02, 'gate_b': jax.random.normal(ks[6], (N_RANKS,), jnp.float32) * 0.02}
    _L0_ffn_in = _L0_ffn_setup()

    def _L1_attn_setup():
        import jax, jax.numpy as jnp
        import numpy as np
        import math
        D_MODEL = 512
        N_HEADS = 32
        HEAD_DIM = D_MODEL // N_HEADS
        CLIP_QKV = 8.0
        ALIBI_BIAS_MAX = 8
        LN_EPS = 1e-05

        def _alibi_slopes(total_num_heads: int, alibi_bias_max: int) -> jnp.ndarray:
            next_p2 = 2 ** math.ceil(math.log2(total_num_heads))
            m = jnp.arange(1, next_p2 + 1, dtype=jnp.float32) * (alibi_bias_max / next_p2)
            slopes = 1.0 / jnp.power(2.0, m)
            if next_p2 != total_num_heads:
                slopes = jnp.concatenate([slopes[1::2], slopes[::2]])[:total_num_heads]
            return slopes

        def _layer_norm(x, w, b):
            mu = jnp.mean(x, axis=-1, keepdims=True)
            var = jnp.var(x, axis=-1, keepdims=True)
            return (x - mu) * jax.lax.rsqrt(var + LN_EPS) * w + b
        key = jax.random.key(seed)
        k0, k1, k2 = jax.random.split(key, 3)
        B, S = (2, 256)
        return {'hidden_states': jax.random.normal(k0, (B, S, D_MODEL), dtype=jnp.float32), 'w_qkv': jax.random.normal(k1, (3 * D_MODEL, D_MODEL), dtype=jnp.float32) * 0.02, 'q_ln_w': jnp.ones((D_MODEL,), jnp.float32), 'q_ln_b': jnp.zeros((D_MODEL,), jnp.float32), 'k_ln_w': jnp.ones((D_MODEL,), jnp.float32), 'k_ln_b': jnp.zeros((D_MODEL,), jnp.float32), 'w_out': jax.random.normal(k2, (D_MODEL, D_MODEL), dtype=jnp.float32) * 0.02}
    _L1_attn_in = _L1_attn_setup()

    def _L1_ffn_setup():
        import jax, jax.numpy as jnp
        import numpy as np
        RMS_EPS = 1e-05
        key = jax.random.key(seed)
        k1, k2, k3, k4 = jax.random.split(key, 4)
        B, S, H, I = (1, 256, 512, 1792)
        x = jax.random.normal(k1, (B, S, H), dtype=jnp.float32)
        ln_w = jnp.ones((H,), dtype=jnp.float32)
        gate_w = jax.random.normal(k2, (I, H), dtype=jnp.float32) * 0.02
        up_w = jax.random.normal(k3, (I, H), dtype=jnp.float32) * 0.02
        down_w = jax.random.normal(k4, (H, I), dtype=jnp.float32) * 0.02
        return {'x': x, 'ln_w': ln_w, 'gate_w': gate_w, 'up_w': up_w, 'down_w': down_w}
    _L1_ffn_in = _L1_ffn_setup()
    _d = {'L0_attn_hidden_states': _L0_attn_in['hidden_states'], 'L0_attn_w_q_down': _L0_attn_in['w_q_down'], 'L0_attn_w_q_up_nope': _L0_attn_in['w_q_up_nope'], 'L0_attn_w_q_up_rope': _L0_attn_in['w_q_up_rope'], 'L0_attn_w_kv_down': _L0_attn_in['w_kv_down'], 'L0_attn_w_k_rope': _L0_attn_in['w_k_rope'], 'L0_attn_w_uk': _L0_attn_in['w_uk'], 'L0_attn_w_uv': _L0_attn_in['w_uv'], 'L0_attn_w_out': _L0_attn_in['w_out'], 'L0_ffn_W': _L0_ffn_in['W'], 'L0_ffn_b': _L0_ffn_in['b'], 'L0_ffn_A': _L0_ffn_in['A'], 'L0_ffn_B': _L0_ffn_in['B'], 'L0_ffn_gate_w': _L0_ffn_in['gate_w'], 'L0_ffn_gate_b': _L0_ffn_in['gate_b'], 'L1_attn_w_qkv': _L1_attn_in['w_qkv'], 'L1_attn_q_ln_w': _L1_attn_in['q_ln_w'], 'L1_attn_q_ln_b': _L1_attn_in['q_ln_b'], 'L1_attn_k_ln_w': _L1_attn_in['k_ln_w'], 'L1_attn_k_ln_b': _L1_attn_in['k_ln_b'], 'L1_attn_w_out': _L1_attn_in['w_out'], 'L1_ffn_ln_w': _L1_ffn_in['ln_w'], 'L1_ffn_gate_w': _L1_ffn_in['gate_w'], 'L1_ffn_up_w': _L1_ffn_in['up_w'], 'L1_ffn_down_w': _L1_ffn_in['down_w']}
    _x0 = _d['L0_attn_hidden_states']
    _d['L0_attn_hidden_states'] = jax.random.normal(jax.random.fold_in(jax.random.key(seed), 1), (1, 1024, 512), dtype=_x0.dtype)
    del _x0
    return _d

def reference(L0_attn_hidden_states, L0_attn_w_q_down, L0_attn_w_q_up_nope, L0_attn_w_q_up_rope, L0_attn_w_kv_down, L0_attn_w_k_rope, L0_attn_w_uk, L0_attn_w_uv, L0_attn_w_out, L0_ffn_W, L0_ffn_b, L0_ffn_A, L0_ffn_B, L0_ffn_gate_w, L0_ffn_gate_b, L1_attn_w_qkv, L1_attn_q_ln_w, L1_attn_q_ln_b, L1_attn_k_ln_w, L1_attn_k_ln_b, L1_attn_w_out, L1_ffn_ln_w, L1_ffn_gate_w, L1_ffn_up_w, L1_ffn_down_w):

    def _L0_attn_ref(hidden_states, w_q_down, w_q_up_nope, w_q_up_rope, w_kv_down, w_k_rope, w_uk, w_uv, w_out):
        import jax, jax.numpy as jnp
        import numpy as np
        B, S, D = (1, 256, 512)
        H = 32
        QL = 192
        KVL = 64
        DN = 128
        DR = 64
        DV = 128
        BASE = 10000.0
        FACTOR = 40.0
        BFAST, BSLOW = (32.0, 1.0)
        OLD_CTX = 4096.0
        MSCALE = 1.0

        def _yarn_inv_freq():
            freqs = 1.0 / BASE ** (jnp.arange(0, DR, 2, dtype=jnp.float32) / DR)
            wavelengths = 2.0 * jnp.pi / freqs
            ramp = jnp.clip((wavelengths / OLD_CTX - BSLOW) / (BFAST - BSLOW), 0.0, 1.0)
            scale = 1.0 - ramp + ramp * FACTOR
            return (freqs / scale, MSCALE)

        def _apply_rope(x, inv_freq, mscale):
            seq = x.shape[-2]
            pos = jnp.arange(seq, dtype=jnp.float32)
            f = jnp.concatenate([pos[:, None] * inv_freq[None, :]] * 2, axis=-1)
            cos = jnp.cos(f) * mscale
            sin = jnp.sin(f) * mscale
            half = DR // 2
            x1, x2 = (x[..., :half], x[..., half:])
            c1, c2 = (cos[:, :half], cos[:, half:])
            s2 = sin[:, half:]
            return jnp.concatenate([x1 * c1 - x2 * s2, x1 * s2 + x2 * c2], axis=-1)
        b, s, _ = hidden_states.shape
        c_q = hidden_states @ w_q_down
        q_nope = (c_q @ w_q_up_nope).reshape(b, s, H, DN).transpose(0, 2, 1, 3)
        q_rope = (c_q @ w_q_up_rope).reshape(b, s, H, DR).transpose(0, 2, 1, 3)
        c_kv = hidden_states @ w_kv_down
        k_rope = (hidden_states @ w_k_rope)[:, None]
        inv_freq, mscale = _yarn_inv_freq()
        q_rope = _apply_rope(q_rope, inv_freq, mscale)
        k_rope = _apply_rope(k_rope, inv_freq, mscale)
        wuk = w_uk.reshape(H, DN, KVL)
        q_lat = jnp.einsum('bhsd,hdr->bhsr', q_nope, wuk)
        scores = jnp.einsum('bhsr,btr->bhst', q_lat, c_kv) + jnp.einsum('bhsd,btd->bhst', q_rope, k_rope[:, 0])
        scores = scores / jnp.sqrt(jnp.float32(DN + DR))
        causal = jnp.tril(jnp.ones((s, s), dtype=bool))
        scores = jnp.where(causal, scores, jnp.finfo(scores.dtype).min)
        probs = jax.nn.softmax(scores, axis=-1)
        out_lat = jnp.einsum('bhst,btr->bhsr', probs, c_kv)
        wuv = w_uv.reshape(H, DV, KVL)
        out = jnp.einsum('bhsr,hdr->bhsd', out_lat, wuv)
        out = out.transpose(0, 2, 1, 3).reshape(b, s, H * DV)
        return out @ w_out

    def _L0_ffn_ref(hidden_states, W, b, A, B, gate_w, gate_b):
        import jax, jax.numpy as jnp
        import numpy as np
        RANKS = (8, 16, 32, 64)
        TOPK = 1
        SCALING = 1.0 / 4
        bsz, seq, d_in = hidden_states.shape
        out = jnp.einsum('bsd,od->bso', hidden_states, W) + b
        x = hidden_states.reshape(-1, d_in)
        scores = x @ gate_w.T + gate_b
        probs = jax.nn.softmax(scores, axis=-1)
        routing_weights, selected = jax.lax.top_k(probs, TOPK)
        routing_weights = routing_weights / jnp.sum(routing_weights, axis=-1, keepdims=True)
        lora_outputs = jnp.stack([x @ A[:r, :].T @ B[:, :r].T for r in RANKS], axis=1)
        sel = jnp.take_along_axis(lora_outputs, selected[:, :, None], axis=1)
        final = jnp.sum(sel * routing_weights[:, :, None], axis=1)
        return out + final.reshape(bsz, seq, -1)

    def _L1_attn_ref(hidden_states, w_qkv, q_ln_w, q_ln_b, k_ln_w, k_ln_b, w_out):
        import jax, jax.numpy as jnp
        import numpy as np
        import math
        D_MODEL = 512
        N_HEADS = 32
        HEAD_DIM = D_MODEL // N_HEADS
        CLIP_QKV = 8.0
        ALIBI_BIAS_MAX = 8
        LN_EPS = 1e-05

        def _alibi_slopes(total_num_heads: int, alibi_bias_max: int) -> jnp.ndarray:
            next_p2 = 2 ** math.ceil(math.log2(total_num_heads))
            m = jnp.arange(1, next_p2 + 1, dtype=jnp.float32) * (alibi_bias_max / next_p2)
            slopes = 1.0 / jnp.power(2.0, m)
            if next_p2 != total_num_heads:
                slopes = jnp.concatenate([slopes[1::2], slopes[::2]])[:total_num_heads]
            return slopes

        def _layer_norm(x, w, b):
            mu = jnp.mean(x, axis=-1, keepdims=True)
            var = jnp.var(x, axis=-1, keepdims=True)
            return (x - mu) * jax.lax.rsqrt(var + LN_EPS) * w + b
        B, S, D = hidden_states.shape
        qkv = jnp.einsum('bsd,ed->bse', hidden_states, w_qkv)
        qkv = jnp.clip(qkv, -CLIP_QKV, CLIP_QKV)
        q, k, v = jnp.split(qkv, 3, axis=-1)
        q = _layer_norm(q, q_ln_w, q_ln_b)
        k = _layer_norm(k, k_ln_w, k_ln_b)
        q = q.reshape(B, S, N_HEADS, HEAD_DIM)
        k = k.reshape(B, S, N_HEADS, HEAD_DIM)
        v = v.reshape(B, S, N_HEADS, HEAD_DIM)
        scale = HEAD_DIM ** (-0.5)
        scores = jnp.einsum('bqhd,bkhd->bhqk', q, k) * scale
        pos = jnp.arange(S)
        rel = pos[None, :] - pos[:, None]
        slopes = _alibi_slopes(N_HEADS, ALIBI_BIAS_MAX)
        bias = slopes[:, None, None] * rel.astype(jnp.float32)
        causal = rel <= 0
        scores = jnp.where(causal[None, None], scores + bias[None], -jnp.inf)
        probs = jax.nn.softmax(scores, axis=-1)
        attn = jnp.einsum('bhqk,bkhd->bqhd', probs, v).reshape(B, S, D)
        return jnp.einsum('bsd,ed->bse', attn, w_out)

    def _L1_ffn_ref(x, ln_w, gate_w, up_w, down_w):
        import jax, jax.numpy as jnp
        import numpy as np
        RMS_EPS = 1e-05
        var = jnp.mean(jnp.square(x), axis=-1, keepdims=True)
        nx = x * jax.lax.rsqrt(var + RMS_EPS) * ln_w
        g = jnp.einsum('bsh,ih->bsi', nx, gate_w)
        u = jnp.einsum('bsh,ih->bsi', nx, up_w)
        return jnp.einsum('bsi,hi->bsh', jax.nn.silu(g) * u, down_w)
    x = L0_attn_hidden_states
    x = _layernorm(x + _L0_attn_ref(x, L0_attn_w_q_down, L0_attn_w_q_up_nope, L0_attn_w_q_up_rope, L0_attn_w_kv_down, L0_attn_w_k_rope, L0_attn_w_uk, L0_attn_w_uv, L0_attn_w_out), axis=-1)
    x = _layernorm(x + _L0_ffn_ref(x, L0_ffn_W, L0_ffn_b, L0_ffn_A, L0_ffn_B, L0_ffn_gate_w, L0_ffn_gate_b), axis=-1)
    x = _layernorm(x + _L1_attn_ref(x, L1_attn_w_qkv, L1_attn_q_ln_w, L1_attn_q_ln_b, L1_attn_k_ln_w, L1_attn_k_ln_b, L1_attn_w_out), axis=-1)
    x = _layernorm(x + _L1_ffn_ref(x, L1_ffn_ln_w, L1_ffn_gate_w, L1_ffn_up_w, L1_ffn_down_w), axis=-1)
    return x

_drawn_inputs = setup_inputs


def setup_inputs(seed=0):
    import zlib

    import numpy as np

    out = dict(_drawn_inputs(seed))
    spreads = {'L1_attn_q_ln_w': (1.0, 0.6),
     'L1_attn_q_ln_b': (0.0, 0.8),
     'L1_attn_k_ln_w': (1.0, 0.6),
     'L1_attn_k_ln_b': (0.0, 2.0),
     'L1_ffn_ln_w': (1.0, 0.2)}
    factors = {'L0_attn_w_q_down': 5.332,
     'L0_attn_w_q_up_nope': 8.0,
     'L0_attn_w_q_up_rope': 5.613,
     'L0_attn_w_k_rope': 5.749,
     'L0_attn_w_uk': 8.0,
     'L0_ffn_b': 3.152,
     'L0_ffn_gate_b': 28.148}
    for name, (base, spread) in spreads.items():
        noise = np.random.default_rng([zlib.crc32(name.encode()), seed]).standard_normal(out[name].shape)
        drawn = base * np.exp(spread * noise) if base else spread * noise
        out[name] = jnp.asarray(drawn.astype(out[name].dtype))
    for name, factor in factors.items():
        out[name] = (out[name] * factor).astype(out[name].dtype)
    return out
```

```python
from contextlib import ExitStack

import numpy as np

import concourse.bass as bass
from concourse import mybir

F32 = mybir.dt.float32
F32R = mybir.dt.float32r
BF16 = mybir.dt.bfloat16
ACT = mybir.ActivationFunctionType
ALU = mybir.AluOpType
AX = mybir.AxisListType

P = 128
S = 1024
D = 512
ST = S // P
DK = D // P
BANK = 512
NEG = -3.0e38

H0, QL, KVL, DN, DR, DV = 32, 192, 64, 128, 64, 128
PAIRS = H0 // 2
SCALE0 = float(1.0 / np.sqrt(np.float32(DN + DR)))


def rope_tables():
    freqs = np.float32(1.0) / np.float32(10000.0) ** (np.arange(0, DR, 2, dtype=np.float32) / np.float32(DR))
    wavelengths = np.float32(2.0 * np.pi) / freqs
    ramp = np.clip((wavelengths / np.float32(4096.0) - np.float32(1.0)) / np.float32(31.0), 0, 1).astype(np.float32)
    inv = (freqs / (np.float32(1.0) - ramp + ramp * np.float32(40.0))).astype(np.float32)
    f = np.arange(S, dtype=np.float32)[None, :] * inv[:, None]
    cos, sin = np.cos(f).astype(np.float32), np.sin(f).astype(np.float32)
    return np.tile(cos, (4, 1)), np.concatenate([-sin, sin, -sin, sin])


class Alloc:

    def __init__(self, nc, ctx):
        self.nc, self.ctx = nc, ctx

    def sb(self, name, shape, dt=F32):
        return self.ctx.enter_context(self.nc.sbuf_tensor(name, shape, dt))

    def ps(self, name, shape, dt=F32):
        return self.ctx.enter_context(self.nc.psum_tensor(name, shape, dt))

    def sem(self, name):
        return self.ctx.enter_context(self.nc.semaphore(name))


def from_one(eng, sem, value):
    if not (isinstance(value, int) and value <= 0):
        eng.wait_ge(sem, value)


def three(pe, out, terms, start=True, stop=True):
    for n, (l, r) in enumerate(terms):
        last = pe.matmul(out, l, r, start=start and n == 0, stop=stop and n == len(terms) - 1)
    return last


def stage_latent(nc, io, keep):
    with ExitStack() as ctx:
        al = Alloc(nc, ctx)
        xT_h = al.sb("xT_h", [P, DK, S], F32R)
        xT_l = al.sb("xT_l", [P, DK, S], F32R)
        WD = QL + 4 * 64
        wd_f = al.sb("wd_f", [P, DK, WD])
        wd_h = al.sb("wd_h", [P, DK, WD], F32R)
        wd_l = al.sb("wd_l", [P, DK, WD], F32R)
        k_f = al.sb("k_f", [P, S])
        k_sw = al.sb("k_sw", [P, S])
        tr = [al.ps(f"tr{i}", [P, DK, P]) for i in range(2)]
        pj = [al.ps(f"pj{i}", [P, BANK]) for i in range(4)]
        pc = al.ps("pc", [P, ST, KVL])

        x_in, wd_in = [al.sem(f"a_x_in{n}") for n in range(2)], al.sem("a_wd_in")
        const_ok, xT_ps, xTh_ok, xTl_ok = (al.sem(n) for n in ("a_const", "a_xT_ps", "a_xTh", "a_xTl"))
        wdh_ok, wdl_ok = al.sem("a_wdh"), al.sem("a_wdl")
        proj_ps, act_ev, dve_ev = al.sem("a_proj"), al.sem("a_act_ev"), al.sem("a_dve_ev")
        kf_ok, kh_ok = al.sem("a_kf"), al.sem("a_kh")
        ckv_ps, done = al.sem("a_ckv_ps"), al.sem("a_done")
        tiles = [(0, P), (P, QL - P), (QL, P), (QL + P, P)]

        with nc.Block() as block:

            @block.sync
            def _(sp):
                x = io["x"].rearrange("b (j p) d -> p (b j) d", p=P)
                for n in range(2):
                    sp.dma_start(keep.x[:, 4 * n:4 * n + 4, :], x[:, 4 * n:4 * n + 4, :]).then_inc(x_in[n], 16)
                rope = io["w_k_rope"].rearrange("(k p) n -> p k n", p=P)
                kv = io["w_kv_down"].rearrange("(k p) n -> p k n", p=P)
                sp.dma_start(wd_f[:, :, 0:QL], io["w_q_down"].rearrange("(k p) n -> p k n", p=P)).then_inc(wd_in, 16)
                for n in range(2):
                    at = QL + n * P
                    sp.dma_start(wd_f[:, :, at:at + 64], kv).then_inc(wd_in, 16)
                sp.dma_start(wd_f[:, :, QL + 64:QL + 128], rope).then_inc(wd_in, 16)
                sp.dma_start(wd_f[:, :, QL + 192:QL + 224], rope[:, :, 32:64]).then_inc(wd_in, 16)
                sp.dma_start(wd_f[:, :, QL + 224:QL + 256], rope[:, :, 0:32]).then_inc(wd_in, 16)
                sp.dma_start(keep.cos[:], io["cos"]).then_inc(wd_in, 16)
                sp.dma_start(keep.sin[:], io["sin"]).then_inc(wd_in, 16)

            @block.gpsimd
            def _(pool):
                pool.memset(keep.ident[:], 0.0).then_inc(const_ok, 1)
                pool.memset(keep.ident_b[:], 0.0).then_inc(const_ok, 1)
                pool.memset(keep.mask[:], 0.0).then_inc(const_ok, 1)
                pool.memset(keep.mask_t[:], 0.0).then_inc(const_ok, 1)
                pool.wait_ge(const_ok, 4)
                for m in (keep.ident, keep.ident_b):
                    pool.affine_select(out=m[:], in_=m[:], compare_op=ALU.not_equal, fill=1.0, base=0,
                                       pattern=[[-1, P]], channel_multiplier=1).then_inc(const_ok, 1)
                pool.affine_select(out=keep.mask[:], in_=keep.mask[:], compare_op=ALU.is_ge, fill=NEG, base=0,
                                   pattern=[[-1, P]], channel_multiplier=1).then_inc(const_ok, 1)
                pool.affine_select(out=keep.mask_t[:], in_=keep.mask_t[:], compare_op=ALU.is_ge, fill=NEG, base=0,
                                   pattern=[[1, P]], channel_multiplier=-1).then_inc(const_ok, 1)

            @block.tensor
            def _(pe):
                pe.wait_ge(const_ok, 8)
                for j in range(ST):
                    pe.wait_ge(x_in[j // 4], 16)
                    if j >= 2:
                        pe.wait_ge(xTl_ok, j - 1)
                    for k in range(DK):
                        last = pe.transpose(tr[j % 2][:, k, :], keep.x[:, j, k * P:(k + 1) * P], keep.ident[:])
                    last.then_inc(xT_ps, 1)
                pe.wait_ge(wdl_ok, 1)
                for n in range(2):
                    pe.wait_ge(xTl_ok, 4 * n + 4)
                    half = slice(n * BANK, (n + 1) * BANK)
                    for t, (c, m) in enumerate(tiles):
                        if n == 1:
                            pe.wait_ge(act_ev, t + 1)
                            pe.wait_ge(dve_ev, t + 1)
                        terms = []
                        for k in range(DK):
                            h, l = wd_h[:, k, c:c + m], wd_l[:, k, c:c + m]
                            terms += [(h, xT_h[:, k, half]), (h, xT_l[:, k, half]), (l, xT_h[:, k, half])]
                        three(pe, pj[t][0:m, :], terms).then_inc(proj_ps, 1)
                kv = slice(QL, QL + KVL)
                for j in range(ST):
                    cols = slice(j * P, (j + 1) * P)
                    terms = []
                    for k in range(DK):
                        h, l = wd_h[:, k, kv], wd_l[:, k, kv]
                        terms += [(xT_h[:, k, cols], h), (xT_l[:, k, cols], h), (xT_h[:, k, cols], l)]
                    last = three(pe, pc[:, j, :], terms)
                last.then_inc(ckv_ps, 1)

            @block.scalar
            def _(act):
                for j in range(ST):
                    act.wait_ge(xT_ps, j + 1)
                    act.copy(xT_h[:, :, j * P:(j + 1) * P], tr[j % 2][:]).then_inc(xTh_ok, 1)
                for n in range(2):
                    half = slice(n * BANK, (n + 1) * BANK)
                    act.wait_ge(proj_ps, 4 * n + 1)
                    act.copy(keep.cqa_h[:, half], pj[0][:]).then_inc(act_ev, 1)
                    act.wait_ge(proj_ps, 4 * n + 2)
                    act.copy(keep.cqb_hh[64:128, half], pj[1][0:64, :]).then_inc(done, 1)
                    act.copy(keep.cqb_hh[0:64, half], pj[1][0:64, :]).then_inc(act_ev, 1)
                    act.wait_ge(proj_ps, 4 * n + 3)
                    act.copy(k_f[0:64, half], pj[2][0:64, :]).then_inc(act_ev, 1)
                    act.wait_ge(act_ev, 4 * n + 3)
                    act.wait_ge(kf_ok, n + 1)
                    act.copy(keep.k_h[:, half], k_f[:, half]).then_inc(act_ev, 1)
                act.wait_ge(ckv_ps, 1)
                act.copy(keep.ckv[:], pc[:]).then_inc(done, 1)

            @block.vector
            def _(dve):
                dve.wait_ge(wd_in, 128)
                dve.tensor_copy(wd_h[:], wd_f[:]).then_inc(wdh_ok, 1)
                dve.wait_ge(wdh_ok, 1)
                dve.tensor_tensor(wd_l[:], wd_f[:], wd_h[:].bitcast(F32), ALU.subtract).then_inc(wdl_ok, 1)
                for j in range(ST):
                    dve.wait_ge(xTh_ok, j + 1)
                    dve.tensor_tensor(xT_l[:, :, j * P:(j + 1) * P], tr[j % 2][:],
                                      xT_h[:, :, j * P:(j + 1) * P].bitcast(F32), ALU.subtract).then_inc(xTl_ok, 1)
                rope = slice(64, 128)
                for n in range(2):
                    half = slice(n * BANK, (n + 1) * BANK)
                    dve.wait_ge(act_ev, 4 * n + 1)
                    dve.tensor_tensor(keep.cqa_l[:, half], pj[0][:], keep.cqa_h[:, half].bitcast(F32),
                                      ALU.subtract).then_inc(dve_ev, 1)
                    dve.wait_ge(act_ev, 4 * n + 2)
                    dve.tensor_tensor(keep.cqb_l[0:64, half], pj[1][0:64, :], keep.cqb_hh[0:64, half].bitcast(F32),
                                      ALU.subtract).then_inc(dve_ev, 1)
                    dve.wait_ge(proj_ps, 4 * n + 3)
                    dve.tensor_tensor(k_f[rope, half], pj[2][rope, :], keep.cos[rope, half], ALU.mult).then_inc(dve_ev, 1)
                    dve.wait_ge(proj_ps, 4 * n + 4)
                    dve.tensor_tensor(k_sw[rope, half], pj[3][rope, :], keep.sin[rope, half], ALU.mult).then_inc(dve_ev, 1)
                    dve.wait_ge(dve_ev, 4 * n + 4)
                    dve.tensor_tensor(k_f[rope, half], k_f[rope, half], k_sw[rope, half], ALU.add).then_inc(kf_ok, 1)
                    dve.wait_ge(act_ev, 4 * n + 4)
                    dve.tensor_tensor(keep.k_l[:, half], k_f[:, half], keep.k_h[:, half].bitcast(F32),
                                      ALU.subtract).then_inc(done, 1)


def stage_mla(nc, io, keep):
    with ExitStack() as ctx:
        al = Alloc(nc, ctx)
        nope_a, nope_b = al.sb("nope_a", [P, 2 * DN]), al.sb("nope_b", [64, 2 * DN])
        wuk, wuv = al.sb("wuk", [P, 2, KVL]), al.sb("wuv", [P, 2, KVL])
        wout = al.sb("wout", [P, 2, D])
        nope_t = al.sb("nope_t", [P, 2, QL])
        wa_f, wb_f = al.sb("wa_f", [P, 3 * P]), al.sb("wb_f", [64, 3 * P])
        wa_h, wa_l = al.sb("wa_h", [P, 3 * P], F32R), al.sb("wa_l", [P, 3 * P], F32R)
        wb_hl = al.sb("wb_hl", [P, 3 * P], F32R)
        q_f = [al.sb(f"q_f{e}", [P, S]) for e in range(2)]
        q_sw = [al.sb(f"q_sw{e}", [P, S]) for e in range(2)]
        q_h = [al.sb(f"q_h{e}", [P, S], F32R) for e in range(2)]
        q_l = [al.sb(f"q_l{e}", [P, S], F32R) for e in range(2)]
        probs = [al.sb(f"probs{i}", [P, S]) for i in range(4)]
        stat = al.sb("stat", [P, 3, 4])
        pt = [al.sb(f"pt{g}", [P, 2, 4 * (g + 1), BANK]) for g in range(2)]
        ol_h, ol_l = al.sb("ol_h", [P, S], F32R), al.sb("ol_l", [P, S], F32R)
        wo_h, wo_l = al.sb("wo_h", [P, D], F32R), al.sb("wo_l", [P, D], F32R)

        sc = [al.ps(f"sc{i}", [P, S]) for i in range(2)]
        tb = [al.ps(f"tb{i}", [P, 4, P]) for i in range(2)]
        mb = [al.ps(f"mb{i}", [P, BANK]) for i in range(2)]

        names = ("wq_in wo_in scores negmax exp recip pnorm pt_ps pt_ev pv olat_h olat_l wt_ps wt_ev wlat_ps wlat_ev "
                 "wsplit qp qlat qdve qadd qh ql wo_ps wo_h wo_l op acc").split()
        (wq_in, wo_in, scores, negmax, exped, recip, pnorm, pt_ps, pt_ev, pv, olat_h, olat_l, wt_ps, wt_ev, wlat_ps,
         wlat_ev, wsplit, qp, qlat, qdve, qadd, qh_ok, ql_ok, wo_ps, woh_ok, wol_ok, op, acc) = (
            al.sem("b_" + n) for n in names)

        NS = 2 * ST
        groups = []
        for n in range(NS):
            for j0 in range(0, n // 2 + 1, 4):
                groups.append((n, j0, min(4, n // 2 + 1 - j0)))
        NG = len(groups)
        NWQ, NWO = 9, 2

        def load_q(sp, r):
            cols = lambda w, c0, n, r0, r1: io[w][r0:r1, bass.ds(r * c0, n)]
            sp.dma_start(nope_a[:], cols("w_q_up_nope", 2 * DN, 2 * DN, 0, P)).then_inc(wq_in, 16)
            sp.dma_start(nope_b[:], cols("w_q_up_nope", 2 * DN, 2 * DN, P, QL)).then_inc(wq_in, 16)
            for w, r0, r1 in ((wa_f, 0, P), (wb_f, P, QL)):
                src = cols("w_q_up_rope", 2 * DR, 2 * DR, r0, r1)
                heads = w[:, 0:2 * P].rearrange("p (e c) -> p e c", e=2)
                swapped = w[:, 2 * P:3 * P].rearrange("p (e t f) -> p e t f", e=2, t=2)
                sp.dma_start(heads[:, :, KVL:P], src.rearrange("p (e c) -> p e c", e=2)).then_inc(wq_in, 16)
                halves = src.rearrange("p (e t f) -> p e t f", e=2, t=2)
                for t in range(2):
                    sp.dma_start(swapped[:, :, t, :], halves[:, :, 1 - t, :]).then_inc(wq_in, 16)

        def load_o(sp, r):
            rows = lambda w: io[w][bass.ds(r * 2 * DV, 2 * DV), :].rearrange("(e d) n -> d e n", e=2)
            sp.dma_start(wuv[:], rows("w_uv")).then_inc(wo_in, 16)
            sp.dma_start(wout[:], rows("w_out")).then_inc(wo_in, 16)

        def load_k(sp, r):
            sp.dma_start(wuk[:], io["w_uk"][bass.ds(r * 2 * DN, 2 * DN), :].rearrange("(e d) n -> d e n", e=2))\
                .then_inc(wq_in, 16)

        with nc.Block() as block:

            @block.sync
            def _(sp):
                load_q(sp, 0)
                load_k(sp, 0)
                load_o(sp, 0)

                def pair(p, more):
                    if more:
                        sp.wait_ge(wt_ps, p + 1)
                        sp.wait_ge(wlat_ps, p + 1)
                        sp.wait_ge(wsplit, 4 * p + 4)
                        load_q(sp, p + 1)
                        load_k(sp, p + 1)
                        sp.wait_ge(wo_ps, p + 1)
                        load_o(sp, p + 1)

                pair(0, True)
                with sp.Fori(1, PAIRS - 1) as p:
                    pair(p, True)

            @block.tensor
            def _(pe):
                def weights(r, first):
                    pe.wait_ge(wq_in, (r + 1) * (16 * NWQ))
                    if not first:
                        from_one(pe, acc, 8 * r - 8)
                    wt = mb[0][:, 0:2 * QL].rearrange("p (e c) -> p e c", e=2)
                    for e in range(2):
                        pe.transpose(wt[:, e, 0:P], nope_a[:, e * DN:(e + 1) * DN], keep.ident[:])
                        last = pe.transpose(wt[:, e, P:QL], nope_b[:, e * DN:(e + 1) * DN], keep.ident[0:64, 0:64])
                    last.then_inc(wt_ps, 1)

                def weights2(r):
                    pe.wait_ge(wt_ev, r + 1)
                    for e in range(2):
                        pe.matmul(mb[1][:, e * 64:e * 64 + 64], nope_t[:, e, 0:P], wuk[:, e, :], start=True, stop=True)
                        last = pe.matmul(mb[1][0:64, P + e * 64:P + e * 64 + 64], nope_t[:, e, P:QL], wuk[:, e, :],
                                         start=True, stop=True)
                    last.then_inc(wlat_ps, 1)

                def queries(r, first):
                    pe.wait_ge(wsplit, 4 * r + 4)
                    for n in range(6):
                        t, half = n // 2, slice((n % 2) * BANK, (n % 2 + 1) * BANK)
                        if n == 1 and not first:
                            pe.wait_ge(olat_l, 2 * r - 1)
                        if n >= 2:
                            pe.wait_ge(qdve, 6 * r + n - 1)
                            if n < 6:
                                pe.wait_ge(qlat, 4 * r + min(n - 1, 4))
                        cols = slice(t * P, (t + 1) * P)
                        three(pe, mb[(n + 1) % 2][:], [
                            (wa_h[:, cols], keep.cqa_h[:, half]), (wa_h[:, cols], keep.cqa_l[:, half]),
                            (wa_l[:, cols], keep.cqa_h[:, half]), (wb_hl[:, cols], keep.cqb_hh[:, half]),
                            (wb_hl[0:64, cols], keep.cqb_l[0:64, half])]).then_inc(qp, 1)

                def score(p, n):
                    i, e = n // 2, n % 2
                    if n >= 2:
                        pe.wait_ge(exped, NS * p + n - 1)
                    if n == 0:
                        pe.wait_ge(qh_ok, 2 * p + 2)
                        pe.wait_ge(ql_ok, 2 * p + 2)
                    rows = slice(i * P, (i + 1) * P)
                    width = (i + 1) * P
                    for c0 in range(0, width, BANK):
                        w = min(BANK, width - c0)
                        keys = slice(c0, c0 + w)
                        diagonal = c0 + w == width
                        last = three(pe, sc[n % 2][:, keys], [
                            (q_h[e][:, rows], keep.k_h[:, keys]), (q_h[e][:, rows], keep.k_l[:, keys]),
                            (q_l[e][:, rows], keep.k_h[:, keys])], stop=not diagonal)
                        if diagonal:
                            last = pe.matmul(sc[n % 2][:, width - P:width], keep.ident_b[:], keep.mask[:],
                                             start=False, stop=True)
                    last.then_inc(scores, 1)

                def turn(p, n):
                    pe.wait_ge(pnorm, NS * p + n + 1)
                    for g, (m, j0, nb) in enumerate(groups):
                        if m == n:
                            from_one(pe, pt_ev, NG * p + max(g - 1, 0))
                            for b in range(nb):
                                last = pe.transpose(tb[g % 2][:, b, :], probs[n % 4][:, (j0 + b) * P:(j0 + b + 1) * P],
                                                    keep.ident[:])
                            last.then_inc(pt_ps, 1)

                def values(p, g):
                    pe.wait_ge(pt_ev, NG * p + (8 if g == 0 else NG))
                    if g == 1:
                        pe.wait_ge(acc, 8 * p + 3)
                    for j in range(4 * (g + 1)):
                        off = max(0, j - 4 * g) * P
                        for e in range(2):
                            last = pe.matmul(mb[0][64 * e:64 * e + 64, off:BANK], keep.ckv[:, j, :],
                                             pt[g][:, e, j, off:BANK], start=(j == 0), stop=(j == 4 * g + 3))
                    last.then_inc(pv, 1)

                def out_weights(p, more):
                    pe.wait_ge(wo_in, (p + 1) * (16 * NWO))
                    if more:
                        pe.wait_ge(qdve, 6 * p + 11)
                    for e in range(2):
                        last = pe.matmul(mb[1][64 * e:64 * e + 64, :], wuv[:, e, :], wout[:, e, :], start=True, stop=True)
                    last.then_inc(wo_ps, 1)

                def out_tile(p, j, more):
                    bank = [0, 1, 0, 1, 1, 0, 1, 0][j]
                    if j == 0:
                        pe.wait_ge(wol_ok, p + 1)
                        pe.wait_ge(olat_l, 2 * p + 1)
                        if more:
                            pe.wait_ge(qdve, 6 * p + 12)
                    elif j in (2, 3):
                        pe.wait_ge(acc, 8 * p + j - 1)
                    elif j == 4:
                        pe.wait_ge(acc, 8 * p + 4)
                        pe.wait_ge(olat_l, 2 * p + 2)
                    elif j > 5:
                        pe.wait_ge(acc, 8 * p + j - 1)
                    rows = slice(j * P, (j + 1) * P)
                    three(pe, mb[bank][:], [(ol_h[:, rows], wo_h[:]), (ol_h[:, rows], wo_l[:]),
                                            (ol_l[:, rows], wo_h[:])]).then_inc(op, 1)

                def pair(p, more):
                    for n in range(NS):
                        score(p, n)
                        if n >= 2:
                            turn(p, n - 2)
                        if n == 4 and more:
                            weights(p + 1, False)
                        if n == 6 and more:
                            weights2(p + 1)
                        if n == 10:
                            if not more:
                                pe.wait_ge(acc, 8 * p)
                            values(p, 0)
                    if more:
                        queries(p + 1, False)
                    turn(p, NS - 2)
                    turn(p, NS - 1)
                    out_weights(p, more)
                    for j in range(4):
                        out_tile(p, j, more)
                    values(p, 1)
                    for j in range(4, 8):
                        out_tile(p, j, more)

                weights(0, True)
                weights2(0)
                queries(0, True)
                pair(0, True)
                with pe.Fori(1, PAIRS - 1) as p:
                    pair(p, True)
                pair(PAIRS - 1, False)

            @block.scalar
            def _(act):
                def weights(r):
                    act.wait_ge(wt_ps, r + 1)
                    act.copy(nope_t[:].rearrange("p e c -> p (e c)"), mb[0][:, 0:2 * QL]).then_inc(wt_ev, 1)

                def weights2(r):
                    act.wait_ge(wlat_ps, r + 1)
                    for w, m, c in ((wa_f, P, 0), (wb_f, 64, P)):
                        act.copy(w[:, 0:2 * P].rearrange("p (e c) -> p e c", e=2)[:, :, 0:KVL],
                                 mb[1][0:m, c:c + P].rearrange("p (e c) -> p e c", e=2)).then_inc(wlat_ev, 1)

                def latent_queries(r):
                    for n in range(4):
                        act.wait_ge(qp, 6 * r + n + 1)
                        act.mul(q_f[n // 2][0:64, (n % 2) * BANK:(n % 2 + 1) * BANK], mb[(n + 1) % 2][0:64, :],
                                SCALE0).then_inc(qlat, 1)

                def split_queries(r):
                    for e in range(2):
                        act.wait_ge(qadd, 2 * r + e + 1)
                        act.copy(q_h[e][:], q_f[e][:]).then_inc(qh_ok, 1)

                def exp(p, n):
                    act.wait_ge(negmax, NS * p + n + 1)
                    w, s = (n // 2 + 1) * P, n % 4
                    act.activation(probs[s][:, 0:w], sc[n % 2][:, 0:w], ACT.Exp, bias=stat[:, 0, s:s + 1],
                                   accum_out=stat[:, 1, s:s + 1]).then_inc(exped, 1)

                def turned(p, n):
                    i, e = n // 2, n % 2
                    for g, (m, j0, nb) in enumerate(groups):
                        if m == n:
                            act.wait_ge(pt_ps, NG * p + g + 1)
                            act.copy(pt[i // 4][:, e, j0:j0 + nb, (i % 4) * P:(i % 4 + 1) * P],
                                     tb[g % 2][:, 0:nb, :]).then_inc(pt_ev, 1)

                def latent_out(p, g):
                    act.wait_ge(pv, 2 * p + g + 1)
                    from_one(act, op, 8 * p)
                    act.copy(ol_h[:, g * BANK:(g + 1) * BANK], mb[0][:]).then_inc(olat_h, 1)

                def pair(p, more):
                    for n in range(NS):
                        exp(p, n)
                        if n >= 2:
                            turned(p, n - 2)
                        if n == 5 and more:
                            weights(p + 1)
                        if n == 7 and more:
                            weights2(p + 1)
                        if n == 11:
                            latent_out(p, 0)
                    if more:
                        latent_queries(p + 1)
                    turned(p, NS - 2)
                    turned(p, NS - 1)
                    if more:
                        split_queries(p + 1)
                    act.wait_ge(wo_ps, p + 1)
                    act.copy(wo_h[:], mb[1][:]).then_inc(woh_ok, 1)
                    latent_out(p, 1)

                weights(0)
                weights2(0)
                latent_queries(0)
                split_queries(0)
                pair(0, True)
                with act.Fori(1, PAIRS - 1) as p:
                    pair(p, True)
                pair(PAIRS - 1, False)

            @block.vector
            def _(dve):
                def split_weights(r):
                    dve.wait_ge(wlat_ev, 2 * r + 2)
                    dve.wait_ge(wq_in, (r + 1) * (16 * NWQ))
                    from_one(dve, qp, 6 * r)
                    dve.tensor_copy(wa_h[:], wa_f[:]).then_inc(wsplit, 1)
                    dve.tensor_copy(wb_hl[0:64, :], wb_f[:]).then_inc(wsplit, 1)
                    dve.wait_ge(wsplit, 4 * r + 2)
                    dve.tensor_tensor(wa_l[:], wa_f[:], wa_h[:].bitcast(F32), ALU.subtract).then_inc(wsplit, 1)
                    dve.tensor_tensor(wb_hl[64:128, :], wb_f[:], wb_hl[0:64, :].bitcast(F32),
                                      ALU.subtract).then_inc(wsplit, 1)

                def rope_queries(r):
                    rope = slice(64, 128)
                    for n in range(6):
                        half = slice((n % 2) * BANK, (n % 2 + 1) * BANK)
                        bank = mb[(n + 1) % 2]
                        dve.wait_ge(qp, 6 * r + n + 1)
                        if n < 4:
                            dve.scalar_tensor_tensor(out=q_f[n // 2][rope, half], in0=bank[rope, :], scalar=SCALE0,
                                                     in1=keep.cos[rope, half], op0=ALU.mult, op1=ALU.mult).then_inc(qdve, 1)
                        else:
                            for e in range(2):
                                rows = slice(64 * e, 64 * e + 64)
                                last = dve.scalar_tensor_tensor(
                                    out=q_sw[e][rope, half], in0=bank[rows, :], scalar=SCALE0,
                                    in1=keep.sin[rows, half], op0=ALU.mult, op1=ALU.mult)
                            last.then_inc(qdve, 1)

                def row_max(p, n):
                    dve.wait_ge(scores, NS * p + n + 1)
                    dve.tensor_reduce(stat[:, 0, n % 4:n % 4 + 1], sc[n % 2][:, 0:(n // 2 + 1) * P], AX.X, ALU.max,
                                      negate=True).then_inc(negmax, 1)

                def normalise(p, n):
                    s, w = n % 4, (n // 2 + 1) * P
                    dve.wait_ge(exped, NS * p + n + 1)
                    dve.reciprocal(stat[:, 2, s:s + 1], stat[:, 1, s:s + 1]).then_inc(recip, 1)
                    dve.wait_ge(recip, NS * p + n + 1)
                    dve.tensor_scalar(probs[s][:, 0:w], probs[s][:, 0:w], stat[:, 2, s:s + 1], None,
                                      ALU.mult).then_inc(pnorm, 1)

                def latent_out(p, g):
                    dve.wait_ge(olat_h, 2 * p + g + 1)
                    half = slice(g * BANK, (g + 1) * BANK)
                    dve.tensor_tensor(ol_l[:, half], mb[0][:], ol_h[:, half].bitcast(F32), ALU.subtract).then_inc(olat_l, 1)

                def out_tile(p, j):
                    bank = mb[[0, 1, 0, 1, 1, 0, 1, 0][j]]
                    dve.wait_ge(op, 8 * p + j + 1)
                    dve.tensor_tensor(keep.x[:, j, :], bank[:], keep.x[:, j, :], ALU.add).then_inc(acc, 1)

                def pair(p, more):
                    for n in range(NS):
                        row_max(p, n)
                        if n >= 1:
                            normalise(p, n - 1)
                        if n == 9 and more:
                            split_weights(p + 1)
                        if n == 12:
                            latent_out(p, 0)
                    normalise(p, NS - 1)
                    if more:
                        rope_queries(p + 1)
                    dve.wait_ge(woh_ok, p + 1)
                    dve.tensor_tensor(wo_l[:], mb[1][:], wo_h[:].bitcast(F32), ALU.subtract).then_inc(wol_ok, 1)
                    for j in range(4):
                        out_tile(p, j)
                    latent_out(p, 1)
                    for j in range(4, 8):
                        out_tile(p, j)

                split_weights(0)
                rope_queries(0)
                pair(0, True)
                with dve.Fori(1, PAIRS - 1) as p:
                    pair(p, True)
                pair(PAIRS - 1, False)

            @block.gpsimd
            def _(pool):
                def queries(r):
                    for e in range(2):
                        if e == 0:
                            pool.wait_ge(qdve, 6 * r + 6)
                            pool.wait_ge(qlat, 4 * r + 4)
                        pool.tensor_tensor(q_f[e][64:128, :], q_f[e][64:128, :], q_sw[e][64:128, :],
                                           ALU.add).then_inc(qadd, 1)
                    pool.wait_ge(qadd, 2 * r + 2)
                    for e in range(2):
                        pool.wait_ge(qh_ok, 2 * r + e + 1)
                        pool.tensor_tensor(q_l[e][:], q_f[e][:], q_h[e][:].bitcast(F32), ALU.subtract).then_inc(ql_ok, 1)

                queries(0)
                with pool.Fori(1, PAIRS) as r:
                    queries(r)


class Norm:

    def __init__(self, al, name, n):
        self.n = n
        self.st, self.mv = al.sb(name + "_st", [P, n, 6]), al.sb(name + "_mv", [P, n, 2])
        self.sd, self.rs = al.sb(name + "_sd", [P, n]), al.sb(name + "_rs", [P, n])
        self.st_ok, self.mv_ok, self.ve_ok, self.sd_ok, self.rs_ok, self.x_ok = (
            al.sem(f"{name}_{s}") for s in ("st", "mv", "ve", "sd", "rs", "x"))

    def stats(self, dve, t, x):
        dve.bn_stats(self.st[:, t, :], x).then_inc(self.st_ok, 1)
        dve.wait_ge(self.st_ok, t + 1)
        dve.bn_aggr(self.mv[:, t, :], self.st[:, t, :]).then_inc(self.mv_ok, 1)

    def variance(self, dve, eps=1e-5):
        dve.wait_ge(self.mv_ok, self.n)
        dve.tensor_scalar(self.sd[:], self.mv[:, :, 1], eps, None, ALU.add).then_inc(self.ve_ok, 1)

    def root(self, act):
        act.wait_ge(self.ve_ok, 1)
        act.activation(self.sd[:], self.sd[:], ACT.Sqrt).then_inc(self.sd_ok, 1)

    def inverse(self, dve):
        dve.wait_ge(self.sd_ok, 1)
        dve.reciprocal(self.rs[:], self.sd[:]).then_inc(self.rs_ok, 1)
        dve.wait_ge(self.rs_ok, 1)

    def apply(self, dve, t, x):
        dve.tensor_scalar(x, x, self.mv[:, t, 0:1], self.rs[:, t:t + 1], ALU.subtract, ALU.mult).then_inc(self.x_ok, 1)


RANKS = (8, 16, 32, 64)
MR = RANKS[-1]
NR = len(RANKS)
CLIP = 8.0
HD1 = 16
SCALE1 = HD1 ** -0.5


def stage_route(nc, io, keep):
    with ExitStack() as ctx:
        al = Alloc(nc, ctx)
        w_f, ag_f, b_f = al.sb("c_w", [P, DK, D]), al.sb("c_ag", [MR + NR, D]), al.sb("c_b", [P, DK, MR])
        bias, gate_b = al.sb("c_bias", [P, D]), al.sb("c_gate_b", [P, NR])
        wT_h, wT_l = al.sb("wT_h", [P, DK, D], F32R), al.sb("wT_l", [P, DK, D], F32R)
        agT_h, agT_l = al.sb("agT_h", [P, DK, MR + NR], F32R), al.sb("agT_l", [P, DK, MR + NR], F32R)
        bT_h, bT_l = al.sb("bT_h", [MR, DK, P], F32R), al.sb("bT_l", [MR, DK, P], F32R)
        xT_h, xT_l = al.sb("x1T_h", [P, DK, S], F32R), al.sb("x1T_l", [P, DK, S], F32R)
        ag = al.sb("ag", [P, ST, MR + NR])
        top, less, gate = al.sb("top", [P, ST]), al.sb("less", [P, ST, NR]), al.sb("gate", [P, ST, NR])
        loT_h, loT_l = al.sb("loT_h", [MR, ST, P], F32R), al.sb("loT_l", [MR, ST, P], F32R)
        tr = [al.ps(f"c_tr{i}", [P, DK, P]) for i in range(2)]
        pag = [al.ps(f"c_ag{i}", [P, 4, MR + NR]) for i in range(2)]
        po = [al.ps(f"c_po{i}", [P, D]) for i in range(4)]
        n1, n2 = Norm(al, "n1", ST), Norm(al, "n2", ST)
        names = "w_in b_in tr_ps tr_h tr_l ag_ps ag_ev route biased out_ps out_ev"
        w_in, b_in, tr_ps, tr_h, tr_l, ag_ps, ag_ev, route, biased, out_ps, out_ev = (
            al.sem("c_" + n) for n in names.split())

        jobs = [([w_f[:, t, k * P:(k + 1) * P] for k in range(DK)], (wT_h, wT_l), slice(t * P, (t + 1) * P)) for t in range(DK)]
        jobs += [([ag_f[:, k * P:(k + 1) * P] for k in range(DK)], (agT_h, agT_l), slice(0, MR + NR))]
        jobs += [([b_f[:, t, :] for t in range(DK)], (bT_h, bT_l), slice(0, P))]
        JX = len(jobs)
        jobs += [([keep.x[:, j, k * P:(k + 1) * P] for k in range(DK)], (xT_h, xT_l), slice(j * P, (j + 1) * P)) for j in range(ST)]
        JL = len(jobs)
        jobs += [([ag[:, 4 * n + t, 0:MR] for t in range(4)], (loT_h[:, 4 * n:4 * n + 4], loT_l[:, 4 * n:4 * n + 4]),
                  slice(0, P)) for n in range(2)]

        def shape(n):
            src, dst, cols = jobs[n]
            return src[0].shape[0], src[0].shape[1]

        with nc.Block() as block:

            @block.sync
            def _(sp):
                sp.dma_start(w_f[:], io["L0_ffn_W"].rearrange("(t p) n -> p t n", p=P)).then_inc(w_in, 16)
                sp.dma_start(ag_f[0:MR, :], io["L0_ffn_A"]).then_inc(w_in, 16)
                sp.dma_start(ag_f[MR:MR + NR, :], io["L0_ffn_gate_w"]).then_inc(w_in, 16)
                sp.dma_start(b_f[:], io["L0_ffn_B"].rearrange("(t p) n -> p t n", p=P)).then_inc(w_in, 16)
                sp.dma_start(bias[:], io["L0_ffn_b"].partition_broadcast(P)).then_inc(b_in, 16)
                sp.dma_start(gate_b[:], io["L0_ffn_gate_b"].partition_broadcast(P)).then_inc(b_in, 16)
                sp.dma_start(keep.wqkv[:], io["L1_attn_w_qkv"].rearrange("(t p) n -> p t n", p=P)).then_inc(keep.wqkv_in, 16)
                for n, name in enumerate(("q_ln_w", "q_ln_b", "k_ln_w", "k_ln_b")):
                    sp.dma_start(keep.qk_ln[:, n, :], io["L1_attn_" + name].partition_broadcast(P)).then_inc(keep.ln_in, 16)

            @block.tensor
            def _(pe):
                def turn(n):
                    rows, cols = shape(n)
                    if n >= 2:
                        pe.wait_ge(tr_l, n - 1)
                    for b, src in enumerate(jobs[n][0]):
                        last = pe.transpose(tr[n % 2][0:cols, b, 0:rows], src, keep.ident[0:rows, 0:rows])
                    last.then_inc(tr_ps, 1)

                pe.wait_ge(w_in, 64)
                for n in range(JX):
                    turn(n)
                for j in range(ST):
                    pe.wait_ge(n1.x_ok, j + 1)
                    turn(JX + j)
                for n in range(2):
                    pe.wait_ge(tr_l, JX + 4 * n + 4)
                    for t in range(4):
                        cols = slice((4 * n + t) * P, (4 * n + t + 1) * P)
                        terms = []
                        for k in range(DK):
                            terms += [(xT_h[:, k, cols], agT_h[:, k, :]), (xT_l[:, k, cols], agT_h[:, k, :]),
                                      (xT_h[:, k, cols], agT_l[:, k, :])]
                        last = three(pe, pag[n][:, t, :], terms)
                    last.then_inc(ag_ps, 1)

                def ffn(j, start):
                    cols = slice(j * P, (j + 1) * P)
                    if start:
                        if j >= 4:
                            pe.wait_ge(out_ev, j - 3)
                        terms = []
                        for k in range(DK):
                            terms += [(xT_h[:, k, cols], wT_h[:, k, :]), (xT_l[:, k, cols], wT_h[:, k, :]),
                                      (xT_h[:, k, cols], wT_l[:, k, :])]
                        three(pe, po[j % 4][:], terms, stop=False)
                    else:
                        bh, bl = (b[:].rearrange("r t n -> r (t n)") for b in (bT_h, bT_l))
                        three(pe, po[j % 4][:], [(loT_h[:, j, :], bh), (loT_l[:, j, :], bh), (loT_h[:, j, :], bl)],
                              start=False).then_inc(out_ps, 1)

                for j in range(4):
                    ffn(j, True)
                pe.wait_ge(route, 2 + NR - 1 + 3)
                for n in range(2):
                    turn(JL + n)
                pe.wait_ge(tr_l, JL + 2)
                for j in range(4):
                    ffn(j, False)
                for j in range(4, ST):
                    ffn(j, True)
                    ffn(j, False)

            @block.scalar
            def _(act):
                def split(n):
                    rows, cols = shape(n)
                    act.wait_ge(tr_ps, n + 1)
                    dst = jobs[n][1][0]
                    act.copy(dst[:, :, jobs[n][2]], tr[n % 2][0:cols, :, 0:rows]).then_inc(tr_h, 1)

                for n in range(JX):
                    split(n)
                n1.root(act)
                for n in range(JX, JL):
                    split(n)
                for n in range(2):
                    act.wait_ge(ag_ps, n + 1)
                    act.copy(ag[:, 4 * n:4 * n + 4, :], pag[n][:]).then_inc(ag_ev, 1)
                for n in range(JL, JL + 2):
                    split(n)
                n2.root(act)

            @block.vector
            def _(dve):
                def split(n):
                    rows, cols = shape(n)
                    dst_h, dst_l = jobs[n][1]
                    dve.wait_ge(tr_h, n + 1)
                    dve.tensor_tensor(dst_l[:, :, jobs[n][2]], tr[n % 2][0:cols, :, 0:rows],
                                      dst_h[:, :, jobs[n][2]].bitcast(F32), ALU.subtract).then_inc(tr_l, 1)

                for j in range(ST):
                    n1.stats(dve, j, keep.x[:, j, :])
                n1.variance(dve)
                for n in range(JX):
                    split(n)
                n1.inverse(dve)
                for j in range(ST):
                    n1.apply(dve, j, keep.x[:, j, :])
                    if j >= 1:
                        split(JX + j - 1)
                split(JL - 1)
                scores = ag[:, :, MR:MR + NR]
                dve.wait_ge(ag_ev, 2)
                dve.wait_ge(b_in, 32)
                for j in range(ST):
                    last = dve.tensor_tensor(ag[:, j, MR:MR + NR], ag[:, j, MR:MR + NR], gate_b[:], ALU.add)
                last.then_inc(route, 1)
                dve.wait_ge(route, 1)
                dve.tensor_reduce(top[:], scores, AX.X, ALU.max).then_inc(route, 1)
                dve.wait_ge(route, 2)
                dve.tensor_tensor(less[:], scores, top[:].unsqueeze(2).to_broadcast([P, ST, NR]), ALU.is_lt).then_inc(route, 1)
                dve.wait_ge(route, 3)
                for r in range(1, NR - 1):
                    dve.tensor_tensor(less[:, :, r], less[:, :, r], less[:, :, r - 1], ALU.mult).then_inc(route, 1)
                    dve.wait_ge(route, 3 + r)
                for r in range(1, NR):
                    c0, c1 = RANKS[r - 1], RANKS[r]
                    dve.tensor_tensor(ag[:, :, c0:c1], ag[:, :, c0:c1],
                                      less[:, :, r - 1:r].to_broadcast([P, ST, c1 - c0]), ALU.mult).then_inc(route, 1)
                for n in range(JL, JL + 2):
                    split(n)
                for j in range(ST):
                    dve.wait_ge(out_ps, j + 1)
                    dve.wait_ge(biased, j + 1)
                    dve.tensor_tensor(keep.x[:, j, :], po[j % 4][:], keep.x[:, j, :], ALU.add).then_inc(out_ev, 1)
                    dve.wait_ge(out_ev, j + 1)
                    n2.stats(dve, j, keep.x[:, j, :])
                n2.variance(dve)
                n2.inverse(dve)
                for j in range(ST):
                    n2.apply(dve, j, keep.x[:, j, :])

            @block.gpsimd
            def _(pool):
                pool.wait_ge(b_in, 32)
                for j in range(ST):
                    pool.wait_ge(tr_ps, JX + j + 1)
                    pool.tensor_tensor(keep.x[:, j, :], keep.x[:, j, :], bias[:], ALU.add).then_inc(biased, 1)


def stage_qkv(nc, io, keep):
    with ExitStack() as ctx:
        al = Alloc(nc, ctx)
        xT_h, xT_l = al.sb("x2T_h", [P, DK, S], F32R), al.sb("x2T_l", [P, DK, S], F32R)
        NW = 3 * D // P
        wT_h, wT_l = al.sb("wqkvT_h", [P, DK, 3 * D], F32R), al.sb("wqkvT_l", [P, DK, 3 * D], F32R)
        tr = [al.ps(f"d_tr{i}", [P, DK, P]) for i in range(2)]
        po = [al.ps(f"d_po{i}", [P, D]) for i in range(4)]
        nq = Norm(al, "nqk", 2 * ST)
        names = "tr_ps tr_h tr_l out_ps clip scaled_q scaled_k done"
        tr_ps, tr_h, tr_l, out_ps, clip, scaled_q, scaled_k, done = (al.sem("d_" + n) for n in names.split())
        jobs = [([keep.x[:, j, k * P:(k + 1) * P] for k in range(DK)], xT_h, xT_l, slice(j * P, (j + 1) * P)) for j in range(ST)]
        jobs += [([keep.wqkv[:, t, k * P:(k + 1) * P] for k in range(DK)], wT_h, wT_l, slice(t * P, (t + 1) * P)) for t in range(NW)]
        order = [(j, c) for c in range(2) for j in range(ST)] + [(j, 2) for j in range(ST)]
        dest = (keep.q, keep.k, keep.v)

        with nc.Block() as block:

            @block.tensor
            def _(pe):
                pe.wait_ge(keep.wqkv_in, 16)
                for n, (src, h, l, cols) in enumerate(jobs):
                    if n >= 2:
                        pe.wait_ge(tr_l, n - 1)
                    for k in range(DK):
                        last = pe.transpose(tr[n % 2][:, k, :], src[k], keep.ident[:])
                    last.then_inc(tr_ps, 1)
                for n, (j, c) in enumerate(order):
                    if j == 0:
                        pe.wait_ge(tr_l, ST + 4 * (c + 1))
                    if n >= 4:
                        pe.wait_ge(clip, n - 3)
                    rows, cols = slice(j * P, (j + 1) * P), slice(c * D, (c + 1) * D)
                    terms = []
                    for k in range(DK):
                        terms += [(xT_h[:, k, rows], wT_h[:, k, cols]), (xT_l[:, k, rows], wT_h[:, k, cols]),
                                  (xT_h[:, k, rows], wT_l[:, k, cols])]
                    three(pe, po[n % 4][:], terms).then_inc(out_ps, 1)

            @block.scalar
            def _(act):
                for n, (src, h, l, cols) in enumerate(jobs):
                    act.wait_ge(tr_ps, n + 1)
                    act.copy(h[:, :, cols], tr[n % 2][:]).then_inc(tr_h, 1)
                nq.root(act)

            @block.vector
            def _(dve):
                for n, (src, h, l, cols) in enumerate(jobs):
                    dve.wait_ge(tr_h, n + 1)
                    dve.tensor_tensor(l[:, :, cols], tr[n % 2][:], h[:, :, cols].bitcast(F32), ALU.subtract).then_inc(tr_l, 1)
                for n, (j, c) in enumerate(order):
                    dve.wait_ge(out_ps, n + 1)
                    dve.tensor_scalar(dest[c][:, j, :], po[n % 4][:], CLIP, -CLIP, ALU.min, ALU.max).then_inc(clip, 1)
                    if c < 2:
                        dve.wait_ge(clip, n + 1)
                        nq.stats(dve, n, dest[c][:, j, :])
                    if n == 2 * ST:
                        nq.variance(dve)
                nq.inverse(dve)
                dve.wait_ge(keep.ln_in, 64)
                for t in list(range(ST, 2 * ST)) + list(range(ST)):
                    nq.apply(dve, t, dest[t // ST][:, t % ST, :])
                for j in range(ST):
                    dve.wait_ge(nq.x_ok, ST + j + 1)
                    dve.scalar_tensor_tensor(out=keep.q[:, j, :], in0=keep.q[:, j, :], scalar=SCALE1,
                                             in1=keep.qk_ln[:, 0, :], op0=ALU.mult, op1=ALU.mult).then_inc(scaled_q, 1)
                for j in range(ST):
                    dve.wait_ge(scaled_q, j + 1)
                    dve.scalar_tensor_tensor(out=keep.q[:, j, :], in0=keep.qk_ln[:, 1, :], scalar=SCALE1,
                                             in1=keep.q[:, j, :], op0=ALU.mult, op1=ALU.add).then_inc(done, 1)

            @block.gpsimd
            def _(pool):
                pool.wait_ge(keep.ln_in, 64)
                for j in range(ST):
                    pool.wait_ge(nq.x_ok, j + 1)
                    pool.tensor_tensor(keep.k[:, j, :], keep.k[:, j, :], keep.qk_ln[:, 2, :], ALU.mult).then_inc(scaled_k, 1)
                for j in range(ST):
                    pool.wait_ge(scaled_k, j + 1)
                    pool.tensor_tensor(keep.k[:, j, :], keep.k[:, j, :], keep.qk_ln[:, 3, :], ALU.add).then_inc(done, 1)


H1 = 32
HG = 4
GROUPS = H1 // HG
EX = 16


def alibi_columns():
    m = np.arange(1, H1 + 1, dtype=np.float32) * np.float32(8.0 / H1)
    slope = np.float32(1.0) / np.power(np.float32(2.0), m)
    bits = slope.view(np.uint32)
    slope_h = ((bits + np.uint32(0x800)) & np.uint32(0xFFFFF000)).view(np.float32)
    slope_l = slope - slope_h
    q, k = (np.zeros((GROUPS, P, ST, HG, EX), np.float32) for _ in range(2))
    pos = (np.arange(ST)[None, :] * P + np.arange(P)[:, None]).astype(np.float32)[None, :, :, None]
    sh, sl = (x.reshape(GROUPS, 1, 1, HG) for x in (slope_h, slope_l))
    k[..., 0] = k[..., 1] = 1.0
    q[..., 2], q[..., 3], q[..., 4], q[..., 5] = sh, sl, -pos, -pos
    k[..., 2], k[..., 3], k[..., 4], k[..., 5] = pos, pos, sh, sl
    return q, k


def stage_alibi(nc, io, keep):
    with ExitStack() as ctx:
        al = Alloc(nc, ctx)
        qx, kx = al.sb("qx", [P, ST, HG, 64], F32R), al.sb("kx", [P, ST, HG, 64], F32R)
        qT, kT = al.sb("qT", [P, 2, S], F32R), al.sb("kT", [P, 2, S], F32R)
        vx = al.sb("vx", [P, ST, HG, 32])
        probs = [al.sb(f"l1_probs{i}", [P, HG, S]) for i in range(2)]
        nmax, nmax_h = al.sb("nmax", [P, HG, ST]), al.sb("nmax_h", [P, HG, ST], F32R)
        nmax_hl = al.sb("nmax_hl", [P, HG, ST, 2])
        oT = al.sb("oT", [P, S])
        rsum = al.sb("rsum", [P, ST, HG])
        sc = [al.ps(f"l1_sc{i}", [P, S]) for i in range(2)]
        pv, pm = al.ps("l1_pv", [P, S]), al.ps("l1_pm", [P, S])
        names = ("x_in ones qx_ok kx_ok vx_ok t_ps qT_ok kT_ok scores maxed split mT_ps mT_ok sE exped pv_ps oT_ok "
                 "back recip done")
        (x_in, ones, qx_ok, kx_ok, vx_ok, t_ps, qT_ok, kT_ok, scores, maxed, split, mT_ps, mT_ok, sE, exped, pv_ps, oT_ok,
         back, recip, done) = (al.sem("e_" + n) for n in names.split())
        STEPS = HG * ST

        def cols(w, g):
            return w[:, :, bass.ds(g * (HG * HD1), HG * HD1)].rearrange("p j (h c) -> p j h c", h=HG)

        def rows(h):
            return slice(64 * (h % 2), 64 * (h % 2) + 64), h // 2

        with nc.Block() as block:

            @block.sync
            def _(sp):
                def load(g):
                    for dst, src in ((qx, "alibi_q"), (kx, "alibi_k")):
                        sp.dma_start(dst[:, :, :, 0:EX].bitcast(F32), io[src][bass.ds(g, 1)].squeeze(0) if 0 else
                                     io[src][g]).then_inc(x_in, 16)

                load(0)
                with sp.Fori(1, GROUPS) as g:
                    sp.wait_ge(t_ps, 4 * g)
                    load(g)

            @block.tensor
            def _(pe):
                def group(g):
                    pe.wait_ge(x_in, 32 * g + 32)
                    for n, (src, ok) in enumerate(((qx, qx_ok), (kx, kx_ok))):
                        pe.wait_ge(ok, 3 * g + 3)
                        for b in range(2):
                            if n == 1:
                                pe.wait_ge(qT_ok, 2 * g + b + 1)
                            for j in range(ST):
                                last = pe.transpose(sc[b][:, j * P:(j + 1) * P],
                                                    src[:, j, 2 * b:2 * b + 2, :].rearrange("p h c -> p (h c)").bitcast(F32),
                                                    keep.ident[:])
                            last.then_inc(t_ps, 1)

                    def maxima(h):
                        pe.wait_ge(split, HG * g + h + 1)
                        if h >= 1:
                            pe.wait_ge(mT_ok, HG * g + h)
                        for i in range(ST):
                            last = pe.transpose(pm[0:2, i * P:(i + 1) * P], nmax_hl[:, h, i, :], keep.ident[:])
                        last.then_inc(mT_ps, 1)

                    for n in range(STEPS):
                        h, i = n // ST, n % ST
                        r, b = rows(h)
                        if n < 2:
                            pe.wait_ge(kT_ok, 2 * g + 2)
                            pe.wait_ge(qT_ok, 2 * g + 2)
                        else:
                            pe.wait_ge(maxed, STEPS * g + n - 1)
                        if i == 3 and h >= 1:
                            maxima(h - 1)
                        width = (i + 1) * P
                        for c0 in range(0, width, BANK):
                            c1 = min(width, c0 + BANK)
                            pe.matmul(sc[n % 2][:, c0:c1], qT[r, b, i * P:(i + 1) * P], kT[r, b, c0:c1],
                                      start=True, stop=c1 < width)
                        pe.matmul(sc[n % 2][:, width - P:width], keep.ident_b[:], keep.mask[:],
                                  start=False, stop=True).then_inc(scores, 1)
                    maxima(HG - 1)

                    def values(j):
                        pe.wait_ge(exped, STEPS * g + HG * (j + 1))
                        if j == 0:
                            pe.wait_ge(vx_ok, g + 1)
                        for half in range(j // 4, 2):
                            c0, c1 = max(j * P, half * BANK), (half + 1) * BANK
                            for h in range(HG):
                                last = pe.matmul(pv[32 * h:32 * h + 32, c0:c1], vx[:, j, h, :], probs[j % 2][:, h, c0:c1],
                                                 start=(j == 0), stop=(j == 4 * half + 3))
                        last.then_inc(pv_ps, 1)

                    for n in range(STEPS):
                        j, h = n // HG, n % HG
                        r, b = rows(h)
                        if n < 2:
                            pe.wait_ge(maxed, STEPS * (g + 1))
                        else:
                            pe.wait_ge(exped, STEPS * g + n - 1)
                        if j == 0:
                            pe.wait_ge(mT_ok, HG * g + h + 1)
                        for c0, c1 in ((j * P, BANK), (max(j * P, BANK), S)):
                            if c0 < c1:
                                last = pe.matmul(sc[n % 2][:, c0:c1], kT[r, b, j * P:(j + 1) * P], qT[r, b, c0:c1],
                                                 start=True, stop=not c0 <= j * P < c1)
                            if c0 <= j * P < c1:
                                last = pe.matmul(sc[n % 2][:, j * P:(j + 1) * P], keep.ident_b[:], keep.mask_t[:],
                                                 start=False, stop=True)
                        last.then_inc(sE, 1)
                        if h == 2 and j >= 1:
                            values(j - 1)
                    values(ST - 1)

                    pe.wait_ge(oT_ok, 2 * g + 2)
                    for j in range(ST):
                        last = pe.transpose(sc[0][:, j * P:(j + 1) * P], oT[:, j * P:(j + 1) * P], keep.ident[:])
                    last.then_inc(back, 1)

                def first(g):
                    group(g)

                group(0)
                with pe.Fori(1, GROUPS) as g:
                    pe.wait_ge(done, g)
                    group(g)

            @block.scalar
            def _(act):
                def group(g):
                    act.copy(qx[:, :, :, 16:32], cols(keep.q, g)).then_inc(qx_ok, 1)
                    act.copy(kx[:, :, :, 16:32], cols(keep.k, g)).then_inc(kx_ok, 1)
                    for b in range(2):
                        act.wait_ge(t_ps, 4 * g + b + 1)
                        act.copy(qT[:, b, :], sc[b][:]).then_inc(qT_ok, 1)
                    for h in range(HG):
                        act.wait_ge(mT_ps, HG * g + h + 1)
                        act.copy(qT[64 * (h % 2):64 * (h % 2) + 2, h // 2, :], pm[0:2, :]).then_inc(mT_ok, 1)
                    for n in range(STEPS):
                        j, h = n // HG, n % HG
                        act.wait_ge(sE, STEPS * g + n + 1)
                        if h == 0 and j >= 2:
                            act.wait_ge(pv_ps, ST * g + j - 1)
                        act.activation(probs[j % 2][:, h, j * P:S], sc[n % 2][:, j * P:S], ACT.Exp).then_inc(exped, 1)
                    act.wait_ge(pv_ps, ST * g + ST)
                    act.copy(oT[:, 0:BANK], pv[:, 0:BANK]).then_inc(oT_ok, 1)

                group(0)
                with act.Fori(1, GROUPS) as g:
                    act.wait_ge(t_ps, 4 * g)
                    group(g)

            @block.vector
            def _(dve):
                def group(g):
                    dve.tensor_copy(qx[:, :, :, 32:48], cols(keep.q, g)).then_inc(qx_ok, 1)
                    dve.tensor_copy(kx[:, :, :, 48:64], cols(keep.k, g)).then_inc(kx_ok, 1)
                    dve.wait_ge(qx_ok, 3 * g + 2)
                    dve.tensor_tensor(qx[:, :, :, 48:64], cols(keep.q, g), qx[:, :, :, 32:48].bitcast(F32),
                                      ALU.subtract).then_inc(qx_ok, 1)
                    dve.wait_ge(kx_ok, 3 * g + 2)
                    dve.tensor_tensor(kx[:, :, :, 32:48], cols(keep.k, g), kx[:, :, :, 48:64].bitcast(F32),
                                      ALU.subtract).then_inc(kx_ok, 1)
                    for b in range(2):
                        dve.wait_ge(t_ps, 4 * g + 3 + b)
                        dve.tensor_copy(kT[:, b, :], sc[b][:]).then_inc(kT_ok, 1)
                    for n in range(STEPS):
                        h, i = n // ST, n % ST
                        dve.wait_ge(scores, STEPS * g + n + 1)
                        dve.tensor_reduce(nmax[:, h, i:i + 1], sc[n % 2][:, 0:(i + 1) * P], AX.X, ALU.max,
                                          negate=True).then_inc(maxed, 1)
                        if i == ST - 1:
                            dve.wait_ge(maxed, STEPS * g + n + 1)
                            dve.tensor_copy(nmax_h[:, h, :], nmax[:, h, :]).then_inc(recip, 1)
                            dve.wait_ge(recip, (HG + 1) * g + h + 1)
                            dve.tensor_copy(nmax_hl[:, h, :, 0], nmax_h[:, h, :].bitcast(F32))
                            dve.tensor_tensor(nmax_hl[:, h, :, 1], nmax[:, h, :], nmax_h[:, h, :].bitcast(F32),
                                              ALU.subtract).then_inc(split, 1)
                    dve.wait_ge(pv_ps, ST * g + ST)
                    dve.tensor_copy(oT[:, BANK:S], pv[:, BANK:S]).then_inc(oT_ok, 1)
                    dve.wait_ge(back, g + 1)
                    byhead = sc[0][:].rearrange("p (j h c) -> p j h c", j=ST, h=HG)
                    dve.reciprocal(rsum[:], byhead[:, :, :, HD1]).then_inc(recip, 1)
                    dve.wait_ge(recip, (HG + 1) * (g + 1))
                    dve.tensor_tensor(cols(keep.attn, g), byhead[:, :, :, 0:HD1],
                                      rsum[:].unsqueeze(3).to_broadcast([P, ST, HG, HD1]), ALU.mult).then_inc(done, 1)

                group(0)
                with dve.Fori(1, GROUPS) as g:
                    group(g)

            @block.gpsimd
            def _(pool):
                pool.memset(vx[:], 0.0).then_inc(ones, 1)
                pool.wait_ge(ones, 1)
                pool.memset(vx[:, :, :, HD1:HD1 + 1], 1.0).then_inc(ones, 1)
                pool.wait_ge(ones, 2)
                pool.tensor_copy(vx[:, :, :, 0:HD1], cols(keep.v, 0)).then_inc(vx_ok, 1)
                with pool.Fori(1, GROUPS) as g:
                    pool.wait_ge(pv_ps, ST * g)
                    pool.tensor_copy(vx[:, :, :, 0:HD1], cols(keep.v, g)).then_inc(vx_ok, 1)


IM = 1792
IT = IM // P


def stage_gated(nc, io, keep, upto=9):
    with ExitStack() as ctx:
        al = Alloc(nc, ctx)
        xT_h, xT_l = al.sb("x3T_h", [P, DK, S], F32R), al.sb("x3T_l", [P, DK, S], F32R)
        RING = 3
        gT, uT, dT = (al.sb(n, [P, IT, D]) for n in ("gT", "uT", "dT"))
        lnw = al.sb("lnw", [P, D])
        ms, m2 = al.sb("ms", [P, ST]), al.sb("m2", [P, ST])
        n3, n4 = Norm(al, "n3", ST), Norm(al, "n4", ST)
        nr = Norm(al, "nr", ST)
        names = "wo_in ln_in w_in tr_ps tr_h tr_l wt_ps wt_act wt_dve out_ps out_ev nx ms"
        wo_in, ln_in, w_in, tr_ps, tr_h, tr_l, wt_ps, wt_act, wt_dve, out_ps, out_ev, nx, ms_ok = (
            al.sem("g_" + n) for n in names.split())
        w_ins = [al.sem(f"g_w_in{i}") for i in range(RING)]
        tr_src = keep.attn

        with ExitStack() as c1:
            a1 = Alloc(nc, c1)
            wo_f = a1.sb("wo_f", [P, DK, D])
            woT_h, woT_l = a1.sb("woT_h", [P, DK, D], F32R), a1.sb("woT_l", [P, DK, D], F32R)
            stage = a1.sb("w_stage", [P, RING, 3, D])
            tr = [a1.ps(f"g_tr{i}", [P, DK, P]) for i in range(4)]
            po = [a1.ps(f"g_po{i}", [P, D]) for i in range(4)]
            jobs = [([wo_f[:, t, k * P:(k + 1) * P] for k in range(DK)], woT_h, woT_l, slice(t * P, (t + 1) * P)) for t in range(DK)]
            jobs += [([keep.attn[:, j, k * P:(k + 1) * P] for k in range(DK)], xT_h, xT_l, slice(j * P, (j + 1) * P)) for j in range(ST)]
            JX = len(jobs)
            jobs += [([keep.attn[:, j, k * P:(k + 1) * P] for k in range(DK)], xT_h, xT_l, slice(j * P, (j + 1) * P)) for j in range(ST)]
            wjobs = [(t, c) for t in range(IT) for c in range(3)]

            with nc.Block() as block:

                @block.sync
                def _(sp):
                    sp.dma_start(wo_f[:], io["L1_attn_w_out"].rearrange("(t p) n -> p t n", p=P)).then_inc(wo_in, 16)
                    sp.dma_start(lnw[:], io["L1_ffn_ln_w"].partition_broadcast(P)).then_inc(ln_in, 16)
                    for t in range(IT):
                        if t >= RING:
                            sp.wait_ge(wt_ps, 3 * (t - RING) + 3)
                        r = slice(t * P, (t + 1) * P)
                        sp.dma_start(stage[:, t % RING, 0, :], io["L1_ffn_gate_w"][r, :]).then_inc(w_ins[t % RING], 16)
                        sp.dma_start(stage[:, t % RING, 1, :], io["L1_ffn_up_w"][r, :]).then_inc(w_ins[t % RING], 16)
                        sp.dma_start(stage[:, t % RING, 2, :].rearrange("p (k c) -> p k c", k=DK),
                                     io["L1_ffn_down_w"][:, r].rearrange("(k p) c -> p k c", p=P)).then_inc(w_ins[t % RING], 16)

                @block.tensor
                def _(pe):
                    def turn(n):
                        if n >= 2:
                            pe.wait_ge(tr_l, n - 1)
                        for k, src in enumerate(jobs[n][0]):
                            last = pe.transpose(tr[n % 2][:, k, :], src, keep.ident[:])
                        last.then_inc(tr_ps, 1)

                    def turn_weight(m):
                        t, c = wjobs[m]
                        if c == 0:
                            pe.wait_ge(w_ins[t % RING], 48 * (t // RING + 1))
                        if m >= 2:
                            pe.wait_ge((wt_act, wt_dve)[m % 2], m // 2)
                        for k in range(DK):
                            last = pe.transpose(tr[2 + m % 2][:, k, :], stage[:, t % RING, c, k * P:(k + 1) * P], keep.ident[:])
                        last.then_inc(wt_ps, 1)

                    pe.wait_ge(wo_in, 16)
                    for n in range(JX):
                        turn(n)
                    for j in range(ST):
                        pe.wait_ge(tr_l, DK + j + 1)
                        if j >= 4:
                            pe.wait_ge(out_ev, j - 3)
                        rows = slice(j * P, (j + 1) * P)
                        terms = []
                        for k in range(DK):
                            terms += [(xT_h[:, k, rows], woT_h[:, k, :]), (xT_l[:, k, rows], woT_h[:, k, :]),
                                      (xT_h[:, k, rows], woT_l[:, k, :])]
                        three(pe, po[j % 4][:], terms).then_inc(out_ps, 1)
                    for m in range(len(wjobs)):
                        turn_weight(m)
                    for j in range(ST):
                        pe.wait_ge(nx, j + 1)
                        turn(JX + j)

                @block.scalar
                def _(act):
                    def split(n):
                        act.wait_ge(tr_ps, n + 1)
                        act.copy(jobs[n][1][:, :, jobs[n][3]], tr[n % 2][:]).then_inc(tr_h, 1)

                    for n in range(JX):
                        split(n)
                    for m in range(0, len(wjobs), 2):
                        t, c = wjobs[m]
                        act.wait_ge(wt_ps, m + 1)
                        act.copy((gT, uT, dT)[c][:, t, :], tr[2][:].rearrange("p k c -> p (k c)")).then_inc(wt_act, 1)
                        if m == 20:
                            n3.root(act)
                    nr.root(act)
                    for n in range(JX, len(jobs)):
                        split(n)

                @block.vector
                def _(dve):
                    def split(n):
                        dve.wait_ge(tr_h, n + 1)
                        h, l, cols = jobs[n][1:]
                        dve.tensor_tensor(l[:, :, cols], tr[n % 2][:], h[:, :, cols].bitcast(F32), ALU.subtract).then_inc(tr_l, 1)

                    for n in range(JX):
                        split(n)
                    for j in range(ST):
                        dve.wait_ge(out_ps, j + 1)
                        dve.tensor_tensor(keep.x[:, j, :], po[j % 4][:], keep.x[:, j, :], ALU.add).then_inc(out_ev, 1)
                        dve.wait_ge(out_ev, j + 1)
                        n3.stats(dve, j, keep.x[:, j, :])
                    n3.variance(dve)

                    def weight(m):
                        t, c = wjobs[m]
                        dve.wait_ge(wt_ps, m + 1)
                        dve.tensor_copy((gT, uT, dT)[c][:, t, :], tr[3][:].rearrange("p k c -> p (k c)")).then_inc(wt_dve, 1)

                    for m in range(1, 26, 2):
                        weight(m)
                    n3.inverse(dve)
                    for j in range(ST):
                        n3.apply(dve, j, keep.x[:, j, :])
                    for j in range(ST):
                        dve.wait_ge(n3.x_ok, j + 1)
                        nr.stats(dve, j, keep.x[:, j, :])
                    dve.wait_ge(nr.mv_ok, ST)
                    dve.tensor_tensor(m2[:], nr.mv[:, :, 0], nr.mv[:, :, 0], ALU.mult).then_inc(ms_ok, 1)
                    dve.wait_ge(ms_ok, 1)
                    dve.scalar_tensor_tensor(out=nr.sd[:], in0=nr.mv[:, :, 1], scalar=1e-5, in1=m2[:], op0=ALU.add,
                                             op1=ALU.add).then_inc(nr.ve_ok, 1)
                    for m in range(27, len(wjobs), 2):
                        weight(m)
                    nr.inverse(dve)
                    dve.wait_ge(ln_in, 16)
                    for j in range(ST):
                        dve.scalar_tensor_tensor(out=keep.attn[:, j, :], in0=keep.x[:, j, :], scalar=nr.rs[:, j:j + 1],
                                                 in1=lnw[:], op0=ALU.mult, op1=ALU.mult).then_inc(nx, 1)
                    for n in range(JX, len(jobs)):
                        split(n)

        if upto == 3:
            return
        names = "wh wl gu ex den rec sil a_f a_h a_l down fin"
        wh, wl, gu, ex_ok, den_ok, rec_ok, sil_ok, af_ok, ah_ok, al_ok, down, fin = (al.sem("h_" + n) for n in names.split())
        w_h = [[al.sb(f"{n}_h{i}", [P, D], F32R) for n in "gud"] for i in range(2)]
        w_l = [[al.sb(f"{n}_l{i}", [P, D], F32R) for n in "gud"] for i in range(2)]
        ex, den = al.sb("ex", [P, BANK]), al.sb("den", [P, BANK])
        act_f = al.sb("act_f", [P, BANK])
        a_h = [al.sb(f"a_h{i}", [P, BANK], F32R) for i in range(2)]
        a_l = [al.sb(f"a_l{i}", [P, BANK], F32R) for i in range(2)]
        pg, pu = ([al.ps(f"h_{n}{i}", [P, BANK]) for i in range(2)] for n in "gu")
        pd = [al.ps(f"h_d{i}", [P, D]) for i in range(4)]
        steps = 2 * IT

        with nc.Block() as block:

            def each(eng, step, half):
                base = half * IT
                for t in range(2):
                    step(base, base + t, t, t)
                with eng.Fori(1, IT // 2 - 1) as i:
                    for u in range(2):
                        step(base, i * 2 + (base + u), i * 2 + u, u)
                for u in range(2):
                    step(base, base + IT - 2 + u, IT - 2 + u, u)

            @block.tensor
            def _(pe):
                def down_part(n, u, first, last):
                    pe.wait_ge(ah_ok, n + 1)
                    pe.wait_ge(al_ok, n + 1)
                    for j in range(4):
                        rows = slice(j * P, (j + 1) * P)
                        end = three(pe, pd[j][:], [(a_h[u][:, rows], w_h[u][2][:]), (a_l[u][:, rows], w_h[u][2][:]),
                                                   (a_h[u][:, rows], w_l[u][2][:])], start=first, stop=last)
                    end.then_inc(down, 1)

                def make(half):
                    def step(base, n, t, u):
                        first, cols = isinstance(t, int) and t == 0, slice(half * BANK, (half + 1) * BANK)
                        pe.wait_ge(wh, 3 * n + 3)
                        pe.wait_ge(wl, 3 * n + 3)
                        if not (isinstance(n, int) and n < 2):
                            pe.wait_ge(af_ok, n - 1)
                        for c, dst in ((0, pg[u]), (1, pu[u])):
                            terms = []
                            for k in range(DK):
                                b = slice(k * P, (k + 1) * P)
                                h, l = w_h[u][c][:, b], w_l[u][c][:, b]
                                terms += [(h, xT_h[:, k, cols]), (h, xT_l[:, k, cols]), (l, xT_h[:, k, cols])]
                            three(pe, dst[:], terms).then_inc(gu, 1)
                        if not first:
                            before = isinstance(t, int) and t == 1
                            down_part(n - 1, 1 - u, before, False)
                    return step

                for half in range(2):
                    if half == 1:
                        pe.wait_ge(fin, 4)
                    each(pe, make(half), half)
                    down_part(half * IT + IT - 1, 1, False, True)

            @block.scalar
            def _(act):
                def step(base, n, t, u):
                    if not (isinstance(n, int) and n < 2):
                        act.wait_ge(down, n - 1)
                    for c, w in enumerate((gT, uT, dT)):
                        src = w[:, t, :] if isinstance(t, int) else w[:, bass.ds(t, 1), :].rearrange("p o c -> p (o c)")
                        act.copy(w_h[u][c][:], src).then_inc(wh, 1)
                    act.wait_ge(gu, 2 * n + 1)
                    if not (isinstance(n, int) and n == 0):
                        act.wait_ge(den_ok, n)
                    act.activation(ex[:], pg[u][:], ACT.Exp, scale=-1.0).then_inc(ex_ok, 1)
                    act.wait_ge(af_ok, n + 1)
                    act.copy(a_h[u][:], act_f[:]).then_inc(ah_ok, 1)

                for half in range(2):
                    each(act, step, half)
                n4.root(act)

            @block.gpsimd
            def _(pool):
                def step(base, n, t, u):
                    if not (isinstance(n, int) and n < 2):
                        pool.wait_ge(down, n - 1)
                    for c, w in enumerate((gT, uT, dT)):
                        src = w[:, t, :] if isinstance(t, int) else w[:, bass.ds(t, 1), :].rearrange("p o c -> p (o c)")
                        pool.wait_ge(wh, 3 * n + c + 1)
                        pool.tensor_tensor(w_l[u][c][:], src, w_h[u][c][:].bitcast(F32), ALU.subtract).then_inc(wl, 1)

                for half in range(2):
                    each(pool, step, half)

            @block.vector
            def _(dve):
                def step(base, n, t, u):
                    dve.wait_ge(ex_ok, n + 1)
                    dve.tensor_scalar(den[:], ex[:], 1.0, None, ALU.add).then_inc(den_ok, 1)
                    dve.wait_ge(den_ok, n + 1)
                    dve.reciprocal(den[:], den[:]).then_inc(rec_ok, 1)
                    dve.wait_ge(rec_ok, n + 1)
                    dve.wait_ge(gu, 2 * n + 2)
                    dve.tensor_tensor(act_f[:], pg[u][:], den[:], ALU.mult).then_inc(sil_ok, 1)
                    dve.wait_ge(sil_ok, n + 1)
                    dve.tensor_tensor(act_f[:], pu[u][:], act_f[:], ALU.mult).then_inc(af_ok, 1)
                    dve.wait_ge(ah_ok, n + 1)
                    dve.tensor_tensor(a_l[u][:], act_f[:], a_h[u][:].bitcast(F32), ALU.subtract).then_inc(al_ok, 1)

                for half in range(2):
                    each(dve, step, half)
                    dve.wait_ge(down, (half + 1) * IT)
                    for j in range(4):
                        x = keep.x[:, 4 * half + j, :]
                        dve.tensor_tensor(x, pd[j][:], x, ALU.add).then_inc(fin, 1)
                        dve.wait_ge(fin, 4 * half + j + 1)
                        n4.stats(dve, 4 * half + j, x)
                n4.variance(dve)
                n4.inverse(dve)
                for j in range(ST):
                    n4.apply(dve, j, keep.x[:, j, :])


class Kept:
    pass


def program(nc, io, out, upto=9):
    with ExitStack() as ctx:
        al = Alloc(nc, ctx)
        keep = Kept()
        keep.x = al.sb("x_tok", [P, ST, D])
        keep.ident, keep.ident_b = al.sb("ident", [P, P]), al.sb("ident_b", [P, P], BF16)
        keep.mask, keep.mask_t = al.sb("mask", [P, P], BF16), al.sb("mask_t", [P, P], BF16)
        with ExitStack() as layer0:
            a0 = Alloc(nc, layer0)
            keep.cos, keep.sin = a0.sb("cos", [P, S]), a0.sb("sin", [P, S])
            keep.cqa_h, keep.cqa_l = a0.sb("cqa_h", [P, S], F32R), a0.sb("cqa_l", [P, S], F32R)
            keep.cqb_hh, keep.cqb_l = a0.sb("cqb_hh", [P, S], F32R), a0.sb("cqb_l", [64, S], F32R)
            keep.k_h, keep.k_l = a0.sb("k_h", [P, S], F32R), a0.sb("k_l", [P, S], F32R)
            keep.ckv = a0.sb("ckv", [P, ST, KVL])
            stage_latent(nc, io, keep)
            if upto >= 1:
                stage_mla(nc, io, keep)
        with ExitStack() as layer1:
            a1 = Alloc(nc, layer1)
            keep.attn = a1.sb("attn", [P, ST, D])
            with ExitStack() as heads:
                a2 = Alloc(nc, heads)
                keep.q, keep.k, keep.v = (a2.sb("l1_" + n, [P, ST, D]) for n in "qkv")
                with ExitStack() as proj:
                    a3 = Alloc(nc, proj)
                    keep.wqkv, keep.qk_ln = a3.sb("wqkv", [P, 3 * D // P, D]), a3.sb("qk_ln", [P, 4, D])
                    keep.wqkv_in, keep.ln_in = a3.sem("wqkv_in"), a3.sem("ln_in")
                    if upto >= 2:
                        stage_route(nc, io, keep)
                    if upto >= 3:
                        stage_qkv(nc, io, keep)
                if upto >= 3:
                    stage_alibi(nc, io, keep)
            if upto >= 3:
                stage_gated(nc, io, keep, upto)
        with ExitStack() as last:
            stored = Alloc(nc, last).sem("stored")
            with nc.Block() as block:

                @block.sync
                def _(sp):
                    sp.dma_start(out.rearrange("b (j p) d -> p (b j) d", p=P), keep.x[:]).then_inc(stored, 16)
                    sp.wait_ge(stored, 16)


_NAMES = {n.split("_", 2)[2] if n.startswith("L0_attn") else n: n for n in [
    "L0_attn_w_q_down", "L0_attn_w_q_up_nope", "L0_attn_w_q_up_rope", "L0_attn_w_kv_down", "L0_attn_w_k_rope",
    "L0_attn_w_uk", "L0_attn_w_uv", "L0_attn_w_out", "L0_ffn_W", "L0_ffn_b", "L0_ffn_A", "L0_ffn_B",
    "L0_ffn_gate_w", "L0_ffn_gate_b", "L1_attn_w_qkv", "L1_attn_q_ln_w", "L1_attn_q_ln_b", "L1_attn_k_ln_w",
    "L1_attn_k_ln_b", "L1_attn_w_out", "L1_ffn_ln_w", "L1_ffn_gate_w", "L1_ffn_up_w", "L1_ffn_down_w"]}


def layout(inputs):
    arrays = {"x": np.ascontiguousarray(inputs["L0_attn_hidden_states"])}
    for short, name in _NAMES.items():
        arrays[short] = np.ascontiguousarray(inputs[name])
    arrays["cos"], arrays["sin"] = rope_tables()
    arrays["alibi_q"], arrays["alibi_k"] = alibi_columns()
    return arrays


def kernel(**inputs):
    import concourse.bacc as bacc
    from concourse.bass_utils import run_bass_kernel_spmd

    nc = bacc.Bacc("TRN2", target_bir_lowering=False, num_devices=1)
    arrays = layout(inputs)
    io = {n: nc.dram_tensor(f"in_{n}", a.shape, mybir.dt.from_np(a.dtype), kind="ExternalInput").ap()
          for n, a in arrays.items()}
    out = nc.dram_tensor("out_0_dram", (1, S, D), F32, kind="ExternalOutput").ap()
    program(nc, io, out)
    r = run_bass_kernel_spmd(nc, [{f"in_{n}": a for n, a in arrays.items()}], core_ids=[0])
    return r.results[0]["out_0_dram"]
```

```python
from contextlib import ExitStack

import numpy as np

import concourse.bass as bass
from concourse import mybir

F32 = mybir.dt.float32
F32R = mybir.dt.float32r
BF16 = mybir.dt.bfloat16
ACT = mybir.ActivationFunctionType
ALU = mybir.AluOpType
AX = mybir.AxisListType

P = 128
S = 1024
D = 512
ST = S // P
DK = D // P
BANK = 512
NEG = -3.0e38

H0, QL, KVL, DN, DR, DV = 32, 192, 64, 128, 64, 128
PAIRS = H0 // 2
SCALE0 = float(1.0 / np.sqrt(np.float32(DN + DR)))


def rope_tables():
    freqs = np.float32(1.0) / np.float32(10000.0) ** (np.arange(0, DR, 2, dtype=np.float32) / np.float32(DR))
    wavelengths = np.float32(2.0 * np.pi) / freqs
    ramp = np.clip((wavelengths / np.float32(4096.0) - np.float32(1.0)) / np.float32(31.0), 0, 1).astype(np.float32)
    inv = (freqs / (np.float32(1.0) - ramp + ramp * np.float32(40.0))).astype(np.float32)
    f = np.arange(S, dtype=np.float32)[None, :] * inv[:, None]
    cos, sin = np.cos(f).astype(np.float32), np.sin(f).astype(np.float32)
    return np.tile(cos, (4, 1)), np.concatenate([-sin, sin, -sin, sin])


class Alloc:

    def __init__(self, nc, ctx):
        self.nc, self.ctx = nc, ctx

    def sb(self, name, shape, dt=F32):
        return self.ctx.enter_context(self.nc.sbuf_tensor(name, shape, dt))

    def ps(self, name, shape, dt=F32):
        return self.ctx.enter_context(self.nc.psum_tensor(name, shape, dt))

    def sem(self, name):
        return self.ctx.enter_context(self.nc.semaphore(name))


def from_one(eng, sem, value):
    if not (isinstance(value, int) and value <= 0):
        eng.wait_ge(sem, value)


def three(pe, out, terms, start=True, stop=True):
    for n, (l, r) in enumerate(terms):
        last = pe.matmul(out, l, r, start=start and n == 0, stop=stop and n == len(terms) - 1)
    return last


def stage_latent(nc, io, keep):
    with ExitStack() as ctx:
        al = Alloc(nc, ctx)
        xT_h = al.sb("xT_h", [P, DK, S], F32R)
        xT_l = al.sb("xT_l", [P, DK, S], F32R)
        WD = QL + 4 * 64
        wd_f = al.sb("wd_f", [P, DK, WD])
        wd_h = al.sb("wd_h", [P, DK, WD], F32R)
        wd_l = al.sb("wd_l", [P, DK, WD], F32R)
        k_f = al.sb("k_f", [P, S])
        k_sw = al.sb("k_sw", [P, S])
        tr = [al.ps(f"tr{i}", [P, DK, P]) for i in range(2)]
        pj = [al.ps(f"pj{i}", [P, BANK]) for i in range(4)]
        pc = al.ps("pc", [P, ST, KVL])

        x_in, wd_in = [al.sem(f"a_x_in{n}") for n in range(2)], al.sem("a_wd_in")
        const_ok, xT_ps, xTh_ok, xTl_ok = (al.sem(n) for n in ("a_const", "a_xT_ps", "a_xTh", "a_xTl"))
        wdh_ok, wdl_ok = al.sem("a_wdh"), al.sem("a_wdl")
        proj_ps, act_ev, dve_ev = al.sem("a_proj"), al.sem("a_act_ev"), al.sem("a_dve_ev")
        kf_ok, kh_ok = al.sem("a_kf"), al.sem("a_kh")
        ckv_ps, done = al.sem("a_ckv_ps"), al.sem("a_done")
        tiles = [(0, P), (P, QL - P), (QL, P), (QL + P, P)]

        with nc.Block() as block:

            @block.sync
            def _(sp):
                x = io["x"].rearrange("b (j p) d -> p (b j) d", p=P)
                for n in range(2):
                    sp.dma_start(keep.x[:, 4 * n:4 * n + 4, :], x[:, 4 * n:4 * n + 4, :]).then_inc(x_in[n], 16)
                rope = io["w_k_rope"].rearrange("(k p) n -> p k n", p=P)
                kv = io["w_kv_down"].rearrange("(k p) n -> p k n", p=P)
                sp.dma_start(wd_f[:, :, 0:QL], io["w_q_down"].rearrange("(k p) n -> p k n", p=P)).then_inc(wd_in, 16)
                for n in range(2):
                    at = QL + n * P
                    sp.dma_start(wd_f[:, :, at:at + 64], kv).then_inc(wd_in, 16)
                sp.dma_start(wd_f[:, :, QL + 64:QL + 128], rope).then_inc(wd_in, 16)
                sp.dma_start(wd_f[:, :, QL + 192:QL + 224], rope[:, :, 32:64]).then_inc(wd_in, 16)
                sp.dma_start(wd_f[:, :, QL + 224:QL + 256], rope[:, :, 0:32]).then_inc(wd_in, 16)
                sp.dma_start(keep.cos[:], io["cos"]).then_inc(wd_in, 16)
                sp.dma_start(keep.sin[:], io["sin"]).then_inc(wd_in, 16)

            @block.gpsimd
            def _(pool):
                pool.memset(keep.ident[:], 0.0).then_inc(const_ok, 1)
                pool.memset(keep.ident_b[:], 0.0).then_inc(const_ok, 1)
                pool.memset(keep.mask[:], 0.0).then_inc(const_ok, 1)
                pool.memset(keep.mask_t[:], 0.0).then_inc(const_ok, 1)
                pool.wait_ge(const_ok, 4)
                for m in (keep.ident, keep.ident_b):
                    pool.affine_select(out=m[:], in_=m[:], compare_op=ALU.not_equal, fill=1.0, base=0,
                                       pattern=[[-1, P]], channel_multiplier=1).then_inc(const_ok, 1)
                pool.affine_select(out=keep.mask[:], in_=keep.mask[:], compare_op=ALU.is_ge, fill=NEG, base=0,
                                   pattern=[[-1, P]], channel_multiplier=1).then_inc(const_ok, 1)
                pool.affine_select(out=keep.mask_t[:], in_=keep.mask_t[:], compare_op=ALU.is_ge, fill=NEG, base=0,
                                   pattern=[[1, P]], channel_multiplier=-1).then_inc(const_ok, 1)

            @block.tensor
            def _(pe):
                pe.wait_ge(const_ok, 8)
                for j in range(ST):
                    pe.wait_ge(x_in[j // 4], 16)
                    if j >= 2:
                        pe.wait_ge(xTl_ok, j - 1)
                    for k in range(DK):
                        last = pe.transpose(tr[j % 2][:, k, :], keep.x[:, j, k * P:(k + 1) * P], keep.ident[:])
                    last.then_inc(xT_ps, 1)
                pe.wait_ge(wdl_ok, 1)
                for n in range(2):
                    pe.wait_ge(xTl_ok, 4 * n + 4)
                    half = slice(n * BANK, (n + 1) * BANK)
                    for t, (c, m) in enumerate(tiles):
                        if n == 1:
                            pe.wait_ge(act_ev, t + 1)
                            pe.wait_ge(dve_ev, t + 1)
                        terms = []
                        for k in range(DK):
                            h, l = wd_h[:, k, c:c + m], wd_l[:, k, c:c + m]
                            terms += [(h, xT_h[:, k, half]), (h, xT_l[:, k, half]), (l, xT_h[:, k, half])]
                        three(pe, pj[t][0:m, :], terms).then_inc(proj_ps, 1)
                kv = slice(QL, QL + KVL)
                for j in range(ST):
                    cols = slice(j * P, (j + 1) * P)
                    terms = []
                    for k in range(DK):
                        h, l = wd_h[:, k, kv], wd_l[:, k, kv]
                        terms += [(xT_h[:, k, cols], h), (xT_l[:, k, cols], h), (xT_h[:, k, cols], l)]
                    last = three(pe, pc[:, j, :], terms)
                last.then_inc(ckv_ps, 1)

            @block.scalar
            def _(act):
                for j in range(ST):
                    act.wait_ge(xT_ps, j + 1)
                    act.copy(xT_h[:, :, j * P:(j + 1) * P], tr[j % 2][:]).then_inc(xTh_ok, 1)
                for n in range(2):
                    half = slice(n * BANK, (n + 1) * BANK)
                    act.wait_ge(proj_ps, 4 * n + 1)
                    act.copy(keep.cqa_h[:, half], pj[0][:]).then_inc(act_ev, 1)
                    act.wait_ge(proj_ps, 4 * n + 2)
                    act.copy(keep.cqb_hh[64:128, half], pj[1][0:64, :]).then_inc(done, 1)
                    act.copy(keep.cqb_hh[0:64, half], pj[1][0:64, :]).then_inc(act_ev, 1)
                    act.wait_ge(proj_ps, 4 * n + 3)
                    act.copy(k_f[0:64, half], pj[2][0:64, :]).then_inc(act_ev, 1)
                    act.wait_ge(act_ev, 4 * n + 3)
                    act.wait_ge(kf_ok, n + 1)
                    act.copy(keep.k_h[:, half], k_f[:, half]).then_inc(act_ev, 1)
                act.wait_ge(ckv_ps, 1)
                act.copy(keep.ckv[:], pc[:]).then_inc(done, 1)

            @block.vector
            def _(dve):
                dve.wait_ge(wd_in, 128)
                dve.tensor_copy(wd_h[:], wd_f[:]).then_inc(wdh_ok, 1)
                dve.wait_ge(wdh_ok, 1)
                dve.tensor_tensor(wd_l[:], wd_f[:], wd_h[:].bitcast(F32), ALU.subtract).then_inc(wdl_ok, 1)
                for j in range(ST):
                    dve.wait_ge(xTh_ok, j + 1)
                    dve.tensor_tensor(xT_l[:, :, j * P:(j + 1) * P], tr[j % 2][:],
                                      xT_h[:, :, j * P:(j + 1) * P].bitcast(F32), ALU.subtract).then_inc(xTl_ok, 1)
                rope = slice(64, 128)
                for n in range(2):
                    half = slice(n * BANK, (n + 1) * BANK)
                    dve.wait_ge(act_ev, 4 * n + 1)
                    dve.tensor_tensor(keep.cqa_l[:, half], pj[0][:], keep.cqa_h[:, half].bitcast(F32),
                                      ALU.subtract).then_inc(dve_ev, 1)
                    dve.wait_ge(act_ev, 4 * n + 2)
                    dve.tensor_tensor(keep.cqb_l[0:64, half], pj[1][0:64, :], keep.cqb_hh[0:64, half].bitcast(F32),
                                      ALU.subtract).then_inc(dve_ev, 1)
                    dve.wait_ge(proj_ps, 4 * n + 3)
                    dve.tensor_tensor(k_f[rope, half], pj[2][rope, :], keep.cos[rope, half], ALU.mult).then_inc(dve_ev, 1)
                    dve.wait_ge(proj_ps, 4 * n + 4)
                    dve.tensor_tensor(k_sw[rope, half], pj[3][rope, :], keep.sin[rope, half], ALU.mult).then_inc(dve_ev, 1)
                    dve.wait_ge(dve_ev, 4 * n + 4)
                    dve.tensor_tensor(k_f[rope, half], k_f[rope, half], k_sw[rope, half], ALU.add).then_inc(kf_ok, 1)
                    dve.wait_ge(act_ev, 4 * n + 4)
                    dve.tensor_tensor(keep.k_l[:, half], k_f[:, half], keep.k_h[:, half].bitcast(F32),
                                      ALU.subtract).then_inc(done, 1)


def stage_mla(nc, io, keep):
    with ExitStack() as ctx:
        al = Alloc(nc, ctx)
        nope_a, nope_b = al.sb("nope_a", [P, 2 * DN]), al.sb("nope_b", [64, 2 * DN])
        wuk, wuv = al.sb("wuk", [P, 2, KVL]), al.sb("wuv", [P, 2, KVL])
        wout = al.sb("wout", [P, 2, D])
        nope_t = al.sb("nope_t", [P, 2, QL])
        wa_f, wb_f = al.sb("wa_f", [P, 3 * P]), al.sb("wb_f", [64, 3 * P])
        wa_h, wa_l = al.sb("wa_h", [P, 3 * P], F32R), al.sb("wa_l", [P, 3 * P], F32R)
        wb_hl = al.sb("wb_hl", [P, 3 * P], F32R)
        q_f = [al.sb(f"q_f{e}", [P, S]) for e in range(2)]
        q_sw = [al.sb(f"q_sw{e}", [P, S]) for e in range(2)]
        q_h = [al.sb(f"q_h{e}", [P, S], F32R) for e in range(2)]
        q_l = [al.sb(f"q_l{e}", [P, S], F32R) for e in range(2)]
        probs = [al.sb(f"probs{i}", [P, S]) for i in range(4)]
        stat = al.sb("stat", [P, 3, 4])
        pt = [al.sb(f"pt{g}", [P, 2, 4 * (g + 1), BANK]) for g in range(2)]
        ol_h, ol_l = al.sb("ol_h", [P, S], F32R), al.sb("ol_l", [P, S], F32R)
        wo_h, wo_l = al.sb("wo_h", [P, D], F32R), al.sb("wo_l", [P, D], F32R)

        sc = [al.ps(f"sc{i}", [P, S]) for i in range(2)]
        tb = [al.ps(f"tb{i}", [P, 4, P]) for i in range(2)]
        mb = [al.ps(f"mb{i}", [P, BANK]) for i in range(2)]

        names = ("wq_in wo_in scores negmax exp recip pnorm pt_ps pt_ev pv olat_h wt_ps wlat_ps wlat_ev "
                 "wsplit qp qlat qadd qh ql wo_ps wo_h op").split()
        (wq_in, wo_in, scores, negmax, exped, recip, pnorm, pt_ps, pt_ev, pv, olat_h, wt_ps, wlat_ps, wlat_ev,
         wsplit, qp, qlat, qadd, qh_ok, ql_ok, wo_ps, woh_ok, op) = (al.sem("b_" + n) for n in names)
        mb_read = [al.sem(f"b_mb_read{i}") for i in range(2)]

        NS = 2 * ST
        groups = []
        for n in range(NS):
            for j0 in range(0, n // 2 + 1, 4):
                groups.append((n, j0, min(4, n // 2 + 1 - j0)))
        NG = len(groups)
        NWQ, NWO = 9, 2
        QUERIES = [(2, 0), (2, 1), (0, 0), (0, 1), (1, 0), (1, 1)]
        WORK = {1: [("out", 0)], 2: [("out", 1), ("up", 0)], 3: [("values", 1)], 4: [("out", 2), ("out", 3)],
                5: [("latent", 0), ("out", 4)], 6: [("out", 5)], 7: [("out", 6)], 8: [("out", 7)],
                9: [("out_weights", 0), ("query", 0)], 10: [("query", 1)], 11: [("query", 2), ("query", 3)],
                12: [("query", 4)], 13: [("query", 5)], 15: [("values", 0)]}

        OUT_BANK = (0, 1, 0, 1, 1, 0, 1, 0)

        def bank(kind, k):
            return {"up": 0, "latent": 0, "out_weights": 1, "out": OUT_BANK[k]}.get(kind, k % 2)

        def pair_of(kind, k):
            if kind in ("up", "latent", "query"):
                return 1
            return -1 if kind == "out" or (kind, k) == ("values", 1) else 0

        def works(rnd, n=None):
            kept = (1,) if rnd == -1 else (0, 1) if rnd == 0 else (-1, 0) if rnd == PAIRS - 1 else (-1,) if rnd == PAIRS else (-1, 0, 1)
            return [w for m in range(NS) for w in WORK.get(m, ()) if pair_of(*w) in kept and n in (None, m)]

        def reads(rnd, kind, k):
            same = lambda r: [w for w in works(r) if bank(*w) == bank(kind, k)]
            if not isinstance(rnd, int):
                return rnd * len(same(1)) + (reads(1, kind, k) - len(same(1)))
            return sum(len(same(r)) for r in range(-1, rnd)) + same(rnd).index((kind, k)) + 1

        def shape_of(rnd):
            return rnd if isinstance(rnd, int) else 1

        def load_q(sp, r):
            cols = lambda w, c0, n, r0, r1: io[w][r0:r1, bass.ds(r * c0, n)]
            sp.dma_start(nope_a[:], cols("w_q_up_nope", 2 * DN, 2 * DN, 0, P)).then_inc(wq_in, 16)
            sp.dma_start(nope_b[:], cols("w_q_up_nope", 2 * DN, 2 * DN, P, QL)).then_inc(wq_in, 16)
            for w, r0, r1 in ((wa_f, 0, P), (wb_f, P, QL)):
                src = cols("w_q_up_rope", 2 * DR, 2 * DR, r0, r1)
                heads = w[:, 0:2 * P].rearrange("p (e c) -> p e c", e=2)
                swapped = w[:, 2 * P:3 * P].rearrange("p (e t f) -> p e t f", e=2, t=2)
                sp.dma_start(heads[:, :, KVL:P], src.rearrange("p (e c) -> p e c", e=2)).then_inc(wq_in, 16)
                halves = src.rearrange("p (e t f) -> p e t f", e=2, t=2)
                for t in range(2):
                    sp.dma_start(swapped[:, :, t, :], halves[:, :, 1 - t, :]).then_inc(wq_in, 16)

        def load_o(sp, r):
            rows = lambda w: io[w][bass.ds(r * 2 * DV, 2 * DV), :].rearrange("(e d) n -> d e n", e=2)
            sp.dma_start(wuv[:], rows("w_uv")).then_inc(wo_in, 16)
            sp.dma_start(wout[:], rows("w_out")).then_inc(wo_in, 16)

        def load_k(sp, r):
            sp.dma_start(wuk[:], io["w_uk"][bass.ds(r * 2 * DN, 2 * DN), :].rearrange("(e d) n -> d e n", e=2))\
                .then_inc(wq_in, 16)

        with nc.Block() as block:

            @block.sync
            def _(sp):
                load_q(sp, 0)
                load_k(sp, 0)
                load_o(sp, 0)

                def pair(p, more):
                    if more:
                        sp.wait_ge(wt_ps, p + 1)
                        sp.wait_ge(wlat_ps, p + 1)
                        sp.wait_ge(wsplit, 4 * p + 4)
                        load_q(sp, p + 1)
                        load_k(sp, p + 1)
                        sp.wait_ge(wo_ps, p + 1)
                        load_o(sp, p + 1)

                pair(0, True)
                with sp.Fori(1, PAIRS - 1) as p:
                    pair(p, True)

            @block.tensor
            def _(pe):
                def bank_free(rnd, kind, k):
                    from_one(pe, mb_read[bank(kind, k)], reads(rnd, kind, k) - 1)

                def up(rnd, r, k):
                    pe.wait_ge(wq_in, (r + 1) * (16 * NWQ))
                    bank_free(rnd, "up", k)
                    wt = mb[0][:, 0:2 * QL].rearrange("p (e c) -> p e c", e=2)
                    for e in range(2):
                        pe.transpose(wt[:, e, 0:P], nope_a[:, e * DN:(e + 1) * DN], keep.ident[:])
                        last = pe.transpose(wt[:, e, P:QL], nope_b[:, e * DN:(e + 1) * DN], keep.ident[0:64, 0:64])
                    last.then_inc(wt_ps, 1)

                def latent(rnd, r, k):
                    bank_free(rnd, "latent", k)
                    for e in range(2):
                        pe.matmul(mb[0][:, e * 64:e * 64 + 64], nope_t[:, e, 0:P], wuk[:, e, :], start=True, stop=True)
                        last = pe.matmul(mb[0][0:64, P + e * 64:P + e * 64 + 64], nope_t[:, e, P:QL], wuk[:, e, :],
                                         start=True, stop=True)
                    last.then_inc(wlat_ps, 1)

                def query(rnd, r, k):
                    t, h = QUERIES[k]
                    if k == 0:
                        pe.wait_ge(wsplit, 4 * r + 4)
                    bank_free(rnd, "query", k)
                    cols, half = slice(t * P, (t + 1) * P), slice(h * BANK, (h + 1) * BANK)
                    three(pe, mb[k % 2][:], [
                        (wa_h[:, cols], keep.cqa_h[:, half]), (wa_h[:, cols], keep.cqa_l[:, half]),
                        (wa_l[:, cols], keep.cqa_h[:, half]), (wb_hl[:, cols], keep.cqb_hh[:, half]),
                        (wb_hl[0:64, cols], keep.cqb_l[0:64, half])]).then_inc(qp, 1)

                def score(p, n):
                    i, e = n // 2, n % 2
                    from_one(pe, exped, NS * p + n - 1)
                    if n < 2:
                        pe.wait_ge(qh_ok, 2 * p + e + 1)
                        pe.wait_ge(ql_ok, 2 * p + e + 1)
                    rows = slice(i * P, (i + 1) * P)
                    width = (i + 1) * P
                    for c0 in range(0, width, BANK):
                        w = min(BANK, width - c0)
                        keys = slice(c0, c0 + w)
                        diagonal = c0 + w == width
                        last = three(pe, sc[n % 2][:, keys], [
                            (q_h[e][:, rows], keep.k_h[:, keys]), (q_h[e][:, rows], keep.k_l[:, keys]),
                            (q_l[e][:, rows], keep.k_h[:, keys])], stop=not diagonal)
                        if diagonal:
                            last = pe.matmul(sc[n % 2][:, width - P:width], keep.ident_b[:], keep.mask[:],
                                             start=False, stop=True)
                    last.then_inc(scores, 1)

                def turn(p, n):
                    pe.wait_ge(pnorm, NS * p + n + 1)
                    for g, (m, j0, nb) in enumerate(groups):
                        if m == n:
                            from_one(pe, pt_ev, NG * p + g - 1)
                            for b in range(nb):
                                last = pe.transpose(tb[g % 2][:, b, :], probs[n % 4][:, (j0 + b) * P:(j0 + b + 1) * P],
                                                    keep.ident[:])
                            last.then_inc(pt_ps, 1)

                def values(rnd, p, g):
                    pe.wait_ge(pt_ev, NG * p + (8 if g == 0 else NG))
                    bank_free(rnd, "values", g)
                    for j in range(4 * (g + 1)):
                        off = max(0, j - 4 * g) * P
                        for e in range(2):
                            last = pe.matmul(mb[g][64 * e:64 * e + 64, off:BANK], keep.ckv[:, j, :],
                                             pt[g][:, e, j, off:BANK], start=(j == 0), stop=(j == 4 * g + 3))
                    last.then_inc(pv, 1)

                def out_weights(rnd, p, k):
                    pe.wait_ge(wo_in, (p + 1) * (16 * NWO))
                    bank_free(rnd, "out_weights", k)
                    for e in range(2):
                        last = pe.matmul(mb[1][64 * e:64 * e + 64, :], wuv[:, e, :], wout[:, e, :], start=True, stop=True)
                    last.then_inc(wo_ps, 1)

                def out(rnd, p, j):
                    if j in (0, 4):
                        pe.wait_ge(mb_read[j // 4], reads(rnd - 1 if j == 0 else rnd, "values", j // 4))
                    if j == 0:
                        pe.wait_ge(mb_read[1], reads(rnd - 1, "out_weights", 0))
                    bank_free(rnd, "out", j)
                    rows = slice(j * P, (j + 1) * P)
                    three(pe, mb[OUT_BANK[j]][:], [(ol_h[:, rows], wo_h[:]), (ol_h[:, rows], wo_l[:]),
                                             (ol_l[:, rows], wo_h[:])]).then_inc(op, 1)

                work = {"up": up, "latent": latent, "query": query, "values": values, "out_weights": out_weights, "out": out}

                def steps(rnd):
                    for n in range(NS):
                        score(rnd, n)
                        if n >= 2:
                            turn(rnd, n - 2)
                        elif not (isinstance(rnd, int) and rnd == 0):
                            turn(rnd - 1, NS - 2 + n)
                        for kind, k in works(shape_of(rnd), n):
                            work[kind](rnd, rnd + pair_of(kind, k), k)

                for kind, k in works(-1):
                    work[kind](-1, 0, k)
                steps(0)
                with pe.Fori(1, PAIRS - 1) as rnd:
                    steps(rnd)
                steps(PAIRS - 1)
                turn(PAIRS - 1, NS - 2)
                turn(PAIRS - 1, NS - 1)
                for kind, k in works(PAIRS):
                    work[kind](PAIRS, PAIRS - 1, k)

            @block.scalar
            def _(act):
                def up(rnd, r, k):
                    act.wait_ge(wt_ps, r + 1)
                    act.copy(nope_t[:].rearrange("p e c -> p (e c)"), mb[0][:, 0:2 * QL]).then_inc(mb_read[0], 1)

                def latent(rnd, r, k):
                    act.wait_ge(wlat_ps, r + 1)
                    for w, m, c, ok in ((wa_f, P, 0, wlat_ev), (wb_f, 64, P, mb_read[0])):
                        act.copy(w[:, 0:2 * P].rearrange("p (e c) -> p e c", e=2)[:, :, 0:KVL],
                                 mb[0][0:m, c:c + P].rearrange("p (e c) -> p e c", e=2)).then_inc(ok, 1)
                    act.wait_ge(wlat_ev, r + 1)
                    act.wait_ge(mb_read[0], reads(rnd, "latent", 0))
                    act.wait_ge(wq_in, (r + 1) * (16 * NWQ))
                    from_one(act, qp, 6 * r)
                    act.copy(wa_h[:], wa_f[:]).then_inc(wsplit, 1)
                    act.copy(wb_hl[0:64, :], wb_f[:]).then_inc(wsplit, 1)

                def query(rnd, r, k):
                    e, half = QUERIES[k]
                    if e < 2:
                        act.wait_ge(qp, 6 * r + k + 1)
                        act.mul(q_f[e][0:64, half * BANK:(half + 1) * BANK], mb[k % 2][0:64, :], SCALE0).then_inc(qlat, 1)

                def values(rnd, p, g):
                    act.wait_ge(pv, 2 * p + g + 1)
                    from_one(act, op, 8 * p)
                    act.copy(ol_h[:, g * BANK:(g + 1) * BANK], mb[g][:]).then_inc(olat_h, 1)

                def out_weights(rnd, p, k):
                    act.wait_ge(wo_ps, p + 1)
                    act.copy(wo_h[:], mb[1][:]).then_inc(woh_ok, 1)

                def split_query(r, e):
                    act.wait_ge(qlat, 4 * r + 2 * e + 2)
                    act.wait_ge(qadd, 4 * r + 2 * e + 2)
                    act.copy(q_h[e][:], q_f[e][:]).then_inc(qh_ok, 1)

                def exp(p, n):
                    act.wait_ge(negmax, NS * p + n + 1)
                    w, s = (n // 2 + 1) * P, n % 4
                    act.activation(probs[s][:, 0:w], sc[n % 2][:, 0:w], ACT.Exp, bias=stat[:, 0, s:s + 1],
                                   accum_out=stat[:, 1, s:s + 1]).then_inc(exped, 1)

                def turned(p, n):
                    i, e = n // 2, n % 2
                    for g, (m, j0, nb) in enumerate(groups):
                        if m == n:
                            act.wait_ge(pt_ps, NG * p + g + 1)
                            act.copy(pt[i // 4][:, e, j0:j0 + nb, (i % 4) * P:(i % 4 + 1) * P],
                                     tb[g % 2][:, 0:nb, :]).then_inc(pt_ev, 1)

                work = {"up": up, "latent": latent, "query": query, "values": values, "out_weights": out_weights}

                def steps(rnd):
                    more = not (isinstance(rnd, int) and rnd == PAIRS - 1)
                    for n in range(NS):
                        if n >= NS - 2 and more:
                            act.wait_ge(scores, NS * rnd + n + 1)
                            split_query(rnd + 1, n % 2)
                        if n >= 2:
                            turned(rnd, n - 2)
                        elif not (isinstance(rnd, int) and rnd == 0):
                            turned(rnd - 1, NS - 2 + n)
                        exp(rnd, n)
                        for kind, k in works(shape_of(rnd), n):
                            if kind in work:
                                work[kind](rnd, rnd + pair_of(kind, k), k)

                for kind, k in works(-1):
                    work[kind](-1, 0, k)
                for e in range(2):
                    split_query(0, e)
                steps(0)
                with act.Fori(1, PAIRS - 1) as rnd:
                    steps(rnd)
                steps(PAIRS - 1)
                turned(PAIRS - 1, NS - 2)
                turned(PAIRS - 1, NS - 1)
                for kind, k in works(PAIRS):
                    if kind in work:
                        work[kind](PAIRS, PAIRS - 1, k)

            @block.vector
            def _(dve):
                def query(rnd, r, k):
                    t, h = QUERIES[k]
                    rope, half = slice(64, 128), slice(h * BANK, (h + 1) * BANK)
                    dve.wait_ge(qp, 6 * r + k + 1)
                    if t < 2:
                        dve.wait_ge(qlat, 4 * r + k - 1)
                        last = dve.scalar_tensor_tensor(out=q_f[t][rope, half], in0=mb[k % 2][rope, :], scalar=SCALE0,
                                                        in1=keep.cos[rope, half], op0=ALU.mult, op1=ALU.mult)
                    else:
                        for e in range(2):
                            rows = slice(64 * e, 64 * e + 64)
                            last = dve.scalar_tensor_tensor(out=q_sw[e][rope, half], in0=mb[k % 2][rows, :], scalar=SCALE0,
                                                            in1=keep.sin[rows, half], op0=ALU.mult, op1=ALU.mult)
                    last.then_inc(mb_read[k % 2], 1)

                def values(rnd, p, g):
                    dve.wait_ge(olat_h, 2 * p + g + 1)
                    half = slice(g * BANK, (g + 1) * BANK)
                    dve.tensor_tensor(ol_l[:, half], mb[g][:], ol_h[:, half].bitcast(F32), ALU.subtract).then_inc(mb_read[g], 1)

                def out_weights(rnd, p, k):
                    dve.wait_ge(woh_ok, p + 1)
                    dve.tensor_tensor(wo_l[:], mb[1][:], wo_h[:].bitcast(F32), ALU.subtract).then_inc(mb_read[1], 1)

                def out(rnd, p, j):
                    dve.wait_ge(op, 8 * p + j + 1)
                    dve.tensor_tensor(keep.x[:, j, :], mb[OUT_BANK[j]][:], keep.x[:, j, :],
                                      ALU.add).then_inc(mb_read[OUT_BANK[j]], 1)

                def split_query(r, e):
                    dve.wait_ge(qh_ok, 2 * r + e + 1)
                    dve.tensor_tensor(q_l[e][:], q_f[e][:], q_h[e][:].bitcast(F32), ALU.subtract).then_inc(ql_ok, 1)

                def row_max(p, n):
                    dve.wait_ge(scores, NS * p + n + 1)
                    dve.tensor_reduce(stat[:, 0, n % 4:n % 4 + 1], sc[n % 2][:, 0:(n // 2 + 1) * P], AX.X, ALU.max,
                                      negate=True).then_inc(negmax, 1)

                def normalise(p, n):
                    s, w = n % 4, (n // 2 + 1) * P
                    dve.wait_ge(exped, NS * p + n + 1)
                    dve.reciprocal(stat[:, 2, s:s + 1], stat[:, 1, s:s + 1]).then_inc(recip, 1)
                    dve.wait_ge(recip, NS * p + n + 1)
                    dve.tensor_scalar(probs[s][:, 0:w], probs[s][:, 0:w], stat[:, 2, s:s + 1], None,
                                      ALU.mult).then_inc(pnorm, 1)

                work = {"query": query, "values": values, "out_weights": out_weights, "out": out}

                def steps(rnd):
                    more = not (isinstance(rnd, int) and rnd == PAIRS - 1)
                    for n in range(NS):
                        if n == NS - 1 and more:
                            split_query(rnd + 1, 0)
                        row_max(rnd, n)
                        if n >= 1:
                            normalise(rnd, n - 1)
                        if n == NS - 1:
                            if more:
                                split_query(rnd + 1, 1)
                            normalise(rnd, n)
                        for kind, k in works(shape_of(rnd), n):
                            if kind in work:
                                work[kind](rnd, rnd + pair_of(kind, k), k)

                for kind, k in works(-1):
                    if kind in work:
                        work[kind](-1, 0, k)
                for e in range(2):
                    split_query(0, e)
                steps(0)
                with dve.Fori(1, PAIRS - 1) as rnd:
                    steps(rnd)
                steps(PAIRS - 1)
                for kind, k in works(PAIRS):
                    if kind in work:
                        work[kind](PAIRS, PAIRS - 1, k)

            @block.gpsimd
            def _(pool):
                def lower_weights(r):
                    pool.wait_ge(wsplit, 4 * r + 2)
                    pool.tensor_tensor(wa_l[:], wa_f[:], wa_h[:].bitcast(F32), ALU.subtract).then_inc(wsplit, 1)
                    pool.wait_ge(wsplit, 4 * r + 3)
                    pool.tensor_tensor(wb_hl[64:128, :], wb_f[:], wb_hl[0:64, :].bitcast(F32),
                                       ALU.subtract).then_inc(wsplit, 1)

                def queries(rnd, r):
                    for k in range(2, 6):
                        e, h = QUERIES[k]
                        half = slice(h * BANK, (h + 1) * BANK)
                        pool.wait_ge(mb_read[k % 2], reads(rnd, "query", k))
                        pool.tensor_tensor(q_f[e][64:128, half], q_f[e][64:128, half], q_sw[e][64:128, half],
                                           ALU.add).then_inc(qadd, 1)

                lower_weights(0)
                queries(-1, 0)
                lower_weights(1)
                queries(0, 1)
                with pool.Fori(1, PAIRS - 1) as rnd:
                    lower_weights(rnd + 1)
                    queries(rnd, rnd + 1)




class Norm:

    def __init__(self, al, name, n):
        self.n = n
        self.st, self.mv = al.sb(name + "_st", [P, n, 6]), al.sb(name + "_mv", [P, n, 2])
        self.sd, self.rs = al.sb(name + "_sd", [P, n]), al.sb(name + "_rs", [P, n])
        self.st_ok, self.mv_ok, self.ve_ok, self.sd_ok, self.rs_ok, self.x_ok = (
            al.sem(f"{name}_{s}") for s in ("st", "mv", "ve", "sd", "rs", "x"))

    def stats(self, dve, t, x):
        dve.bn_stats(self.st[:, t, :], x).then_inc(self.st_ok, 1)
        dve.wait_ge(self.st_ok, t + 1)
        dve.bn_aggr(self.mv[:, t, :], self.st[:, t, :]).then_inc(self.mv_ok, 1)

    def variance(self, dve, eps=1e-5):
        dve.wait_ge(self.mv_ok, self.n)
        dve.tensor_scalar(self.sd[:], self.mv[:, :, 1], eps, None, ALU.add).then_inc(self.ve_ok, 1)

    def root(self, act):
        act.wait_ge(self.ve_ok, 1)
        act.activation(self.sd[:], self.sd[:], ACT.Sqrt).then_inc(self.sd_ok, 1)

    def inverse(self, dve):
        dve.wait_ge(self.sd_ok, 1)
        dve.reciprocal(self.rs[:], self.sd[:]).then_inc(self.rs_ok, 1)
        dve.wait_ge(self.rs_ok, 1)

    def apply(self, dve, t, x):
        dve.tensor_scalar(x, x, self.mv[:, t, 0:1], self.rs[:, t:t + 1], ALU.subtract, ALU.mult).then_inc(self.x_ok, 1)


RANKS = (8, 16, 32, 64)
MR = RANKS[-1]
NR = len(RANKS)
CLIP = 8.0
HD1 = 16
SCALE1 = HD1 ** -0.5


def stage_route(nc, io, keep):
    with ExitStack() as ctx:
        al = Alloc(nc, ctx)
        w_f, ag_f, b_f = al.sb("c_w", [P, DK, D]), al.sb("c_ag", [MR + NR, D]), al.sb("c_b", [P, DK, MR])
        bias, gate_b = al.sb("c_bias", [P, D]), al.sb("c_gate_b", [P, NR])
        wT_h, wT_l = al.sb("wT_h", [P, DK, D], F32R), al.sb("wT_l", [P, DK, D], F32R)
        agT_h, agT_l = al.sb("agT_h", [P, DK, MR + NR], F32R), al.sb("agT_l", [P, DK, MR + NR], F32R)
        bT_h, bT_l = al.sb("bT_h", [MR, DK, P], F32R), al.sb("bT_l", [MR, DK, P], F32R)
        xT_h, xT_l = al.sb("x1T_h", [P, DK, S], F32R), al.sb("x1T_l", [P, DK, S], F32R)
        ag = al.sb("ag", [P, ST, MR + NR])
        top, less, gate = al.sb("top", [P, ST]), al.sb("less", [P, ST, NR]), al.sb("gate", [P, ST, NR])
        loT_h, loT_l = al.sb("loT_h", [MR, ST, P], F32R), al.sb("loT_l", [MR, ST, P], F32R)
        tr = [al.ps(f"c_tr{i}", [P, DK, P]) for i in range(2)]
        pag = [al.ps(f"c_ag{i}", [P, 4, MR + NR]) for i in range(2)]
        po = [al.ps(f"c_po{i}", [P, D]) for i in range(4)]
        n1, n2 = Norm(al, "n1", ST), Norm(al, "n2", ST)
        names = "w_in b_in tr_ps tr_h tr_l ag_ps ag_ev route biased out_ps out_ev"
        w_in, b_in, tr_ps, tr_h, tr_l, ag_ps, ag_ev, route, biased, out_ps, out_ev = (
            al.sem("c_" + n) for n in names.split())

        jobs = [([w_f[:, t, k * P:(k + 1) * P] for k in range(DK)], (wT_h, wT_l), slice(t * P, (t + 1) * P)) for t in range(DK)]
        jobs += [([ag_f[:, k * P:(k + 1) * P] for k in range(DK)], (agT_h, agT_l), slice(0, MR + NR))]
        jobs += [([b_f[:, t, :] for t in range(DK)], (bT_h, bT_l), slice(0, P))]
        JX = len(jobs)
        jobs += [([keep.x[:, j, k * P:(k + 1) * P] for k in range(DK)], (xT_h, xT_l), slice(j * P, (j + 1) * P)) for j in range(ST)]
        JL = len(jobs)
        jobs += [([ag[:, 4 * n + t, 0:MR] for t in range(4)], (loT_h[:, 4 * n:4 * n + 4], loT_l[:, 4 * n:4 * n + 4]),
                  slice(0, P)) for n in range(2)]

        def shape(n):
            src, dst, cols = jobs[n]
            return src[0].shape[0], src[0].shape[1]

        with nc.Block() as block:

            @block.sync
            def _(sp):
                sp.dma_start(w_f[:], io["L0_ffn_W"].rearrange("(t p) n -> p t n", p=P)).then_inc(w_in, 16)
                sp.dma_start(ag_f[0:MR, :], io["L0_ffn_A"]).then_inc(w_in, 16)
                sp.dma_start(ag_f[MR:MR + NR, :], io["L0_ffn_gate_w"]).then_inc(w_in, 16)
                sp.dma_start(b_f[:], io["L0_ffn_B"].rearrange("(t p) n -> p t n", p=P)).then_inc(w_in, 16)
                sp.dma_start(bias[:], io["L0_ffn_b"].partition_broadcast(P)).then_inc(b_in, 16)
                sp.dma_start(gate_b[:], io["L0_ffn_gate_b"].partition_broadcast(P)).then_inc(b_in, 16)
                sp.dma_start(keep.wqkv[:], io["L1_attn_w_qkv"].rearrange("(t p) n -> p t n", p=P)).then_inc(keep.wqkv_in, 16)
                for n, name in enumerate(("q_ln_w", "q_ln_b", "k_ln_w", "k_ln_b")):
                    sp.dma_start(keep.qk_ln[:, n, :], io["L1_attn_" + name].partition_broadcast(P)).then_inc(keep.ln_in, 16)

            @block.tensor
            def _(pe):
                def turn(n):
                    rows, cols = shape(n)
                    if n >= 2:
                        pe.wait_ge(tr_l, n - 1)
                    for b, src in enumerate(jobs[n][0]):
                        last = pe.transpose(tr[n % 2][0:cols, b, 0:rows], src, keep.ident[0:rows, 0:rows])
                    last.then_inc(tr_ps, 1)

                pe.wait_ge(w_in, 64)
                for n in range(JX):
                    turn(n)
                for j in range(ST):
                    pe.wait_ge(n1.x_ok, j + 1)
                    turn(JX + j)
                for n in range(2):
                    pe.wait_ge(tr_l, JX + 4 * n + 4)
                    for t in range(4):
                        cols = slice((4 * n + t) * P, (4 * n + t + 1) * P)
                        terms = []
                        for k in range(DK):
                            terms += [(xT_h[:, k, cols], agT_h[:, k, :]), (xT_l[:, k, cols], agT_h[:, k, :]),
                                      (xT_h[:, k, cols], agT_l[:, k, :])]
                        last = three(pe, pag[n][:, t, :], terms)
                    last.then_inc(ag_ps, 1)

                def ffn(j, start):
                    cols = slice(j * P, (j + 1) * P)
                    if start:
                        if j >= 4:
                            pe.wait_ge(out_ev, j - 3)
                        terms = []
                        for k in range(DK):
                            terms += [(xT_h[:, k, cols], wT_h[:, k, :]), (xT_l[:, k, cols], wT_h[:, k, :]),
                                      (xT_h[:, k, cols], wT_l[:, k, :])]
                        three(pe, po[j % 4][:], terms, stop=False)
                    else:
                        bh, bl = (b[:].rearrange("r t n -> r (t n)") for b in (bT_h, bT_l))
                        three(pe, po[j % 4][:], [(loT_h[:, j, :], bh), (loT_l[:, j, :], bh), (loT_h[:, j, :], bl)],
                              start=False).then_inc(out_ps, 1)

                for j in range(4):
                    ffn(j, True)
                pe.wait_ge(route, 2 + NR - 1 + 3)
                for n in range(2):
                    turn(JL + n)
                pe.wait_ge(tr_l, JL + 2)
                for j in range(4):
                    ffn(j, False)
                for j in range(4, ST):
                    ffn(j, True)
                    ffn(j, False)

            @block.scalar
            def _(act):
                def split(n):
                    rows, cols = shape(n)
                    act.wait_ge(tr_ps, n + 1)
                    dst = jobs[n][1][0]
                    act.copy(dst[:, :, jobs[n][2]], tr[n % 2][0:cols, :, 0:rows]).then_inc(tr_h, 1)

                for n in range(JX):
                    split(n)
                n1.root(act)
                for n in range(JX, JL):
                    split(n)
                for n in range(2):
                    act.wait_ge(ag_ps, n + 1)
                    act.copy(ag[:, 4 * n:4 * n + 4, :], pag[n][:]).then_inc(ag_ev, 1)
                for n in range(JL, JL + 2):
                    split(n)
                n2.root(act)

            @block.vector
            def _(dve):
                def split(n):
                    rows, cols = shape(n)
                    dst_h, dst_l = jobs[n][1]
                    dve.wait_ge(tr_h, n + 1)
                    dve.tensor_tensor(dst_l[:, :, jobs[n][2]], tr[n % 2][0:cols, :, 0:rows],
                                      dst_h[:, :, jobs[n][2]].bitcast(F32), ALU.subtract).then_inc(tr_l, 1)

                for j in range(ST):
                    n1.stats(dve, j, keep.x[:, j, :])
                n1.variance(dve)
                for n in range(JX):
                    split(n)
                n1.inverse(dve)
                for j in range(ST):
                    n1.apply(dve, j, keep.x[:, j, :])
                    if j >= 1:
                        split(JX + j - 1)
                split(JL - 1)
                scores = ag[:, :, MR:MR + NR]
                dve.wait_ge(ag_ev, 2)
                dve.wait_ge(b_in, 32)
                for j in range(ST):
                    last = dve.tensor_tensor(ag[:, j, MR:MR + NR], ag[:, j, MR:MR + NR], gate_b[:], ALU.add)
                last.then_inc(route, 1)
                dve.wait_ge(route, 1)
                dve.tensor_reduce(top[:], scores, AX.X, ALU.max).then_inc(route, 1)
                dve.wait_ge(route, 2)
                dve.tensor_tensor(less[:], scores, top[:].unsqueeze(2).to_broadcast([P, ST, NR]), ALU.is_lt).then_inc(route, 1)
                dve.wait_ge(route, 3)
                for r in range(1, NR - 1):
                    dve.tensor_tensor(less[:, :, r], less[:, :, r], less[:, :, r - 1], ALU.mult).then_inc(route, 1)
                    dve.wait_ge(route, 3 + r)
                for r in range(1, NR):
                    c0, c1 = RANKS[r - 1], RANKS[r]
                    dve.tensor_tensor(ag[:, :, c0:c1], ag[:, :, c0:c1],
                                      less[:, :, r - 1:r].to_broadcast([P, ST, c1 - c0]), ALU.mult).then_inc(route, 1)
                for n in range(JL, JL + 2):
                    split(n)
                for j in range(ST):
                    dve.wait_ge(out_ps, j + 1)
                    dve.wait_ge(biased, j + 1)
                    dve.tensor_tensor(keep.x[:, j, :], po[j % 4][:], keep.x[:, j, :], ALU.add).then_inc(out_ev, 1)
                    dve.wait_ge(out_ev, j + 1)
                    n2.stats(dve, j, keep.x[:, j, :])
                n2.variance(dve)
                n2.inverse(dve)
                for j in range(ST):
                    n2.apply(dve, j, keep.x[:, j, :])

            @block.gpsimd
            def _(pool):
                pool.wait_ge(b_in, 32)
                for j in range(ST):
                    pool.wait_ge(tr_ps, JX + j + 1)
                    pool.tensor_tensor(keep.x[:, j, :], keep.x[:, j, :], bias[:], ALU.add).then_inc(biased, 1)


def stage_qkv(nc, io, keep):
    with ExitStack() as ctx:
        al = Alloc(nc, ctx)
        xT_h, xT_l = al.sb("x2T_h", [P, DK, S], F32R), al.sb("x2T_l", [P, DK, S], F32R)
        NW = 3 * D // P
        wT_h, wT_l = al.sb("wqkvT_h", [P, DK, 3 * D], F32R), al.sb("wqkvT_l", [P, DK, 3 * D], F32R)
        tr = [al.ps(f"d_tr{i}", [P, DK, P]) for i in range(2)]
        po = [al.ps(f"d_po{i}", [P, D]) for i in range(4)]
        nq = Norm(al, "nqk", 2 * ST)
        names = "tr_ps tr_h tr_l out_ps clip scaled_q scaled_k done"
        tr_ps, tr_h, tr_l, out_ps, clip, scaled_q, scaled_k, done = (al.sem("d_" + n) for n in names.split())
        jobs = [([keep.x[:, j, k * P:(k + 1) * P] for k in range(DK)], xT_h, xT_l, slice(j * P, (j + 1) * P)) for j in range(ST)]
        jobs += [([keep.wqkv[:, t, k * P:(k + 1) * P] for k in range(DK)], wT_h, wT_l, slice(t * P, (t + 1) * P)) for t in range(NW)]
        order = [(j, c) for c in range(2) for j in range(ST)] + [(j, 2) for j in range(ST)]
        dest = (keep.q, keep.k, keep.v)

        with nc.Block() as block:

            @block.tensor
            def _(pe):
                pe.wait_ge(keep.wqkv_in, 16)
                for n, (src, h, l, cols) in enumerate(jobs):
                    if n >= 2:
                        pe.wait_ge(tr_l, n - 1)
                    for k in range(DK):
                        last = pe.transpose(tr[n % 2][:, k, :], src[k], keep.ident[:])
                    last.then_inc(tr_ps, 1)
                for n, (j, c) in enumerate(order):
                    if j == 0:
                        pe.wait_ge(tr_l, ST + 4 * (c + 1))
                    if n >= 4:
                        pe.wait_ge(clip, n - 3)
                    rows, cols = slice(j * P, (j + 1) * P), slice(c * D, (c + 1) * D)
                    terms = []
                    for k in range(DK):
                        terms += [(xT_h[:, k, rows], wT_h[:, k, cols]), (xT_l[:, k, rows], wT_h[:, k, cols]),
                                  (xT_h[:, k, rows], wT_l[:, k, cols])]
                    three(pe, po[n % 4][:], terms).then_inc(out_ps, 1)

            @block.scalar
            def _(act):
                for n, (src, h, l, cols) in enumerate(jobs):
                    act.wait_ge(tr_ps, n + 1)
                    act.copy(h[:, :, cols], tr[n % 2][:]).then_inc(tr_h, 1)
                nq.root(act)

            @block.vector
            def _(dve):
                for n, (src, h, l, cols) in enumerate(jobs):
                    dve.wait_ge(tr_h, n + 1)
                    dve.tensor_tensor(l[:, :, cols], tr[n % 2][:], h[:, :, cols].bitcast(F32), ALU.subtract).then_inc(tr_l, 1)
                for n, (j, c) in enumerate(order):
                    dve.wait_ge(out_ps, n + 1)
                    dve.tensor_scalar(dest[c][:, j, :], po[n % 4][:], CLIP, -CLIP, ALU.min, ALU.max).then_inc(clip, 1)
                    if c < 2:
                        dve.wait_ge(clip, n + 1)
                        nq.stats(dve, n, dest[c][:, j, :])
                    if n == 2 * ST:
                        nq.variance(dve)
                nq.inverse(dve)
                dve.wait_ge(keep.ln_in, 64)
                for t in list(range(ST, 2 * ST)) + list(range(ST)):
                    nq.apply(dve, t, dest[t // ST][:, t % ST, :])
                for j in range(ST):
                    dve.wait_ge(nq.x_ok, ST + j + 1)
                    dve.scalar_tensor_tensor(out=keep.q[:, j, :], in0=keep.q[:, j, :], scalar=SCALE1,
                                             in1=keep.qk_ln[:, 0, :], op0=ALU.mult, op1=ALU.mult).then_inc(scaled_q, 1)
                for j in range(ST):
                    dve.wait_ge(scaled_q, j + 1)
                    dve.scalar_tensor_tensor(out=keep.q[:, j, :], in0=keep.qk_ln[:, 1, :], scalar=SCALE1,
                                             in1=keep.q[:, j, :], op0=ALU.mult, op1=ALU.add).then_inc(done, 1)

            @block.gpsimd
            def _(pool):
                pool.wait_ge(keep.ln_in, 64)
                for j in range(ST):
                    pool.wait_ge(nq.x_ok, j + 1)
                    pool.tensor_tensor(keep.k[:, j, :], keep.k[:, j, :], keep.qk_ln[:, 2, :], ALU.mult).then_inc(scaled_k, 1)
                for j in range(ST):
                    pool.wait_ge(scaled_k, j + 1)
                    pool.tensor_tensor(keep.k[:, j, :], keep.k[:, j, :], keep.qk_ln[:, 3, :], ALU.add).then_inc(done, 1)


H1 = 32
HG = 4
GROUPS = H1 // HG
EX = 16


def alibi_columns():
    m = np.arange(1, H1 + 1, dtype=np.float32) * np.float32(8.0 / H1)
    slope = np.float32(1.0) / np.power(np.float32(2.0), m)
    bits = slope.view(np.uint32)
    slope_h = ((bits + np.uint32(0x800)) & np.uint32(0xFFFFF000)).view(np.float32)
    slope_l = slope - slope_h
    q, k = (np.zeros((GROUPS, P, ST, HG, EX), np.float32) for _ in range(2))
    pos = (np.arange(ST)[None, :] * P + np.arange(P)[:, None]).astype(np.float32)[None, :, :, None]
    sh, sl = (x.reshape(GROUPS, 1, 1, HG) for x in (slope_h, slope_l))
    k[..., 0] = k[..., 1] = 1.0
    q[..., 2], q[..., 3], q[..., 4], q[..., 5] = sh, sl, -pos, -pos
    k[..., 2], k[..., 3], k[..., 4], k[..., 5] = pos, pos, sh, sl
    return q, k


CHUNKS = [(j, half) for half in range(2) for j in range(4 * (half + 1))]
M_STEPS = HG * ST
E_STEPS = HG * len(CHUNKS)


def m_step(n):
    return n % HG, ST - 1 - n // HG


def chunk_cols(c):
    j, half = CHUNKS[c]
    first = max(j * P, half * BANK)
    return first, (half + 1) * BANK - first


def alibi_order(with_m):
    order, m, m_cols, e_cols = [], 0, -3 * S, 0
    for c in range(len(CHUNKS)):
        for h in range(HG):
            while with_m and m < M_STEPS and m_cols <= e_cols:
                order.append(("m", m))
                m_cols += (m_step(m)[1] + 1) * P
                m += 1
            order.append(("e", HG * c + h))
            e_cols += chunk_cols(c)[1]
        if c >= 1:
            order.append(("pv", c - 1))
    order += [("m", n) for n in range(m, M_STEPS if with_m else 0)]
    return order + [("pv", len(CHUNKS) - 1)]


def stage_alibi(nc, io, keep):
    with ExitStack() as ctx:
        al = Alloc(nc, ctx)
        qx, kx = al.sb("qx", [P, ST, HG, 64], F32R), al.sb("kx", [P, ST, HG, 64], F32R)
        qT = [al.sb(f"qT{u}", [P, 2, S], F32R) for u in range(2)]
        kT = [al.sb(f"kT{u}", [P, HG, S], F32R) for u in range(2)]
        vx = [al.sb(f"vx{u}", [P, ST, HG, 32]) for u in range(2)]
        RING = 3
        probs = [al.sb(f"l1_probs{i}", [P, HG, BANK]) for i in range(RING)]
        nmax, nmax_h = al.sb("nmax", [P, HG, ST]), al.sb("nmax_h", [P, HG, ST], F32R)
        nmax_hl = al.sb("nmax_hl", [P, 2, HG, 2, ST])
        mT = al.sb("mT", [HG * 2 * ST, P], F32R)
        oT = al.sb("oT", [P, S])
        rsum = al.sb("rsum", [P, ST, HG])
        sm = [al.ps(f"l1_sm{i}", [P, S]) for i in range(2)]
        SLOTS = 3
        banks = al.ps("l1_banks", [P, SLOTS + 1, BANK])
        pv = banks[:, SLOTS, :]
        turn_k, turn_q = (banks[:, 2 * n:2 * n + 2, :].rearrange("p b c -> p (b c)") for n in range(2))
        names = ("x_in ones zeros built vx_ok t_ps qT_ok kT_ok scores maxed nmaxh split rows_ps rows_in sE exped pv_ps oT_ok "
                 "back recip tr_free")
        (x_in, ones, zeros, built, vx_ok, t_ps, qT_ok, kT_ok, scores, maxed, nmaxh_ok, split, rows_ps, rows_in, sE, exped, pv_ps,
         oT_ok, back_ps, recip, tr_free) = (al.sem("e_" + n) for n in names.split())
        NC, LAST = len(CHUNKS), GROUPS - 1
        BUILT = 7
        ROWS = 16 * 2 * HG
        first_half = 4

        def cols(w, g, j=slice(None)):
            return w[:, j, bass.ds(g * (HG * HD1), HG * HD1)].rearrange("p j (h c) -> p j h c", h=HG)

        def rows(h):
            return slice(64 * (h % 2), 64 * (h % 2) + 64)

        def phases(eng, phase):
            with eng.Fori(0, (GROUPS - 2) // 2) as i:
                for u in range(2):
                    phase(i * 2 + u, u, True, True)
            phase(LAST - 1, 0, True, False)
            phase(LAST, 1, False, False)

        with nc.Block() as block:

            @block.sync
            def _(sp):
                def load(g):
                    for dst, src in ((qx, "alibi_q"), (kx, "alibi_k")):
                        sp.dma_start(dst[:, :, :, 0:EX].bitcast(F32), io[src][g]).then_inc(x_in, 16)

                def maxima(g, u, first=False):
                    sp.wait_ge(tr_free, 1 if first else 2 * g)
                    for h in range(HG):
                        for c in range(2):
                            src = (2 * h + c) * ST
                            sp.dma_start(qT[u][64 * (h % 2) + c:64 * (h % 2) + c + 1, h // 2, :].bitcast(F32),
                                         mT[src:src + ST, :].bitcast(F32)).then_inc(rows_in, 16)

                def phase(g, u, more):
                    maxima(g + 1, 1 - u)
                    if more:
                        sp.wait_ge(t_ps, 4 * g + 12)
                        load(g + 3)

                load(0)
                sp.wait_ge(t_ps, 4)
                load(1)
                maxima(0, 0, first=True)
                sp.wait_ge(t_ps, 8)
                load(2)
                with sp.Fori(0, 2) as i:
                    for u in range(2):
                        phase(i * 2 + u, u, True)
                for g in range(4, LAST):
                    phase(g, g % 2, g + 3 <= LAST)

            @block.tensor
            def _(pe):
                def build(g, u, first=False):
                    pe.wait_ge(x_in, 32 * g + 32)
                    pe.wait_ge(built, BUILT * g + BUILT)
                    for b, dsts in enumerate(((sm[0], sm[1]), (turn_k, turn_q))):
                        for src, dst in zip((kx, qx), dsts):
                            if dst is turn_k and not first:
                                pe.wait_ge(tr_free, 2 * g - 2 if not (isinstance(g, int) and g == 1) else 1)
                            for j in range(ST):
                                last = pe.transpose(dst[:, j * P:(j + 1) * P],
                                                    src[:, j, 2 * b:2 * b + 2, :].rearrange("p h c -> p (h c)").bitcast(F32),
                                                    keep.ident[:])
                            last.then_inc(t_ps, 1)

                def m(g, u, n):
                    h, i = m_step(n)
                    if n < 2:
                        pe.wait_ge(kT_ok, 4 * g + 4)
                        pe.wait_ge(qT_ok, 2 * g + 2)
                    else:
                        pe.wait_ge(maxed, M_STEPS * g + n - 1)
                    width = (i + 1) * P
                    for c0 in range(0, width, BANK):
                        c1 = min(width, c0 + BANK)
                        pe.matmul(sm[n % 2][:, c0:c1], qT[u][:, h // 2, i * P:(i + 1) * P], kT[u][:, h, c0:c1],
                                  start=True, stop=c1 < width)
                    pe.matmul(sm[n % 2][:, width - P:width], keep.ident_b[:], keep.mask[:],
                              start=False, stop=True).then_inc(scores, 1)

                def maxima(g):
                    pe.wait_ge(split, g + 1)
                    pe.transpose(banks[:, 0, 0:P], nmax_hl[:].rearrange("p z h c i -> p (z h c i)"),
                                 keep.ident[:]).then_inc(rows_ps, 1)

                def e(g, u, n):
                    c, h = n // HG, n % HG
                    j, half = CHUNKS[c]
                    q0, w = chunk_cols(c)
                    if n == 0:
                        pe.wait_ge(rows_in, ROWS * g + ROWS)
                    if n == 2:
                        pe.wait_ge(tr_free, 2 * g + 1)
                    if n >= SLOTS:
                        pe.wait_ge(exped, E_STEPS * g + n + 1 - SLOTS)
                    diagonal = q0 == j * P
                    last = pe.matmul(banks[:, n % SLOTS, 0:w], kT[u][:, h, j * P:(j + 1) * P], qT[u][:, h // 2, q0:q0 + w],
                                     start=True, stop=not diagonal)
                    if diagonal:
                        last = pe.matmul(banks[:, n % SLOTS, 0:P], keep.ident_b[:], keep.mask_t[:], start=False, stop=True)
                    last.then_inc(sE, 1)

                def values(g, u, c):
                    j, half = CHUNKS[c]
                    q0, w = chunk_cols(c)
                    pe.wait_ge(exped, E_STEPS * g + HG * (c + 1))
                    if c == 0:
                        pe.wait_ge(vx_ok, g + 1)
                    if c == first_half:
                        pe.wait_ge(oT_ok, 2 * g + 1)
                    for h in range(HG):
                        last = pe.matmul(pv[32 * h:32 * h + 32, q0 - half * BANK:q0 - half * BANK + w], vx[u][:, j, h, :],
                                         probs[c % RING][:, h, 0:w], start=(j == 0), stop=(j == 4 * half + 3))
                    last.then_inc(pv_ps, 1)

                def back(g):
                    for j in range(ST):
                        last = pe.transpose(turn_q[:, j * P:(j + 1) * P], oT[:, j * P:(j + 1) * P], keep.ident[:])
                    last.then_inc(back_ps, 1)

                def phase(g, u, with_m, with_build):
                    for kind, n in alibi_order(with_m):
                        if kind == "m":
                            m(g + 1, 1 - u, n)
                        elif kind == "e":
                            e(g, u, n)
                        else:
                            values(g, u, n)
                    if with_m:
                        maxima(g + 1)
                    pe.wait_ge(oT_ok, 2 * g + 2)
                    if with_build:
                        pe.wait_ge(maxed, M_STEPS * (g + 2))
                        build(g + 2, u)
                        pe.wait_ge(qT_ok, 2 * g + 6)
                    back(g)

                build(0, 0, first=True)
                for n in range(M_STEPS):
                    m(0, 0, n)
                maxima(0)
                pe.wait_ge(maxed, M_STEPS)
                build(1, 1)
                phases(pe, phase)

            @block.scalar
            def _(act):
                def turned(g, u):
                    for b, src in enumerate((sm[1], turn_q)):
                        act.wait_ge(t_ps, 4 * g + 2 * b + 2)
                        act.copy(qT[u][:, b, :], src[:]).then_inc(qT_ok, 1)
                    act.copy(kT[u][rows(3), 3, :], turn_k[rows(3), :]).then_inc(kT_ok, 1)

                def out(g, half):
                    act.wait_ge(pv_ps, NC * g + (NC if half else first_half))
                    act.copy(oT[:, half * BANK:(half + 1) * BANK], pv).then_inc(oT_ok, 1)

                def phase(g, u, with_m, with_build):
                    for n in range(E_STEPS):
                        c, h = n // HG, n % HG
                        act.wait_ge(sE, E_STEPS * g + n + 1)
                        if h == 0 and c >= RING:
                            act.wait_ge(pv_ps, NC * g + c - RING + 1)
                        w = chunk_cols(c)[1]
                        act.activation(probs[c % RING][:, h, 0:w], banks[:, n % SLOTS, 0:w], ACT.Exp).then_inc(exped, 1)
                        if c == first_half + 1 and h == 0:
                            out(g, 0)
                    out(g, 1)
                    if with_build:
                        turned(g + 2, u)

                act.wait_ge(zeros, 3)
                turned(0, 0)
                turned(1, 1)
                phases(act, phase)

            @block.vector
            def _(dve):
                def turned(g, u):
                    for h, src in enumerate((sm[0], sm[0], turn_k)):
                        dve.wait_ge(t_ps, 4 * g + 2 * (h // 2) + 1)
                        dve.tensor_copy(kT[u][rows(h), h, :], src[rows(h), :]).then_inc(kT_ok, 1)

                def m(g, n):
                    h, i = m_step(n)
                    dve.wait_ge(scores, M_STEPS * g + n + 1)
                    dve.tensor_reduce(nmax[:, h, i:i + 1], sm[n % 2][:, 0:(i + 1) * P], AX.X, ALU.max,
                                      negate=True).then_inc(maxed, 1)

                def maxima(g, first=False):
                    dve.wait_ge(maxed, M_STEPS * (g + 1))
                    dve.tensor_copy(nmax_h[:], nmax[:]).then_inc(nmaxh_ok, 1)
                    dve.wait_ge(nmaxh_ok, g + 1)
                    dve.tensor_copy(nmax_hl[:, 0, :, 0, :], nmax_h[:].bitcast(F32))
                    dve.tensor_tensor(nmax_hl[:, 0, :, 1, :], nmax[:], nmax_h[:].bitcast(F32), ALU.subtract).then_inc(split, 1)
                    if not first:
                        dve.wait_ge(rows_in, ROWS * g)
                    dve.wait_ge(rows_ps, g + 1)
                    dve.tensor_copy(mT[:], banks[0:HG * 2 * ST, 0, 0:P]).then_inc(tr_free, 1)

                def normalise(g):
                    dve.wait_ge(back_ps, g + 1)
                    byhead = turn_q.rearrange("p (j h c) -> p j h c", j=ST, h=HG)
                    dve.reciprocal(rsum[:], byhead[:, :, :, HD1]).then_inc(recip, 1)
                    dve.wait_ge(recip, g + 1)
                    dve.tensor_tensor(cols(keep.attn, g), byhead[:, :, :, 0:HD1],
                                      rsum[:].unsqueeze(3).to_broadcast([P, ST, HG, HD1]), ALU.mult).then_inc(tr_free, 1)

                def phase(g, u, with_m, with_build):
                    if with_m:
                        for n in range(M_STEPS):
                            m(g + 1, n)
                        maxima(g + 1)
                    if with_build:
                        turned(g + 2, u)
                    normalise(g)

                dve.tensor_copy(qx[:, :, :, 32:48], cols(keep.q, 0)).then_inc(built, 1)
                dve.tensor_copy(kx[:, :, :, 48:64], cols(keep.k, 0)).then_inc(built, 1)
                dve.tensor_copy(qx[:, :, :, 16:32], cols(keep.q, 0)).then_inc(built, 1)
                for j in (slice(4, 8), slice(0, 4)):
                    dve.tensor_copy(kx[:, j, :, 16:32], cols(keep.k, 0, j)).then_inc(built, 1)
                dve.wait_ge(built, 2)
                dve.tensor_tensor(qx[:, :, :, 48:64], cols(keep.q, 0), qx[:, :, :, 32:48].bitcast(F32),
                                  ALU.subtract).then_inc(built, 1)
                dve.tensor_tensor(kx[:, :, :, 32:48], cols(keep.k, 0), kx[:, :, :, 48:64].bitcast(F32),
                                  ALU.subtract).then_inc(built, 1)
                dve.wait_ge(zeros, 3)
                turned(0, 0)
                for n in range(M_STEPS):
                    m(0, n)
                maxima(0, first=True)
                turned(1, 1)
                phases(dve, phase)

            @block.gpsimd
            def _(pool):
                def group(g, u):
                    pool.tensor_copy(qx[:, :, :, 32:48], cols(keep.q, g)).then_inc(built, 1)
                    pool.tensor_copy(kx[:, :, :, 48:64], cols(keep.k, g)).then_inc(built, 1)
                    pool.tensor_copy(qx[:, :, :, 16:32], cols(keep.q, g)).then_inc(built, 1)
                    pool.wait_ge(built, BUILT * g + 2)
                    for j in (slice(4, 8), slice(0, 4)):
                        pool.tensor_copy(kx[:, j, :, 16:32], cols(keep.k, g, j)).then_inc(built, 1)
                    pool.tensor_tensor(qx[:, :, :, 48:64], cols(keep.q, g), qx[:, :, :, 32:48].bitcast(F32),
                                       ALU.subtract).then_inc(built, 1)
                    pool.tensor_tensor(kx[:, :, :, 32:48], cols(keep.k, g), kx[:, :, :, 48:64].bitcast(F32),
                                       ALU.subtract).then_inc(built, 1)

                def values(g, u):
                    pool.tensor_copy(vx[u][:, :, :, 0:HD1], cols(keep.v, g)).then_inc(vx_ok, 1)

                for u in range(2):
                    pool.memset(kT[u][:].bitcast(F32), 0.0).then_inc(zeros, 1)
                pool.memset(nmax_hl[:], 0.0).then_inc(zeros, 1)
                for u in range(2):
                    pool.memset(vx[u][:], 0.0).then_inc(ones, 1)
                    pool.wait_ge(ones, 2 * u + 1)
                    pool.memset(vx[u][:, :, :, HD1:HD1 + 1], 1.0).then_inc(ones, 1)
                    pool.wait_ge(ones, 2 * u + 2)
                    values(u, u)
                pool.wait_ge(t_ps, 4)
                group(1, 1)
                with pool.Fori(1, GROUPS // 2) as i:
                    for u in range(2):
                        g = i * 2 + u
                        pool.wait_ge(t_ps, 4 * g)
                        group(g, u)
                        pool.wait_ge(pv_ps, NC * (g - 1))
                        values(g, u)




IM = 1792
IT = IM // P


def stage_gated(nc, io, keep, upto=9):
    with ExitStack() as ctx:
        al = Alloc(nc, ctx)
        xT_h, xT_l = al.sb("x3T_h", [P, DK, S], F32R), al.sb("x3T_l", [P, DK, S], F32R)
        RING = 3
        gT, uT, dT = (al.sb(n, [P, IT, D]) for n in ("gT", "uT", "dT"))
        lnw = al.sb("lnw", [P, D])
        ms, m2 = al.sb("ms", [P, ST]), al.sb("m2", [P, ST])
        n3, n4 = Norm(al, "n3", ST), Norm(al, "n4", ST)
        nr = Norm(al, "nr", ST)
        names = "wo_in ln_in w_in tr_ps tr_h tr_l wt_ps wt_act wt_dve out_ps out_ev nx ms"
        wo_in, ln_in, w_in, tr_ps, tr_h, tr_l, wt_ps, wt_act, wt_dve, out_ps, out_ev, nx, ms_ok = (
            al.sem("g_" + n) for n in names.split())
        w_ins = [al.sem(f"g_w_in{i}") for i in range(RING)]
        tr_src = keep.attn

        with ExitStack() as c1:
            a1 = Alloc(nc, c1)
            wo_f = a1.sb("wo_f", [P, DK, D])
            woT_h, woT_l = a1.sb("woT_h", [P, DK, D], F32R), a1.sb("woT_l", [P, DK, D], F32R)
            stage = a1.sb("w_stage", [P, RING, 3, D])
            tr = [a1.ps(f"g_tr{i}", [P, DK, P]) for i in range(4)]
            po = [a1.ps(f"g_po{i}", [P, D]) for i in range(4)]
            jobs = [([wo_f[:, t, k * P:(k + 1) * P] for k in range(DK)], woT_h, woT_l, slice(t * P, (t + 1) * P)) for t in range(DK)]
            jobs += [([keep.attn[:, j, k * P:(k + 1) * P] for k in range(DK)], xT_h, xT_l, slice(j * P, (j + 1) * P)) for j in range(ST)]
            JX = len(jobs)
            jobs += [([keep.attn[:, j, k * P:(k + 1) * P] for k in range(DK)], xT_h, xT_l, slice(j * P, (j + 1) * P)) for j in range(ST)]
            wjobs = [(t, c) for t in range(IT) for c in range(3)]

            with nc.Block() as block:

                @block.sync
                def _(sp):
                    sp.dma_start(wo_f[:], io["L1_attn_w_out"].rearrange("(t p) n -> p t n", p=P)).then_inc(wo_in, 16)
                    sp.dma_start(lnw[:], io["L1_ffn_ln_w"].partition_broadcast(P)).then_inc(ln_in, 16)
                    for t in range(IT):
                        if t >= RING:
                            sp.wait_ge(wt_ps, 3 * (t - RING) + 3)
                        r = slice(t * P, (t + 1) * P)
                        sp.dma_start(stage[:, t % RING, 0, :], io["L1_ffn_gate_w"][r, :]).then_inc(w_ins[t % RING], 16)
                        sp.dma_start(stage[:, t % RING, 1, :], io["L1_ffn_up_w"][r, :]).then_inc(w_ins[t % RING], 16)
                        sp.dma_start(stage[:, t % RING, 2, :].rearrange("p (k c) -> p k c", k=DK),
                                     io["L1_ffn_down_w"][:, r].rearrange("(k p) c -> p k c", p=P)).then_inc(w_ins[t % RING], 16)

                @block.tensor
                def _(pe):
                    def turn(n):
                        if n >= 2:
                            pe.wait_ge(tr_l, n - 1)
                        for k, src in enumerate(jobs[n][0]):
                            last = pe.transpose(tr[n % 2][:, k, :], src, keep.ident[:])
                        last.then_inc(tr_ps, 1)

                    def turn_weight(m):
                        t, c = wjobs[m]
                        if c == 0:
                            pe.wait_ge(w_ins[t % RING], 48 * (t // RING + 1))
                        if m >= 2:
                            pe.wait_ge((wt_act, wt_dve)[m % 2], m // 2)
                        for k in range(DK):
                            last = pe.transpose(tr[2 + m % 2][:, k, :], stage[:, t % RING, c, k * P:(k + 1) * P], keep.ident[:])
                        last.then_inc(wt_ps, 1)

                    pe.wait_ge(wo_in, 16)
                    for n in range(JX):
                        turn(n)
                    for j in range(ST):
                        pe.wait_ge(tr_l, DK + j + 1)
                        if j >= 4:
                            pe.wait_ge(out_ev, j - 3)
                        rows = slice(j * P, (j + 1) * P)
                        terms = []
                        for k in range(DK):
                            terms += [(xT_h[:, k, rows], woT_h[:, k, :]), (xT_l[:, k, rows], woT_h[:, k, :]),
                                      (xT_h[:, k, rows], woT_l[:, k, :])]
                        three(pe, po[j % 4][:], terms).then_inc(out_ps, 1)
                    for m in range(len(wjobs)):
                        turn_weight(m)
                    for j in range(ST):
                        pe.wait_ge(nx, j + 1)
                        turn(JX + j)

                @block.scalar
                def _(act):
                    def split(n):
                        act.wait_ge(tr_ps, n + 1)
                        act.copy(jobs[n][1][:, :, jobs[n][3]], tr[n % 2][:]).then_inc(tr_h, 1)

                    for n in range(JX):
                        split(n)
                    for m in range(0, len(wjobs), 2):
                        t, c = wjobs[m]
                        act.wait_ge(wt_ps, m + 1)
                        act.copy((gT, uT, dT)[c][:, t, :], tr[2][:].rearrange("p k c -> p (k c)")).then_inc(wt_act, 1)
                        if m == 20:
                            n3.root(act)
                    nr.root(act)
                    for n in range(JX, len(jobs)):
                        split(n)

                @block.vector
                def _(dve):
                    def split(n):
                        dve.wait_ge(tr_h, n + 1)
                        h, l, cols = jobs[n][1:]
                        dve.tensor_tensor(l[:, :, cols], tr[n % 2][:], h[:, :, cols].bitcast(F32), ALU.subtract).then_inc(tr_l, 1)

                    for n in range(JX):
                        split(n)
                    for j in range(ST):
                        dve.wait_ge(out_ps, j + 1)
                        dve.tensor_tensor(keep.x[:, j, :], po[j % 4][:], keep.x[:, j, :], ALU.add).then_inc(out_ev, 1)
                        dve.wait_ge(out_ev, j + 1)
                        n3.stats(dve, j, keep.x[:, j, :])
                    n3.variance(dve)

                    def weight(m):
                        t, c = wjobs[m]
                        dve.wait_ge(wt_ps, m + 1)
                        dve.tensor_copy((gT, uT, dT)[c][:, t, :], tr[3][:].rearrange("p k c -> p (k c)")).then_inc(wt_dve, 1)

                    for m in range(1, 26, 2):
                        weight(m)
                    n3.inverse(dve)
                    for j in range(ST):
                        n3.apply(dve, j, keep.x[:, j, :])
                    for j in range(ST):
                        dve.wait_ge(n3.x_ok, j + 1)
                        nr.stats(dve, j, keep.x[:, j, :])
                    dve.wait_ge(nr.mv_ok, ST)
                    dve.tensor_tensor(m2[:], nr.mv[:, :, 0], nr.mv[:, :, 0], ALU.mult).then_inc(ms_ok, 1)
                    dve.wait_ge(ms_ok, 1)
                    dve.scalar_tensor_tensor(out=nr.sd[:], in0=nr.mv[:, :, 1], scalar=1e-5, in1=m2[:], op0=ALU.add,
                                             op1=ALU.add).then_inc(nr.ve_ok, 1)
                    for m in range(27, len(wjobs), 2):
                        weight(m)
                    nr.inverse(dve)
                    dve.wait_ge(ln_in, 16)
                    for j in range(ST):
                        dve.scalar_tensor_tensor(out=keep.attn[:, j, :], in0=keep.x[:, j, :], scalar=nr.rs[:, j:j + 1],
                                                 in1=lnw[:], op0=ALU.mult, op1=ALU.mult).then_inc(nx, 1)
                    for n in range(JX, len(jobs)):
                        split(n)

        if upto == 3:
            return
        names = "guh gul dh dl gu ex den rec sil a_f a_h a_l down fin"
        guh, gul, dh, dl, gu, ex_ok, den_ok, rec_ok, sil_ok, af_ok, ah_ok, al_ok, down, fin = (al.sem("h_" + n) for n in names.split())
        w_h = [[al.sb(f"{n}_h{i}", [P, D], F32R) for n in "gud"] for i in range(2)]
        w_l = [[al.sb(f"{n}_l{i}", [P, D], F32R) for n in "gud"] for i in range(2)]
        ex, den = al.sb("ex", [P, BANK]), al.sb("den", [P, BANK])
        act_f = al.sb("act_f", [P, BANK])
        a_h = [al.sb(f"a_h{i}", [P, BANK], F32R) for i in range(2)]
        a_l = [al.sb(f"a_l{i}", [P, BANK], F32R) for i in range(2)]
        pg, pu = ([al.ps(f"h_{n}{i}", [P, BANK]) for i in range(2)] for n in "gu")
        pd = [al.ps(f"h_d{i}", [P, D]) for i in range(4)]
        STEPS = 2 * IT

        with nc.Block() as block:

            def each(eng, step):
                for half in range(2):
                    base = half * IT
                    for t in range(2):
                        step(half, base + t, t, t)
                    with eng.Fori(1, IT // 2 - 1) as i:
                        for u in range(2):
                            step(half, i * 2 + (base + u), i * 2 + u, u)
                    for t in range(IT - 2, IT):
                        step(half, base + t, t, t % 2)

            def tile(w, t):
                return w[:, t % IT, :] if isinstance(t, int) else w[:, bass.ds(t, 1), :].rearrange("p o c -> p (o c)")

            def last_step(n):
                return isinstance(n, int) and n == STEPS - 1

            @block.tensor
            def _(pe):
                def down_part(n, u, first, last):
                    pe.wait_ge(dh, n + 1)
                    pe.wait_ge(dl, n + 1)
                    pe.wait_ge(ah_ok, n + 1)
                    pe.wait_ge(al_ok, n + 1)
                    for j in range(4):
                        rows = slice(j * P, (j + 1) * P)
                        end = three(pe, pd[j][:], [(a_h[u][:, rows], w_h[u][2][:]), (a_l[u][:, rows], w_h[u][2][:]),
                                                   (a_h[u][:, rows], w_l[u][2][:])], start=first, stop=last)
                    end.then_inc(down, 1)

                def step(half, n, t, u):
                    cols = slice(half * BANK, (half + 1) * BANK)
                    pe.wait_ge(guh, 2 * n + 2)
                    pe.wait_ge(gul, 2 * n + 2)
                    if not (isinstance(n, int) and n < 2):
                        pe.wait_ge(af_ok, n - 1)
                    for c, dst in ((0, pg[u]), (1, pu[u])):
                        terms = []
                        for k in range(DK):
                            b = slice(k * P, (k + 1) * P)
                            h, l = w_h[u][c][:, b], w_l[u][c][:, b]
                            terms += [(h, xT_h[:, k, cols]), (h, xT_l[:, k, cols]), (l, xT_h[:, k, cols])]
                        three(pe, dst[:], terms).then_inc(gu, 1)
                    if isinstance(n, int) and n == 0:
                        return
                    if isinstance(n, int) and n == IT + 1:
                        pe.wait_ge(fin, 4)
                    before = t - 1 if isinstance(t, int) else None
                    down_part(n - 1, 1 - u, before == 0, before == -1)

                each(pe, step)
                down_part(STEPS - 1, 1, False, True)

            @block.scalar
            def _(act):
                def upper_gu(n, t, u):
                    for c, w in enumerate((gT, uT)):
                        act.copy(w_h[u][c][:], tile(w, t)).then_inc(guh, 1)

                def upper_d(n, t, u):
                    act.copy(w_h[u][2][:], tile(dT, t)).then_inc(dh, 1)

                def step(half, n, t, u):
                    if not last_step(n):
                        if not (isinstance(n, int) and n == 0):
                            act.wait_ge(gu, 2 * n)
                        upper_gu(n + 1, t + 1, 1 - u)
                    act.wait_ge(gu, 2 * n + 1)
                    if not (isinstance(n, int) and n == 0):
                        act.wait_ge(den_ok, n)
                    act.activation(ex[:], pg[u][:], ACT.Exp, scale=-1.0).then_inc(ex_ok, 1)
                    act.wait_ge(af_ok, n + 1)
                    act.copy(a_h[u][:], act_f[:]).then_inc(ah_ok, 1)
                    if not last_step(n):
                        if not (isinstance(n, int) and n == 0):
                            act.wait_ge(down, n)
                        upper_d(n + 1, t + 1, 1 - u)

                upper_gu(0, 0, 0)
                upper_d(0, 0, 0)
                each(act, step)
                n4.root(act)

            @block.gpsimd
            def _(pool):
                def lower_gu(n, t, u):
                    for c, w in enumerate((gT, uT)):
                        pool.wait_ge(guh, 2 * n + c + 1)
                        pool.tensor_tensor(w_l[u][c][:], tile(w, t), w_h[u][c][:].bitcast(F32), ALU.subtract).then_inc(gul, 1)

                def lower_d(n, t, u):
                    pool.wait_ge(dh, n + 1)
                    pool.tensor_tensor(w_l[u][2][:], tile(dT, t), w_h[u][2][:].bitcast(F32), ALU.subtract).then_inc(dl, 1)

                def step(half, n, t, u):
                    if not last_step(n):
                        lower_gu(n + 1, t + 1, 1 - u)
                        lower_d(n + 1, t + 1, 1 - u)

                lower_gu(0, 0, 0)
                lower_d(0, 0, 0)
                each(pool, step)

            @block.vector
            def _(dve):
                def finish(half):
                    dve.wait_ge(down, (half + 1) * IT)
                    for j in range(4):
                        x = keep.x[:, 4 * half + j, :]
                        dve.tensor_tensor(x, pd[j][:], x, ALU.add).then_inc(fin, 1)
                        dve.wait_ge(fin, 4 * half + j + 1)
                        n4.stats(dve, 4 * half + j, x)

                def step(half, n, t, u):
                    dve.wait_ge(ex_ok, n + 1)
                    dve.tensor_scalar(den[:], ex[:], 1.0, None, ALU.add).then_inc(den_ok, 1)
                    dve.wait_ge(den_ok, n + 1)
                    dve.reciprocal(den[:], den[:]).then_inc(rec_ok, 1)
                    dve.wait_ge(rec_ok, n + 1)
                    dve.tensor_tensor(act_f[:], pg[u][:], den[:], ALU.mult).then_inc(sil_ok, 1)
                    dve.wait_ge(sil_ok, n + 1)
                    dve.wait_ge(gu, 2 * n + 2)
                    dve.tensor_tensor(act_f[:], pu[u][:], act_f[:], ALU.mult).then_inc(af_ok, 1)
                    dve.wait_ge(ah_ok, n + 1)
                    dve.tensor_tensor(a_l[u][:], act_f[:], a_h[u][:].bitcast(F32), ALU.subtract).then_inc(al_ok, 1)
                    if isinstance(n, int) and n == IT:
                        finish(0)

                each(dve, step)
                finish(1)
                n4.variance(dve)
                n4.inverse(dve)
                for j in range(ST):
                    n4.apply(dve, j, keep.x[:, j, :])


class Kept:
    pass


def program(nc, io, out, upto=9):
    with ExitStack() as ctx:
        al = Alloc(nc, ctx)
        keep = Kept()
        keep.x = al.sb("x_tok", [P, ST, D])
        keep.ident, keep.ident_b = al.sb("ident", [P, P]), al.sb("ident_b", [P, P], BF16)
        keep.mask, keep.mask_t = al.sb("mask", [P, P], BF16), al.sb("mask_t", [P, P], BF16)
        with ExitStack() as layer0:
            a0 = Alloc(nc, layer0)
            keep.cos, keep.sin = a0.sb("cos", [P, S]), a0.sb("sin", [P, S])
            keep.cqa_h, keep.cqa_l = a0.sb("cqa_h", [P, S], F32R), a0.sb("cqa_l", [P, S], F32R)
            keep.cqb_hh, keep.cqb_l = a0.sb("cqb_hh", [P, S], F32R), a0.sb("cqb_l", [64, S], F32R)
            keep.k_h, keep.k_l = a0.sb("k_h", [P, S], F32R), a0.sb("k_l", [P, S], F32R)
            keep.ckv = a0.sb("ckv", [P, ST, KVL])
            stage_latent(nc, io, keep)
            if upto >= 1:
                stage_mla(nc, io, keep)
        with ExitStack() as layer1:
            a1 = Alloc(nc, layer1)
            keep.attn = a1.sb("attn", [P, ST, D])
            with ExitStack() as heads:
                a2 = Alloc(nc, heads)
                keep.q, keep.k, keep.v = (a2.sb("l1_" + n, [P, ST, D]) for n in "qkv")
                with ExitStack() as proj:
                    a3 = Alloc(nc, proj)
                    keep.wqkv, keep.qk_ln = a3.sb("wqkv", [P, 3 * D // P, D]), a3.sb("qk_ln", [P, 4, D])
                    keep.wqkv_in, keep.ln_in = a3.sem("wqkv_in"), a3.sem("ln_in")
                    if upto >= 2:
                        stage_route(nc, io, keep)
                    if upto >= 3:
                        stage_qkv(nc, io, keep)
                if upto >= 3:
                    stage_alibi(nc, io, keep)
            if upto >= 3:
                stage_gated(nc, io, keep, upto)
        with ExitStack() as last:
            stored = Alloc(nc, last).sem("stored")
            with nc.Block() as block:

                @block.sync
                def _(sp):
                    sp.dma_start(out.rearrange("b (j p) d -> p (b j) d", p=P), keep.x[:]).then_inc(stored, 16)
                    sp.wait_ge(stored, 16)


_NAMES = {n.split("_", 2)[2] if n.startswith("L0_attn") else n: n for n in [
    "L0_attn_w_q_down", "L0_attn_w_q_up_nope", "L0_attn_w_q_up_rope", "L0_attn_w_kv_down", "L0_attn_w_k_rope",
    "L0_attn_w_uk", "L0_attn_w_uv", "L0_attn_w_out", "L0_ffn_W", "L0_ffn_b", "L0_ffn_A", "L0_ffn_B",
    "L0_ffn_gate_w", "L0_ffn_gate_b", "L1_attn_w_qkv", "L1_attn_q_ln_w", "L1_attn_q_ln_b", "L1_attn_k_ln_w",
    "L1_attn_k_ln_b", "L1_attn_w_out", "L1_ffn_ln_w", "L1_ffn_gate_w", "L1_ffn_up_w", "L1_ffn_down_w"]}


def layout(inputs):
    arrays = {"x": np.ascontiguousarray(inputs["L0_attn_hidden_states"])}
    for short, name in _NAMES.items():
        arrays[short] = np.ascontiguousarray(inputs[name])
    arrays["cos"], arrays["sin"] = rope_tables()
    arrays["alibi_q"], arrays["alibi_k"] = alibi_columns()
    return arrays


def kernel(**inputs):
    import concourse.bacc as bacc
    from concourse.bass_utils import run_bass_kernel_spmd

    nc = bacc.Bacc("TRN2", target_bir_lowering=False, num_devices=1)
    arrays = layout(inputs)
    io = {n: nc.dram_tensor(f"in_{n}", a.shape, mybir.dt.from_np(a.dtype), kind="ExternalInput").ap()
          for n, a in arrays.items()}
    out = nc.dram_tensor("out_0_dram", (1, S, D), F32, kind="ExternalOutput").ap()
    program(nc, io, out)
    r = run_bass_kernel_spmd(nc, [{f"in_{n}": a for n, a in arrays.items()}], core_ids=[0])
    return r.results[0]["out_0_dram"]
```

```python
from contextlib import ExitStack

import numpy as np

import concourse.bass as bass
from concourse import mybir

F32 = mybir.dt.float32
F32R = mybir.dt.float32r
BF16 = mybir.dt.bfloat16
ACT = mybir.ActivationFunctionType
ALU = mybir.AluOpType
AX = mybir.AxisListType

P = 128
S = 1024
D = 512
ST = S // P
DK = D // P
BANK = 512
NEG = -3.0e38

H0, QL, KVL, DN, DR, DV = 32, 192, 64, 128, 64, 128
PAIRS = H0 // 2
SCALE0 = float(1.0 / np.sqrt(np.float32(DN + DR)))


SWAPS = ((slice(64, 96), slice(96, 128)), (slice(96, 128), slice(64, 96)))


def rope_tables():
    freqs = np.float32(1.0) / np.float32(10000.0) ** (np.arange(0, DR, 2, dtype=np.float32) / np.float32(DR))
    wavelengths = np.float32(2.0 * np.pi) / freqs
    ramp = np.clip((wavelengths / np.float32(4096.0) - np.float32(1.0)) / np.float32(31.0), 0, 1).astype(np.float32)
    inv = (freqs / (np.float32(1.0) - ramp + ramp * np.float32(40.0))).astype(np.float32)
    f = np.arange(S, dtype=np.float32)[None, :] * inv[:, None]
    cos, sin = np.cos(f).astype(np.float32), np.sin(f).astype(np.float32)
    return np.tile(cos, (4, 1)), np.concatenate([-sin, sin, -sin, sin])


class Alloc:

    def __init__(self, nc, ctx):
        self.nc, self.ctx = nc, ctx

    def sb(self, name, shape, dt=F32):
        return self.ctx.enter_context(self.nc.sbuf_tensor(name, shape, dt))

    def ps(self, name, shape, dt=F32):
        return self.ctx.enter_context(self.nc.psum_tensor(name, shape, dt))

    def sem(self, name):
        return self.ctx.enter_context(self.nc.semaphore(name))


def from_one(eng, sem, value):
    if not (isinstance(value, int) and value <= 0):
        eng.wait_ge(sem, value)


def three(pe, out, terms, start=True, stop=True):
    for n, (l, r) in enumerate(terms):
        last = pe.matmul(out, l, r, start=start and n == 0, stop=stop and n == len(terms) - 1)
    return last


def stage_latent(nc, io, keep):
    with ExitStack() as ctx:
        al = Alloc(nc, ctx)
        xT_h = al.sb("xT_h", [P, DK, S], F32R)
        xT_l = al.sb("xT_l", [P, DK, S], F32R)
        WD = QL + 2 * 64
        wd_f = al.sb("wd_f", [P, DK, WD])
        wd_h = al.sb("wd_h", [P, DK, WD], F32R)
        wd_l = al.sb("wd_l", [P, DK, WD], F32R)
        k_f = al.sb("k_f", [P, S])
        k_sw = al.sb("k_sw", [P, S])
        tr = [al.ps(f"tr{i}", [P, DK, P]) for i in range(2)]
        pj = [al.ps(f"pj{i}", [P, BANK]) for i in range(3)]
        pc = al.ps("pc", [P, ST, KVL])

        x_in, wd_in = [al.sem(f"a_x_in{n}") for n in range(2)], al.sem("a_wd_in")
        const_ok, xT_ps, xTh_ok, xTl_ok = (al.sem(n) for n in ("a_const", "a_xT_ps", "a_xTh", "a_xTl"))
        wdh_ok, wdl_ok = al.sem("a_wdh"), al.sem("a_wdl")
        proj_ps, act_ev, dve_ev = al.sem("a_proj"), al.sem("a_act_ev"), al.sem("a_dve_ev")
        kf_ok, kh_ok = al.sem("a_kf"), al.sem("a_kh")
        ckv_ps, done = al.sem("a_ckv_ps"), al.sem("a_done")
        tiles = [(0, P), (P, QL - P), (QL, P)]

        with nc.Block() as block:

            @block.sync
            def _(sp):
                x = io["x"].rearrange("b (j p) d -> p (b j) d", p=P)
                for n in range(2):
                    sp.dma_start(keep.x[:, 4 * n:4 * n + 4, :], x[:, 4 * n:4 * n + 4, :]).then_inc(x_in[n], 16)
                rope = io["w_k_rope"].rearrange("(k p) n -> p k n", p=P)
                kv = io["w_kv_down"].rearrange("(k p) n -> p k n", p=P)
                sp.dma_start(wd_f[:, :, 0:QL], io["w_q_down"].rearrange("(k p) n -> p k n", p=P)).then_inc(wd_in, 16)
                sp.dma_start(wd_f[:, :, QL:QL + 64], kv).then_inc(wd_in, 16)
                sp.dma_start(wd_f[:, :, QL + 64:QL + 128], rope).then_inc(wd_in, 16)
                sp.dma_start(keep.cos[:], io["cos"]).then_inc(wd_in, 16)
                sp.dma_start(keep.sin[:], io["sin"]).then_inc(wd_in, 16)

            @block.gpsimd
            def _(pool):
                pool.memset(keep.ident[:], 0.0).then_inc(const_ok, 1)
                pool.memset(keep.ident_b[:], 0.0).then_inc(const_ok, 1)
                pool.memset(keep.mask[:], 0.0).then_inc(const_ok, 1)
                pool.memset(keep.mask_t[:], 0.0).then_inc(const_ok, 1)
                pool.wait_ge(const_ok, 4)
                for m in (keep.ident, keep.ident_b):
                    pool.affine_select(out=m[:], in_=m[:], compare_op=ALU.not_equal, fill=1.0, base=0,
                                       pattern=[[-1, P]], channel_multiplier=1).then_inc(const_ok, 1)
                pool.affine_select(out=keep.mask[:], in_=keep.mask[:], compare_op=ALU.is_ge, fill=NEG, base=0,
                                   pattern=[[-1, P]], channel_multiplier=1).then_inc(const_ok, 1)
                pool.affine_select(out=keep.mask_t[:], in_=keep.mask_t[:], compare_op=ALU.is_ge, fill=NEG, base=0,
                                   pattern=[[1, P]], channel_multiplier=-1).then_inc(const_ok, 1)

            @block.tensor
            def _(pe):
                pe.wait_ge(const_ok, 8)
                for j in range(ST):
                    pe.wait_ge(x_in[j // 4], 16)
                    if j >= 2:
                        pe.wait_ge(xTl_ok, j - 1)
                    for k in range(DK):
                        last = pe.transpose(tr[j % 2][:, k, :], keep.x[:, j, k * P:(k + 1) * P], keep.ident[:])
                    last.then_inc(xT_ps, 1)
                pe.wait_ge(wdl_ok, 1)
                for n in range(2):
                    pe.wait_ge(xTl_ok, 4 * n + 4)
                    half = slice(n * BANK, (n + 1) * BANK)
                    for t, (c, m) in enumerate(tiles):
                        if n == 1:
                            pe.wait_ge(act_ev, t + 1)
                            pe.wait_ge(dve_ev, t + 1 if t < 2 else 5)
                        terms = []
                        for k in range(DK):
                            h, l = wd_h[:, k, c:c + m], wd_l[:, k, c:c + m]
                            terms += [(h, xT_h[:, k, half]), (h, xT_l[:, k, half]), (l, xT_h[:, k, half])]
                        three(pe, pj[t][0:m, :], terms).then_inc(proj_ps, 1)
                kv = slice(QL, QL + KVL)
                for j in range(ST):
                    cols = slice(j * P, (j + 1) * P)
                    terms = []
                    for k in range(DK):
                        h, l = wd_h[:, k, kv], wd_l[:, k, kv]
                        terms += [(xT_h[:, k, cols], h), (xT_l[:, k, cols], h), (xT_h[:, k, cols], l)]
                    last = three(pe, pc[:, j, :], terms)
                last.then_inc(ckv_ps, 1)

            @block.scalar
            def _(act):
                for j in range(ST):
                    act.wait_ge(xT_ps, j + 1)
                    act.copy(xT_h[:, :, j * P:(j + 1) * P], tr[j % 2][:]).then_inc(xTh_ok, 1)
                for n in range(2):
                    half = slice(n * BANK, (n + 1) * BANK)
                    act.wait_ge(proj_ps, 3 * n + 1)
                    act.copy(keep.cqa_h[:, half], pj[0][:]).then_inc(act_ev, 1)
                    act.wait_ge(proj_ps, 3 * n + 2)
                    act.copy(keep.cqb_hh[64:128, half], pj[1][0:64, :]).then_inc(done, 1)
                    act.copy(keep.cqb_hh[0:64, half], pj[1][0:64, :]).then_inc(act_ev, 1)
                    act.wait_ge(proj_ps, 3 * n + 3)
                    act.copy(k_f[0:64, half], pj[2][0:64, :]).then_inc(act_ev, 1)
                    act.wait_ge(act_ev, 4 * n + 3)
                    act.wait_ge(kf_ok, n + 1)
                    act.copy(keep.k_h[:, half], k_f[:, half]).then_inc(act_ev, 1)
                act.wait_ge(ckv_ps, 1)
                act.copy(keep.ckv[:], pc[:]).then_inc(done, 1)

            @block.vector
            def _(dve):
                dve.wait_ge(wd_in, 16 * 5)
                dve.tensor_copy(wd_h[:], wd_f[:]).then_inc(wdh_ok, 1)
                dve.wait_ge(wdh_ok, 1)
                dve.tensor_tensor(wd_l[:], wd_f[:], wd_h[:].bitcast(F32), ALU.subtract).then_inc(wdl_ok, 1)
                for j in range(ST):
                    dve.wait_ge(xTh_ok, j + 1)
                    dve.tensor_tensor(xT_l[:, :, j * P:(j + 1) * P], tr[j % 2][:],
                                      xT_h[:, :, j * P:(j + 1) * P].bitcast(F32), ALU.subtract).then_inc(xTl_ok, 1)
                rope = slice(64, 128)
                for n in range(2):
                    half = slice(n * BANK, (n + 1) * BANK)
                    dve.wait_ge(act_ev, 4 * n + 1)
                    dve.tensor_tensor(keep.cqa_l[:, half], pj[0][:], keep.cqa_h[:, half].bitcast(F32),
                                      ALU.subtract).then_inc(dve_ev, 1)
                    dve.wait_ge(act_ev, 4 * n + 2)
                    dve.tensor_tensor(keep.cqb_l[0:64, half], pj[1][0:64, :], keep.cqb_hh[0:64, half].bitcast(F32),
                                      ALU.subtract).then_inc(dve_ev, 1)
                    dve.wait_ge(proj_ps, 3 * n + 3)
                    dve.tensor_tensor(k_f[rope, half], pj[2][rope, :], keep.cos[rope, half], ALU.mult).then_inc(dve_ev, 1)
                    for to, at in SWAPS:
                        dve.scalar_tensor_tensor(out=k_sw[to, half], in0=pj[2][at, :], scalar=-1.0, in1=keep.sin[at, half],
                                                 op0=ALU.mult, op1=ALU.mult).then_inc(dve_ev, 1)
                    dve.wait_ge(dve_ev, 5 * n + 5)
                    dve.tensor_tensor(k_f[rope, half], k_f[rope, half], k_sw[rope, half], ALU.add).then_inc(kf_ok, 1)
                    dve.wait_ge(act_ev, 4 * n + 4)
                    dve.tensor_tensor(keep.k_l[:, half], k_f[:, half], keep.k_h[:, half].bitcast(F32),
                                      ALU.subtract).then_inc(done, 1)


def stage_mla(nc, io, keep):
    with ExitStack() as ctx:
        al = Alloc(nc, ctx)
        nope_a, nope_b = al.sb("nope_a", [P, 2 * DN]), al.sb("nope_b", [64, 2 * DN])
        wuk, wuv = al.sb("wuk", [P, 2, KVL]), al.sb("wuv", [P, 2, KVL])
        wout = al.sb("wout", [P, 2, D])
        nope_t = al.sb("nope_t", [P, 2, QL])
        wa_f, wb_f = al.sb("wa_f", [P, 2 * P]), al.sb("wb_f", [64, 2 * P])
        wa_h, wa_l = al.sb("wa_h", [P, 2 * P], F32R), al.sb("wa_l", [P, 2 * P], F32R)
        wb_hl = al.sb("wb_hl", [P, 2 * P], F32R)
        q_f = [al.sb(f"q_f{e}", [P, S]) for e in range(2)]
        q_sw = [al.sb(f"q_sw{e}", [P, S]) for e in range(2)]
        q_h = [al.sb(f"q_h{e}", [P, S], F32R) for e in range(2)]
        q_l = [al.sb(f"q_l{e}", [P, S], F32R) for e in range(2)]
        probs = [al.sb(f"probs{i}", [P, S]) for i in range(4)]
        stat = al.sb("stat", [P, 3, 4])
        pt = [al.sb(f"pt{g}", [P, 2, 4 * (g + 1), BANK]) for g in range(2)]
        ol_h, ol_l = al.sb("ol_h", [P, S], F32R), al.sb("ol_l", [P, S], F32R)
        wo_h, wo_l = al.sb("wo_h", [P, D], F32R), al.sb("wo_l", [P, D], F32R)

        sc = [al.ps(f"sc{i}", [P, S]) for i in range(2)]
        tb = [al.ps(f"tb{i}", [P, 4, P]) for i in range(2)]
        mb = [al.ps(f"mb{i}", [P, BANK]) for i in range(2)]

        names = ("wq_in wo_in scores negmax exp recip pnorm pt_ps pt_ev pv olat_h wt_ps wlat_ps wlat_ev "
                 "wsplit qp qlat qadd qh ql wo_ps wo_h op").split()
        (wq_in, wo_in, scores, negmax, exped, recip, pnorm, pt_ps, pt_ev, pv, olat_h, wt_ps, wlat_ps, wlat_ev,
         wsplit, qp, qlat, qadd, qh_ok, ql_ok, wo_ps, woh_ok, op) = (al.sem("b_" + n) for n in names)
        mb_read = [al.sem(f"b_mb_read{i}") for i in range(2)]

        NS = 2 * ST
        groups = []
        for n in range(NS):
            for j0 in range(0, n // 2 + 1, 4):
                groups.append((n, j0, min(4, n // 2 + 1 - j0)))
        NG = len(groups)
        NWQ, NWO = 5, 2
        QUERIES = [(0, 0), (0, 1), (1, 0), (1, 1)]
        WORK = {1: [("out", 0)], 2: [("out", 1), ("up", 0)], 3: [("values", 1)], 4: [("out", 2), ("out", 3)],
                5: [("latent", 0), ("out", 4)], 6: [("out", 5)], 7: [("out", 6)], 8: [("out", 7)],
                9: [("out_weights", 0), ("query", 0)], 10: [("query", 1)], 11: [("query", 2)],
                12: [("query", 3)], 15: [("values", 0)]}

        OUT_BANK = (0, 1, 0, 1, 1, 0, 1, 0)

        def bank(kind, k):
            return {"up": 0, "latent": 0, "out_weights": 1, "out": OUT_BANK[k]}.get(kind, k % 2)

        def pair_of(kind, k):
            if kind in ("up", "latent", "query"):
                return 1
            return -1 if kind == "out" or (kind, k) == ("values", 1) else 0

        def works(rnd, n=None):
            kept = (1,) if rnd == -1 else (0, 1) if rnd == 0 else (-1, 0) if rnd == PAIRS - 1 else (-1,) if rnd == PAIRS else (-1, 0, 1)
            return [w for m in range(NS) for w in WORK.get(m, ()) if pair_of(*w) in kept and n in (None, m)]

        def reads(rnd, kind, k):
            same = lambda r: [w for w in works(r) if bank(*w) == bank(kind, k)]
            if not isinstance(rnd, int):
                return rnd * len(same(1)) + (reads(1, kind, k) - len(same(1)))
            return sum(len(same(r)) for r in range(-1, rnd)) + same(rnd).index((kind, k)) + 1

        def shape_of(rnd):
            return rnd if isinstance(rnd, int) else 1

        def load_q(sp, r):
            cols = lambda w, c0, n, r0, r1: io[w][r0:r1, bass.ds(r * c0, n)]
            sp.dma_start(nope_a[:], cols("w_q_up_nope", 2 * DN, 2 * DN, 0, P)).then_inc(wq_in, 16)
            sp.dma_start(nope_b[:], cols("w_q_up_nope", 2 * DN, 2 * DN, P, QL)).then_inc(wq_in, 16)
            for w, r0, r1 in ((wa_f, 0, P), (wb_f, P, QL)):
                src = cols("w_q_up_rope", 2 * DR, 2 * DR, r0, r1)
                heads = w[:].rearrange("p (e c) -> p e c", e=2)
                sp.dma_start(heads[:, :, KVL:P], src.rearrange("p (e c) -> p e c", e=2)).then_inc(wq_in, 16)

        def load_o(sp, r):
            rows = lambda w: io[w][bass.ds(r * 2 * DV, 2 * DV), :].rearrange("(e d) n -> d e n", e=2)
            sp.dma_start(wuv[:], rows("w_uv")).then_inc(wo_in, 16)
            sp.dma_start(wout[:], rows("w_out")).then_inc(wo_in, 16)

        def load_k(sp, r):
            sp.dma_start(wuk[:], io["w_uk"][bass.ds(r * 2 * DN, 2 * DN), :].rearrange("(e d) n -> d e n", e=2))\
                .then_inc(wq_in, 16)

        with nc.Block() as block:

            @block.sync
            def _(sp):
                load_q(sp, 0)
                load_k(sp, 0)
                load_o(sp, 0)

                def pair(p, more):
                    if more:
                        sp.wait_ge(wt_ps, p + 1)
                        sp.wait_ge(wlat_ps, p + 1)
                        sp.wait_ge(wsplit, 4 * p + 4)
                        load_q(sp, p + 1)
                        load_k(sp, p + 1)
                        sp.wait_ge(wo_ps, p + 1)
                        load_o(sp, p + 1)

                pair(0, True)
                with sp.Fori(1, PAIRS - 1) as p:
                    pair(p, True)

            @block.tensor
            def _(pe):
                def bank_free(rnd, kind, k):
                    from_one(pe, mb_read[bank(kind, k)], reads(rnd, kind, k) - 1)

                def up(rnd, r, k):
                    pe.wait_ge(wq_in, (r + 1) * (16 * NWQ))
                    bank_free(rnd, "up", k)
                    wt = mb[0][:, 0:2 * QL].rearrange("p (e c) -> p e c", e=2)
                    for e in range(2):
                        pe.transpose(wt[:, e, 0:P], nope_a[:, e * DN:(e + 1) * DN], keep.ident[:])
                        last = pe.transpose(wt[:, e, P:QL], nope_b[:, e * DN:(e + 1) * DN], keep.ident[0:64, 0:64])
                    last.then_inc(wt_ps, 1)

                def latent(rnd, r, k):
                    bank_free(rnd, "latent", k)
                    for e in range(2):
                        pe.matmul(mb[0][:, e * 64:e * 64 + 64], nope_t[:, e, 0:P], wuk[:, e, :], start=True, stop=True)
                        last = pe.matmul(mb[0][0:64, P + e * 64:P + e * 64 + 64], nope_t[:, e, P:QL], wuk[:, e, :],
                                         start=True, stop=True)
                    last.then_inc(wlat_ps, 1)

                def query(rnd, r, k):
                    t, h = QUERIES[k]
                    if k == 0:
                        pe.wait_ge(wsplit, 4 * r + 4)
                    bank_free(rnd, "query", k)
                    cols, half = slice(t * P, (t + 1) * P), slice(h * BANK, (h + 1) * BANK)
                    three(pe, mb[k % 2][:], [
                        (wa_h[:, cols], keep.cqa_h[:, half]), (wa_h[:, cols], keep.cqa_l[:, half]),
                        (wa_l[:, cols], keep.cqa_h[:, half]), (wb_hl[:, cols], keep.cqb_hh[:, half]),
                        (wb_hl[0:64, cols], keep.cqb_l[0:64, half])]).then_inc(qp, 1)

                def score(p, n):
                    i, e = n // 2, n % 2
                    from_one(pe, exped, NS * p + n - 1)
                    if n < 2:
                        pe.wait_ge(qh_ok, 2 * p + e + 1)
                        pe.wait_ge(ql_ok, 2 * p + e + 1)
                    rows = slice(i * P, (i + 1) * P)
                    width = (i + 1) * P
                    for c0 in range(0, width, BANK):
                        w = min(BANK, width - c0)
                        keys = slice(c0, c0 + w)
                        diagonal = c0 + w == width
                        last = three(pe, sc[n % 2][:, keys], [
                            (q_h[e][:, rows], keep.k_h[:, keys]), (q_h[e][:, rows], keep.k_l[:, keys]),
                            (q_l[e][:, rows], keep.k_h[:, keys])], stop=not diagonal)
                        if diagonal:
                            last = pe.matmul(sc[n % 2][:, width - P:width], keep.ident_b[:], keep.mask[:],
                                             start=False, stop=True)
                    last.then_inc(scores, 1)

                def turn(p, n):
                    pe.wait_ge(pnorm, NS * p + n + 1)
                    for g, (m, j0, nb) in enumerate(groups):
                        if m == n:
                            from_one(pe, pt_ev, NG * p + g - 1)
                            for b in range(nb):
                                last = pe.transpose(tb[g % 2][:, b, :], probs[n % 4][:, (j0 + b) * P:(j0 + b + 1) * P],
                                                    keep.ident[:])
                            last.then_inc(pt_ps, 1)

                def values(rnd, p, g):
                    pe.wait_ge(pt_ev, NG * p + (8 if g == 0 else NG))
                    bank_free(rnd, "values", g)
                    for j in range(4 * (g + 1)):
                        off = max(0, j - 4 * g) * P
                        for e in range(2):
                            last = pe.matmul(mb[g][64 * e:64 * e + 64, off:BANK], keep.ckv[:, j, :],
                                             pt[g][:, e, j, off:BANK], start=(j == 0), stop=(j == 4 * g + 3))
                    last.then_inc(pv, 1)

                def out_weights(rnd, p, k):
                    pe.wait_ge(wo_in, (p + 1) * (16 * NWO))
                    bank_free(rnd, "out_weights", k)
                    for e in range(2):
                        last = pe.matmul(mb[1][64 * e:64 * e + 64, :], wuv[:, e, :], wout[:, e, :], start=True, stop=True)
                    last.then_inc(wo_ps, 1)

                def out(rnd, p, j):
                    if j in (0, 4):
                        pe.wait_ge(mb_read[j // 4], reads(rnd - 1 if j == 0 else rnd, "values", j // 4))
                    if j == 0:
                        pe.wait_ge(mb_read[1], reads(rnd - 1, "out_weights", 0))
                    bank_free(rnd, "out", j)
                    rows = slice(j * P, (j + 1) * P)
                    three(pe, mb[OUT_BANK[j]][:], [(ol_h[:, rows], wo_h[:]), (ol_h[:, rows], wo_l[:]),
                                             (ol_l[:, rows], wo_h[:])]).then_inc(op, 1)

                work = {"up": up, "latent": latent, "query": query, "values": values, "out_weights": out_weights, "out": out}

                def steps(rnd):
                    for n in range(NS):
                        score(rnd, n)
                        if n >= 2:
                            turn(rnd, n - 2)
                        elif not (isinstance(rnd, int) and rnd == 0):
                            turn(rnd - 1, NS - 2 + n)
                        for kind, k in works(shape_of(rnd), n):
                            work[kind](rnd, rnd + pair_of(kind, k), k)

                for kind, k in works(-1):
                    work[kind](-1, 0, k)
                steps(0)
                with pe.Fori(1, PAIRS - 1) as rnd:
                    steps(rnd)
                steps(PAIRS - 1)
                turn(PAIRS - 1, NS - 2)
                turn(PAIRS - 1, NS - 1)
                for kind, k in works(PAIRS):
                    work[kind](PAIRS, PAIRS - 1, k)

            @block.scalar
            def _(act):
                def up(rnd, r, k):
                    act.wait_ge(wt_ps, r + 1)
                    act.copy(nope_t[:].rearrange("p e c -> p (e c)"), mb[0][:, 0:2 * QL]).then_inc(mb_read[0], 1)

                def latent(rnd, r, k):
                    act.wait_ge(wlat_ps, r + 1)
                    for w, m, c, ok in ((wa_f, P, 0, wlat_ev), (wb_f, 64, P, mb_read[0])):
                        act.copy(w[:].rearrange("p (e c) -> p e c", e=2)[:, :, 0:KVL],
                                 mb[0][0:m, c:c + P].rearrange("p (e c) -> p e c", e=2)).then_inc(ok, 1)
                    act.wait_ge(wlat_ev, r + 1)
                    act.wait_ge(mb_read[0], reads(rnd, "latent", 0))
                    act.wait_ge(wq_in, (r + 1) * (16 * NWQ))
                    from_one(act, qp, 4 * r)
                    act.copy(wa_h[:], wa_f[:]).then_inc(wsplit, 1)
                    act.copy(wb_hl[0:64, :], wb_f[:]).then_inc(wsplit, 1)

                def query(rnd, r, k):
                    e, half = QUERIES[k]
                    act.wait_ge(qp, 4 * r + k + 1)
                    act.mul(q_f[e][0:64, half * BANK:(half + 1) * BANK], mb[k % 2][0:64, :], SCALE0).then_inc(qlat, 1)

                def values(rnd, p, g):
                    act.wait_ge(pv, 2 * p + g + 1)
                    from_one(act, op, 8 * p)
                    act.copy(ol_h[:, g * BANK:(g + 1) * BANK], mb[g][:]).then_inc(olat_h, 1)

                def out_weights(rnd, p, k):
                    act.wait_ge(wo_ps, p + 1)
                    act.copy(wo_h[:], mb[1][:]).then_inc(woh_ok, 1)

                def split_query(r, e):
                    act.wait_ge(qlat, 4 * r + 2 * e + 2)
                    act.wait_ge(qadd, 4 * r + 2 * e + 2)
                    act.copy(q_h[e][:], q_f[e][:]).then_inc(qh_ok, 1)

                def exp(p, n):
                    act.wait_ge(negmax, NS * p + n + 1)
                    w, s = (n // 2 + 1) * P, n % 4
                    act.activation(probs[s][:, 0:w], sc[n % 2][:, 0:w], ACT.Exp, bias=stat[:, 0, s:s + 1],
                                   accum_out=stat[:, 1, s:s + 1]).then_inc(exped, 1)

                def turned(p, n):
                    i, e = n // 2, n % 2
                    for g, (m, j0, nb) in enumerate(groups):
                        if m == n:
                            act.wait_ge(pt_ps, NG * p + g + 1)
                            act.copy(pt[i // 4][:, e, j0:j0 + nb, (i % 4) * P:(i % 4 + 1) * P],
                                     tb[g % 2][:, 0:nb, :]).then_inc(pt_ev, 1)

                work = {"up": up, "latent": latent, "query": query, "values": values, "out_weights": out_weights}

                def steps(rnd):
                    more = not (isinstance(rnd, int) and rnd == PAIRS - 1)
                    for n in range(NS):
                        if n >= NS - 2 and more:
                            act.wait_ge(scores, NS * rnd + n + 1)
                            split_query(rnd + 1, n % 2)
                        if n >= 2:
                            turned(rnd, n - 2)
                        elif not (isinstance(rnd, int) and rnd == 0):
                            turned(rnd - 1, NS - 2 + n)
                        exp(rnd, n)
                        for kind, k in works(shape_of(rnd), n):
                            if kind in work:
                                work[kind](rnd, rnd + pair_of(kind, k), k)

                for kind, k in works(-1):
                    work[kind](-1, 0, k)
                for e in range(2):
                    split_query(0, e)
                steps(0)
                with act.Fori(1, PAIRS - 1) as rnd:
                    steps(rnd)
                steps(PAIRS - 1)
                turned(PAIRS - 1, NS - 2)
                turned(PAIRS - 1, NS - 1)
                for kind, k in works(PAIRS):
                    if kind in work:
                        work[kind](PAIRS, PAIRS - 1, k)

            @block.vector
            def _(dve):
                def query(rnd, r, k):
                    e, h = QUERIES[k]
                    rope, half = slice(64, 128), slice(h * BANK, (h + 1) * BANK)
                    dve.wait_ge(qp, 4 * r + k + 1)
                    for to, at in SWAPS:
                        dve.scalar_tensor_tensor(out=q_sw[e][to, half], in0=mb[k % 2][at, :], scalar=-SCALE0,
                                                 in1=keep.sin[at, half], op0=ALU.mult, op1=ALU.mult)
                    dve.wait_ge(qlat, 4 * r + k + 1)
                    last = dve.scalar_tensor_tensor(out=q_f[e][rope, half], in0=mb[k % 2][rope, :], scalar=SCALE0,
                                                    in1=keep.cos[rope, half], op0=ALU.mult, op1=ALU.mult)
                    last.then_inc(mb_read[k % 2], 1)

                def values(rnd, p, g):
                    dve.wait_ge(olat_h, 2 * p + g + 1)
                    half = slice(g * BANK, (g + 1) * BANK)
                    dve.tensor_tensor(ol_l[:, half], mb[g][:], ol_h[:, half].bitcast(F32), ALU.subtract).then_inc(mb_read[g], 1)

                def out_weights(rnd, p, k):
                    dve.wait_ge(woh_ok, p + 1)
                    dve.tensor_tensor(wo_l[:], mb[1][:], wo_h[:].bitcast(F32), ALU.subtract).then_inc(mb_read[1], 1)

                def out(rnd, p, j):
                    dve.wait_ge(op, 8 * p + j + 1)
                    dve.tensor_tensor(keep.x[:, j, :], mb[OUT_BANK[j]][:], keep.x[:, j, :],
                                      ALU.add).then_inc(mb_read[OUT_BANK[j]], 1)

                def split_query(r, e):
                    dve.wait_ge(qh_ok, 2 * r + e + 1)
                    dve.tensor_tensor(q_l[e][:], q_f[e][:], q_h[e][:].bitcast(F32), ALU.subtract).then_inc(ql_ok, 1)

                def row_max(p, n):
                    dve.wait_ge(scores, NS * p + n + 1)
                    dve.tensor_reduce(stat[:, 0, n % 4:n % 4 + 1], sc[n % 2][:, 0:(n // 2 + 1) * P], AX.X, ALU.max,
                                      negate=True).then_inc(negmax, 1)

                def normalise(p, n):
                    s, w = n % 4, (n // 2 + 1) * P
                    dve.wait_ge(exped, NS * p + n + 1)
                    dve.reciprocal(stat[:, 2, s:s + 1], stat[:, 1, s:s + 1]).then_inc(recip, 1)
                    dve.wait_ge(recip, NS * p + n + 1)
                    dve.tensor_scalar(probs[s][:, 0:w], probs[s][:, 0:w], stat[:, 2, s:s + 1], None,
                                      ALU.mult).then_inc(pnorm, 1)

                work = {"query": query, "values": values, "out_weights": out_weights, "out": out}

                def steps(rnd):
                    more = not (isinstance(rnd, int) and rnd == PAIRS - 1)
                    for n in range(NS):
                        if n == NS - 1 and more:
                            split_query(rnd + 1, 0)
                        row_max(rnd, n)
                        if n >= 1:
                            normalise(rnd, n - 1)
                        if n == NS - 1:
                            if more:
                                split_query(rnd + 1, 1)
                            normalise(rnd, n)
                        for kind, k in works(shape_of(rnd), n):
                            if kind in work:
                                work[kind](rnd, rnd + pair_of(kind, k), k)

                for kind, k in works(-1):
                    if kind in work:
                        work[kind](-1, 0, k)
                for e in range(2):
                    split_query(0, e)
                steps(0)
                with dve.Fori(1, PAIRS - 1) as rnd:
                    steps(rnd)
                steps(PAIRS - 1)
                for kind, k in works(PAIRS):
                    if kind in work:
                        work[kind](PAIRS, PAIRS - 1, k)

            @block.gpsimd
            def _(pool):
                def lower_weights(r):
                    pool.wait_ge(wsplit, 4 * r + 2)
                    pool.tensor_tensor(wa_l[:], wa_f[:], wa_h[:].bitcast(F32), ALU.subtract).then_inc(wsplit, 1)
                    pool.wait_ge(wsplit, 4 * r + 3)
                    pool.tensor_tensor(wb_hl[64:128, :], wb_f[:], wb_hl[0:64, :].bitcast(F32),
                                       ALU.subtract).then_inc(wsplit, 1)

                def queries(rnd, r):
                    for k in range(4):
                        e, h = QUERIES[k]
                        half = slice(h * BANK, (h + 1) * BANK)
                        pool.wait_ge(mb_read[k % 2], reads(rnd, "query", k))
                        pool.tensor_tensor(q_f[e][64:128, half], q_f[e][64:128, half], q_sw[e][64:128, half],
                                           ALU.add).then_inc(qadd, 1)

                lower_weights(0)
                queries(-1, 0)
                lower_weights(1)
                queries(0, 1)
                with pool.Fori(1, PAIRS - 1) as rnd:
                    lower_weights(rnd + 1)
                    queries(rnd, rnd + 1)




class Norm:

    def __init__(self, al, name, n):
        self.n = n
        self.st, self.mv = al.sb(name + "_st", [P, n, 6]), al.sb(name + "_mv", [P, n, 2])
        self.sd, self.rs = al.sb(name + "_sd", [P, n]), al.sb(name + "_rs", [P, n])
        self.st_ok, self.mv_ok, self.ve_ok, self.sd_ok, self.rs_ok, self.x_ok = (
            al.sem(f"{name}_{s}") for s in ("st", "mv", "ve", "sd", "rs", "x"))

    def stats(self, dve, t, x):
        dve.bn_stats(self.st[:, t, :], x).then_inc(self.st_ok, 1)
        dve.wait_ge(self.st_ok, t + 1)
        dve.bn_aggr(self.mv[:, t, :], self.st[:, t, :]).then_inc(self.mv_ok, 1)

    def variance(self, dve, eps=1e-5):
        dve.wait_ge(self.mv_ok, self.n)
        dve.tensor_scalar(self.sd[:], self.mv[:, :, 1], eps, None, ALU.add).then_inc(self.ve_ok, 1)

    def root(self, act):
        act.wait_ge(self.ve_ok, 1)
        act.activation(self.sd[:], self.sd[:], ACT.Sqrt).then_inc(self.sd_ok, 1)

    def inverse(self, dve):
        dve.wait_ge(self.sd_ok, 1)
        dve.reciprocal(self.rs[:], self.sd[:]).then_inc(self.rs_ok, 1)
        dve.wait_ge(self.rs_ok, 1)

    def apply(self, dve, t, x):
        dve.tensor_scalar(x, x, self.mv[:, t, 0:1], self.rs[:, t:t + 1], ALU.subtract, ALU.mult).then_inc(self.x_ok, 1)


RANKS = (8, 16, 32, 64)
MR = RANKS[-1]
NR = len(RANKS)
CLIP = 8.0
HD1 = 16
SCALE1 = HD1 ** -0.5


def stage_route(nc, io, keep):
    with ExitStack() as ctx:
        al = Alloc(nc, ctx)
        w_f, ag_f, b_f = al.sb("c_w", [P, DK, D]), al.sb("c_ag", [MR + NR, D]), al.sb("c_b", [P, DK, MR])
        bias, gate_b = al.sb("c_bias", [P, D]), al.sb("c_gate_b", [P, NR])
        wT_h, wT_l = al.sb("wT_h", [P, DK, D], F32R), al.sb("wT_l", [P, DK, D], F32R)
        agT_h, agT_l = al.sb("agT_h", [P, DK, MR + NR], F32R), al.sb("agT_l", [P, DK, MR + NR], F32R)
        bT_h, bT_l = al.sb("bT_h", [MR, DK, P], F32R), al.sb("bT_l", [MR, DK, P], F32R)
        xT_h, xT_l = al.sb("x1T_h", [P, DK, S], F32R), al.sb("x1T_l", [P, DK, S], F32R)
        ag = al.sb("ag", [P, ST, MR + NR])
        top, less, gate = al.sb("top", [P, ST]), al.sb("less", [P, ST, NR]), al.sb("gate", [P, ST, NR])
        loT_h, loT_l = al.sb("loT_h", [MR, ST, P], F32R), al.sb("loT_l", [MR, ST, P], F32R)
        tr = [al.ps(f"c_tr{i}", [P, DK, P]) for i in range(2)]
        pag = [al.ps(f"c_ag{i}", [P, 4, MR + NR]) for i in range(2)]
        po = [al.ps(f"c_po{i}", [P, D]) for i in range(4)]
        n1, n2 = Norm(al, "n1", ST), Norm(al, "n2", ST)
        names = "w_in b_in tr_ps tr_h tr_l ag_ps ag_ev route biased out_ps out_ev"
        w_in, b_in, tr_ps, tr_h, tr_l, ag_ps, ag_ev, route, biased, out_ps, out_ev = (
            al.sem("c_" + n) for n in names.split())

        jobs = [([w_f[:, t, k * P:(k + 1) * P] for k in range(DK)], (wT_h, wT_l), slice(t * P, (t + 1) * P)) for t in range(DK)]
        jobs += [([ag_f[:, k * P:(k + 1) * P] for k in range(DK)], (agT_h, agT_l), slice(0, MR + NR))]
        jobs += [([b_f[:, t, :] for t in range(DK)], (bT_h, bT_l), slice(0, P))]
        JX = len(jobs)
        jobs += [([keep.x[:, j, k * P:(k + 1) * P] for k in range(DK)], (xT_h, xT_l), slice(j * P, (j + 1) * P)) for j in range(ST)]
        JL = len(jobs)
        jobs += [([ag[:, 4 * n + t, 0:MR] for t in range(4)], (loT_h[:, 4 * n:4 * n + 4], loT_l[:, 4 * n:4 * n + 4]),
                  slice(0, P)) for n in range(2)]

        def shape(n):
            src, dst, cols = jobs[n]
            return src[0].shape[0], src[0].shape[1]

        with nc.Block() as block:

            @block.sync
            def _(sp):
                sp.dma_start(w_f[:], io["L0_ffn_W"].rearrange("(t p) n -> p t n", p=P)).then_inc(w_in, 16)
                sp.dma_start(ag_f[0:MR, :], io["L0_ffn_A"]).then_inc(w_in, 16)
                sp.dma_start(ag_f[MR:MR + NR, :], io["L0_ffn_gate_w"]).then_inc(w_in, 16)
                sp.dma_start(b_f[:], io["L0_ffn_B"].rearrange("(t p) n -> p t n", p=P)).then_inc(w_in, 16)
                sp.dma_start(bias[:], io["L0_ffn_b"].partition_broadcast(P)).then_inc(b_in, 16)
                sp.dma_start(gate_b[:], io["L0_ffn_gate_b"].partition_broadcast(P)).then_inc(b_in, 16)
                sp.dma_start(keep.wqkv, io["L1_attn_w_qkv"].rearrange("(t p) n -> p t n", p=P)).then_inc(keep.wqkv_in, 16)
                for n, name in enumerate(("q_ln_w", "q_ln_b", "k_ln_w", "k_ln_b")):
                    sp.dma_start(keep.qk_ln[:, n, :], io["L1_attn_" + name].partition_broadcast(P)).then_inc(keep.ln_in, 16)

            @block.tensor
            def _(pe):
                def turn(n):
                    rows, cols = shape(n)
                    if n >= 2:
                        pe.wait_ge(tr_l, n - 1)
                    for b, src in enumerate(jobs[n][0]):
                        last = pe.transpose(tr[n % 2][0:cols, b, 0:rows], src, keep.ident[0:rows, 0:rows])
                    last.then_inc(tr_ps, 1)

                pe.wait_ge(w_in, 64)
                for n in range(JX):
                    turn(n)
                for j in range(ST):
                    pe.wait_ge(n1.x_ok, j + 1)
                    turn(JX + j)
                for n in range(2):
                    pe.wait_ge(tr_l, JX + 4 * n + 4)
                    for t in range(4):
                        cols = slice((4 * n + t) * P, (4 * n + t + 1) * P)
                        terms = []
                        for k in range(DK):
                            terms += [(xT_h[:, k, cols], agT_h[:, k, :]), (xT_l[:, k, cols], agT_h[:, k, :]),
                                      (xT_h[:, k, cols], agT_l[:, k, :])]
                        last = three(pe, pag[n][:, t, :], terms)
                    last.then_inc(ag_ps, 1)

                def ffn(j, start):
                    cols = slice(j * P, (j + 1) * P)
                    if start:
                        if j >= 4:
                            pe.wait_ge(out_ev, j - 3)
                        terms = []
                        for k in range(DK):
                            terms += [(xT_h[:, k, cols], wT_h[:, k, :]), (xT_l[:, k, cols], wT_h[:, k, :]),
                                      (xT_h[:, k, cols], wT_l[:, k, :])]
                        three(pe, po[j % 4][:], terms, stop=False)
                    else:
                        bh, bl = (b[:].rearrange("r t n -> r (t n)") for b in (bT_h, bT_l))
                        three(pe, po[j % 4][:], [(loT_h[:, j, :], bh), (loT_l[:, j, :], bh), (loT_h[:, j, :], bl)],
                              start=False).then_inc(out_ps, 1)

                for j in range(4):
                    ffn(j, True)
                pe.wait_ge(route, 2 + NR - 1 + 3)
                for n in range(2):
                    turn(JL + n)
                pe.wait_ge(tr_l, JL + 2)
                for j in range(4):
                    ffn(j, False)
                for j in range(4, ST):
                    ffn(j, True)
                    ffn(j, False)

            @block.scalar
            def _(act):
                def split(n):
                    rows, cols = shape(n)
                    act.wait_ge(tr_ps, n + 1)
                    dst = jobs[n][1][0]
                    act.copy(dst[:, :, jobs[n][2]], tr[n % 2][0:cols, :, 0:rows]).then_inc(tr_h, 1)

                for n in range(JX):
                    split(n)
                n1.root(act)
                for n in range(JX, JL):
                    split(n)
                for n in range(2):
                    act.wait_ge(ag_ps, n + 1)
                    act.copy(ag[:, 4 * n:4 * n + 4, :], pag[n][:]).then_inc(ag_ev, 1)
                for n in range(JL, JL + 2):
                    split(n)
                n2.root(act)

            @block.vector
            def _(dve):
                def split(n):
                    rows, cols = shape(n)
                    dst_h, dst_l = jobs[n][1]
                    dve.wait_ge(tr_h, n + 1)
                    dve.tensor_tensor(dst_l[:, :, jobs[n][2]], tr[n % 2][0:cols, :, 0:rows],
                                      dst_h[:, :, jobs[n][2]].bitcast(F32), ALU.subtract).then_inc(tr_l, 1)

                for j in range(ST):
                    n1.stats(dve, j, keep.x[:, j, :])
                n1.variance(dve)
                for n in range(JX):
                    split(n)
                n1.inverse(dve)
                for j in range(ST):
                    n1.apply(dve, j, keep.x[:, j, :])
                    if j >= 1:
                        split(JX + j - 1)
                split(JL - 1)
                scores = ag[:, :, MR:MR + NR]
                dve.wait_ge(ag_ev, 2)
                dve.wait_ge(b_in, 32)
                for j in range(ST):
                    last = dve.tensor_tensor(ag[:, j, MR:MR + NR], ag[:, j, MR:MR + NR], gate_b[:], ALU.add)
                last.then_inc(route, 1)
                dve.wait_ge(route, 1)
                dve.tensor_reduce(top[:], scores, AX.X, ALU.max).then_inc(route, 1)
                dve.wait_ge(route, 2)
                dve.tensor_tensor(less[:], scores, top[:].unsqueeze(2).to_broadcast([P, ST, NR]), ALU.is_lt).then_inc(route, 1)
                dve.wait_ge(route, 3)
                for r in range(1, NR - 1):
                    dve.tensor_tensor(less[:, :, r], less[:, :, r], less[:, :, r - 1], ALU.mult).then_inc(route, 1)
                    dve.wait_ge(route, 3 + r)
                for r in range(1, NR):
                    c0, c1 = RANKS[r - 1], RANKS[r]
                    dve.tensor_tensor(ag[:, :, c0:c1], ag[:, :, c0:c1],
                                      less[:, :, r - 1:r].to_broadcast([P, ST, c1 - c0]), ALU.mult).then_inc(route, 1)
                for n in range(JL, JL + 2):
                    split(n)
                for j in range(ST):
                    dve.wait_ge(out_ps, j + 1)
                    dve.wait_ge(biased, j + 1)
                    dve.tensor_tensor(keep.x[:, j, :], po[j % 4][:], keep.x[:, j, :], ALU.add).then_inc(out_ev, 1)
                    dve.wait_ge(out_ev, j + 1)
                    n2.stats(dve, j, keep.x[:, j, :])
                n2.variance(dve)
                n2.inverse(dve)
                for j in range(ST):
                    n2.apply(dve, j, keep.x[:, j, :])

            @block.gpsimd
            def _(pool):
                pool.wait_ge(b_in, 32)
                for j in range(ST):
                    pool.wait_ge(tr_ps, JX + j + 1)
                    pool.tensor_tensor(keep.x[:, j, :], keep.x[:, j, :], bias[:], ALU.add).then_inc(biased, 1)


def stage_qkv(nc, io, keep):
    with ExitStack() as ctx:
        al = Alloc(nc, ctx)
        xT_h, xT_l = al.sb("x2T_h", [P, DK, S], F32R), al.sb("x2T_l", [P, DK, S], F32R)
        NW = 3 * D // P
        wT_h, wT_l = al.sb("wqkvT_h", [P, DK, 3 * D], F32R), al.sb("wqkvT_l", [P, DK, 3 * D], F32R)
        tr = [al.ps(f"d_tr{i}", [P, DK, P]) for i in range(2)]
        po = [al.ps(f"d_po{i}", [P, D]) for i in range(4)]
        nq = Norm(al, "nqk", 2 * ST)
        names = "tr_ps tr_h tr_l out_ps clip scaled_q scaled_k done"
        tr_ps, tr_h, tr_l, out_ps, clip, scaled_q, scaled_k, done = (al.sem("d_" + n) for n in names.split())
        jobs = [([keep.x[:, j, k * P:(k + 1) * P] for k in range(DK)], xT_h, xT_l, slice(j * P, (j + 1) * P)) for j in range(ST)]
        jobs += [([keep.wqkv[:, t, k * P:(k + 1) * P] for k in range(DK)], wT_h, wT_l, slice(t * P, (t + 1) * P)) for t in range(NW)]
        order = [(j, c) for c in range(2) for j in range(ST)] + [(j, 2) for j in range(ST)]
        dest = (keep.q, keep.k, keep.v)

        with nc.Block() as block:

            @block.sync
            def _(sp):
                for dst, src in ((keep.qx, "alibi_q"), (keep.kx, "alibi_k")):
                    sp.dma_start(dst[:, :, :, 0:EX].bitcast(F32), io[src][0]).then_inc(keep.alibi_in, 16)

            @block.tensor
            def _(pe):
                pe.wait_ge(keep.wqkv_in, 16)
                for n, (src, h, l, cols) in enumerate(jobs):
                    if n >= 2:
                        pe.wait_ge(tr_l, n - 1)
                    for k in range(DK):
                        last = pe.transpose(tr[n % 2][:, k, :], src[k], keep.ident[:])
                    last.then_inc(tr_ps, 1)
                for n, (j, c) in enumerate(order):
                    if j == 0:
                        pe.wait_ge(tr_l, ST + 4 * (c + 1))
                    if n >= 4:
                        pe.wait_ge(clip, n - 3)
                    rows, cols = slice(j * P, (j + 1) * P), slice(c * D, (c + 1) * D)
                    terms = []
                    for k in range(DK):
                        terms += [(xT_h[:, k, rows], wT_h[:, k, cols]), (xT_l[:, k, rows], wT_h[:, k, cols]),
                                  (xT_h[:, k, rows], wT_l[:, k, cols])]
                    three(pe, po[n % 4][:], terms).then_inc(out_ps, 1)

            @block.scalar
            def _(act):
                for n, (src, h, l, cols) in enumerate(jobs):
                    act.wait_ge(tr_ps, n + 1)
                    act.copy(h[:, :, cols], tr[n % 2][:]).then_inc(tr_h, 1)
                nq.root(act)

            @block.vector
            def _(dve):
                for n, (src, h, l, cols) in enumerate(jobs):
                    dve.wait_ge(tr_h, n + 1)
                    dve.tensor_tensor(l[:, :, cols], tr[n % 2][:], h[:, :, cols].bitcast(F32), ALU.subtract).then_inc(tr_l, 1)
                for n, (j, c) in enumerate(order):
                    dve.wait_ge(out_ps, n + 1)
                    dve.tensor_scalar(dest[c][:, j, :], po[n % 4][:], CLIP, -CLIP, ALU.min, ALU.max).then_inc(clip, 1)
                    if c < 2:
                        dve.wait_ge(clip, n + 1)
                        nq.stats(dve, n, dest[c][:, j, :])
                    if n == 2 * ST - 1:
                        nq.variance(dve)
                    if c == 2:
                        if j == 0:
                            nq.inverse(dve)
                            dve.wait_ge(keep.ln_in, 64)
                        nq.apply(dve, ST + j, keep.k[:, j, :])
                        nq.apply(dve, j, keep.q[:, j, :])
                        dve.wait_ge(nq.x_ok, 2 * j + 2)
                        dve.scalar_tensor_tensor(out=keep.q[:, j, :], in0=keep.q[:, j, :], scalar=SCALE1,
                                                 in1=keep.qk_ln[:, 0, :], op0=ALU.mult, op1=ALU.mult).then_inc(scaled_q, 1)
                        dve.wait_ge(scaled_q, j + 1)
                        dve.scalar_tensor_tensor(out=keep.q[:, j, :], in0=keep.qk_ln[:, 1, :], scalar=SCALE1,
                                                 in1=keep.q[:, j, :], op0=ALU.mult, op1=ALU.add).then_inc(done, 1)

            @block.gpsimd
            def _(pool):
                pool.wait_ge(keep.ln_in, 64)
                for j in range(ST):
                    pool.wait_ge(nq.x_ok, 2 * j + 1)
                    pool.tensor_tensor(keep.k[:, j, :], keep.k[:, j, :], keep.qk_ln[:, 2, :], ALU.mult).then_inc(scaled_k, 1)
                    pool.wait_ge(scaled_k, j + 1)
                    pool.tensor_tensor(keep.k[:, j, :], keep.k[:, j, :], keep.qk_ln[:, 3, :], ALU.add).then_inc(done, 1)




H1 = 32
HG = 4
GROUPS = H1 // HG
EX = 16


def alibi_columns():
    m = np.arange(1, H1 + 1, dtype=np.float32) * np.float32(8.0 / H1)
    slope = np.float32(1.0) / np.power(np.float32(2.0), m)
    bits = slope.view(np.uint32)
    slope_h = ((bits + np.uint32(0x800)) & np.uint32(0xFFFFF000)).view(np.float32)
    slope_l = slope - slope_h
    q, k = (np.zeros((GROUPS, P, ST, HG, EX), np.float32) for _ in range(2))
    pos = (np.arange(ST)[None, :] * P + np.arange(P)[:, None]).astype(np.float32)[None, :, :, None]
    sh, sl = (x.reshape(GROUPS, 1, 1, HG) for x in (slope_h, slope_l))
    k[..., 0] = k[..., 1] = 1.0
    q[..., 2], q[..., 3], q[..., 4], q[..., 5] = sh, sl, -pos, -pos
    k[..., 2], k[..., 3], k[..., 4], k[..., 5] = pos, pos, sh, sl
    return q, k


CHUNKS = [(j, half) for half in range(2) for j in range(4 * (half + 1))]
M_STEPS = HG * ST
E_STEPS = HG * len(CHUNKS)


def m_step(n):
    return n % HG, ST - 1 - n // HG


def chunk_cols(c):
    j, half = CHUNKS[c]
    first = max(j * P, half * BANK)
    return first, (half + 1) * BANK - first


def alibi_order(with_m):
    order, m, m_cols, e_cols = [], 0, 0, 0
    for c in range(len(CHUNKS)):
        for h in range(HG):
            while with_m and m < M_STEPS and m_cols <= e_cols:
                order.append(("m", m))
                m_cols += (m_step(m)[1] + 1) * P
                m += 1
            order.append(("e", HG * c + h))
            e_cols += chunk_cols(c)[1]
        if c >= 1:
            order.append(("pv", c - 1))
    order += [("m", n) for n in range(m, M_STEPS if with_m else 0)]
    return order + [("pv", len(CHUNKS) - 1)]


def stage_alibi(nc, io, keep):
    with ExitStack() as ctx:
        al = Alloc(nc, ctx)
        qx, kx, x_in = keep.qx, keep.kx, keep.alibi_in
        qT = [al.sb(f"qT{u}", [P, 2, S], F32R) for u in range(2)]
        kT = [al.sb(f"kT{u}", [P, HG, S], F32R) for u in range(2)]
        vx = [al.sb(f"vx{u}", [P, ST, HG, 32]) for u in range(2)]
        RING = 3
        probs = [al.sb(f"l1_probs{i}", [P, HG, BANK]) for i in range(RING)]
        nmax, nmax_h = al.sb("nmax", [P, HG, ST]), al.sb("nmax_h", [P, HG, ST], F32R)
        nmax_hl = al.sb("nmax_hl", [P, 2, HG, 2, ST])
        mT = al.sb("mT", [HG * 2 * ST, P], F32R)
        oT = al.sb("oT", [P, S])
        rsum = al.sb("rsum", [P, ST, HG])
        sm = [al.ps(f"l1_sm{i}", [P, S]) for i in range(2)]
        SLOTS = 3
        banks = al.ps("l1_banks", [P, SLOTS + 1, BANK])
        pv = banks[:, SLOTS, :]
        turn_k, turn_q = (banks[:, 2 * n:2 * n + 2, :].rearrange("p b c -> p (b c)") for n in range(2))
        names = ("ones zeros zeros0 built vx_ok t_ps qT_ok kT_ok scores maxed nmaxh split rows_ps rows_in sE exped pv_ps oT_ok "
                 "back recip tr_free")
        (ones, zeros, zeros0, built, vx_ok, t_ps, qT_ok, kT_ok, scores, maxed, nmaxh_ok, split, rows_ps, rows_in, sE, exped, pv_ps,
         oT_ok, back_ps, recip, tr_free) = (al.sem("e_" + n) for n in names.split())
        NC, LAST = len(CHUNKS), GROUPS - 1
        BUILT = 7
        ROWS = 16 * 2 * HG
        first_half = 4

        def cols(w, g, j=slice(None)):
            return w[:, j, bass.ds(g * (HG * HD1), HG * HD1)].rearrange("p j (h c) -> p j h c", h=HG)

        def rows(h):
            return slice(64 * (h % 2), 64 * (h % 2) + 64)

        def phases(eng, phase):
            with eng.Fori(0, (GROUPS - 2) // 2) as i:
                for u in range(2):
                    phase(i * 2 + u, u, True, True)
            phase(LAST - 1, 0, True, False)
            phase(LAST, 1, False, False)

        with nc.Block() as block:

            @block.sync
            def _(sp):
                def load(g):
                    for dst, src in ((qx, "alibi_q"), (kx, "alibi_k")):
                        sp.dma_start(dst[:, :, :, 0:EX].bitcast(F32), io[src][g]).then_inc(x_in, 16)

                def maxima(g, u, first=False):
                    sp.wait_ge(tr_free, 1 if first else 2 * g)
                    for h in range(HG):
                        for c in range(2):
                            src = (2 * h + c) * ST
                            sp.dma_start(qT[u][64 * (h % 2) + c:64 * (h % 2) + c + 1, h // 2, :].bitcast(F32),
                                         mT[src:src + ST, :].bitcast(F32)).then_inc(rows_in, 16)

                def phase(g, u, more):
                    maxima(g + 1, 1 - u)
                    if more:
                        sp.wait_ge(t_ps, 4 * g + 12)
                        load(g + 3)

                prefetch_gated(sp, io, keep)
                sp.wait_ge(t_ps, 4)
                load(1)
                maxima(0, 0, first=True)
                sp.wait_ge(t_ps, 8)
                load(2)
                with sp.Fori(0, 2) as i:
                    for u in range(2):
                        phase(i * 2 + u, u, True)
                for g in range(4, LAST):
                    phase(g, g % 2, g + 3 <= LAST)

            @block.tensor
            def _(pe):
                def build(g, u, first=False):
                    pe.wait_ge(x_in, 32 * g + 32)
                    pe.wait_ge(built, BUILT * g + BUILT)
                    for b, dsts in enumerate(((sm[0], sm[1]), (turn_k, turn_q))):
                        for src, dst in zip((kx, qx), dsts):
                            if dst is turn_k and not first:
                                pe.wait_ge(tr_free, 2 * g - 2 if not (isinstance(g, int) and g == 1) else 1)
                            if dst is turn_q and not first and not (isinstance(g, int) and g == 1):
                                pe.wait_ge(oT_ok, 2 * g - 2)
                            for j in range(ST):
                                last = pe.transpose(dst[:, j * P:(j + 1) * P],
                                                    src[:, j, 2 * b:2 * b + 2, :].rearrange("p h c -> p (h c)").bitcast(F32),
                                                    keep.ident[:])
                            last.then_inc(t_ps, 1)

                def m(g, u, n):
                    h, i = m_step(n)
                    if n < 2:
                        pe.wait_ge(kT_ok, 4 * g + 4)
                        pe.wait_ge(qT_ok, 2 * g + 2)
                    else:
                        pe.wait_ge(maxed, M_STEPS * g + n - 1)
                    width = (i + 1) * P
                    for c0 in range(0, width, BANK):
                        c1 = min(width, c0 + BANK)
                        pe.matmul(sm[n % 2][:, c0:c1], qT[u][:, h // 2, i * P:(i + 1) * P], kT[u][:, h, c0:c1],
                                  start=True, stop=c1 < width)
                    pe.matmul(sm[n % 2][:, width - P:width], keep.ident_b[:], keep.mask[:],
                              start=False, stop=True).then_inc(scores, 1)

                def maxima(g):
                    pe.wait_ge(split, g + 1)
                    pe.transpose(banks[:, 0, 0:P], nmax_hl[:].rearrange("p z h c i -> p (z h c i)"),
                                 keep.ident[:]).then_inc(rows_ps, 1)

                def e(g, u, n):
                    c, h = n // HG, n % HG
                    j, half = CHUNKS[c]
                    q0, w = chunk_cols(c)
                    if n == 0:
                        pe.wait_ge(rows_in, ROWS * g + ROWS)
                    if n == 2:
                        pe.wait_ge(tr_free, 2 * g + 1)
                    if n >= SLOTS:
                        pe.wait_ge(exped, E_STEPS * g + n + 1 - SLOTS)
                    diagonal = q0 == j * P
                    last = pe.matmul(banks[:, n % SLOTS, 0:w], kT[u][:, h, j * P:(j + 1) * P], qT[u][:, h // 2, q0:q0 + w],
                                     start=True, stop=not diagonal)
                    if diagonal:
                        last = pe.matmul(banks[:, n % SLOTS, 0:P], keep.ident_b[:], keep.mask_t[:], start=False, stop=True)
                    last.then_inc(sE, 1)

                def values(g, u, c):
                    j, half = CHUNKS[c]
                    q0, w = chunk_cols(c)
                    pe.wait_ge(exped, E_STEPS * g + HG * (c + 1))
                    if c == 0:
                        pe.wait_ge(vx_ok, g + 1)
                    if c == first_half:
                        pe.wait_ge(oT_ok, 2 * g + 1)
                    for h in range(HG):
                        last = pe.matmul(pv[32 * h:32 * h + 32, q0 - half * BANK:q0 - half * BANK + w], vx[u][:, j, h, :],
                                         probs[c % RING][:, h, 0:w], start=(j == 0), stop=(j == 4 * half + 3))
                    last.then_inc(pv_ps, 1)

                def back(g):
                    for j in range(ST):
                        last = pe.transpose(turn_q[:, j * P:(j + 1) * P], oT[:, j * P:(j + 1) * P], keep.ident[:])
                    last.then_inc(back_ps, 1)

                def phase(g, u, with_m, with_build):
                    for kind, n in alibi_order(with_m):
                        if kind == "m":
                            m(g + 1, 1 - u, n)
                        elif kind == "e":
                            e(g, u, n)
                        else:
                            values(g, u, n)
                    if with_m:
                        maxima(g + 1)
                    if with_build:
                        pe.wait_ge(maxed, M_STEPS * (g + 2))
                        build(g + 2, u)
                        pe.wait_ge(qT_ok, 2 * g + 6)
                    else:
                        pe.wait_ge(oT_ok, 2 * g + 2)
                    back(g)

                build(0, 0, first=True)
                for n in range(M_STEPS):
                    m(0, 0, n)
                maxima(0)
                pe.wait_ge(maxed, M_STEPS)
                build(1, 1)
                phases(pe, phase)

            @block.scalar
            def _(act):
                def turned(g, u):
                    for b, src in enumerate((sm[1], turn_q)):
                        act.wait_ge(t_ps, 4 * g + 2 * b + 2)
                        act.copy(qT[u][:, b, :], src[:]).then_inc(qT_ok, 1)
                    act.copy(kT[u][rows(3), 3, :], turn_k[rows(3), :]).then_inc(kT_ok, 1)

                def out(g, half):
                    act.wait_ge(pv_ps, NC * g + (NC if half else first_half))
                    act.copy(oT[:, half * BANK:(half + 1) * BANK], pv).then_inc(oT_ok, 1)

                def phase(g, u, with_m, with_build):
                    for n in range(E_STEPS):
                        c, h = n // HG, n % HG
                        act.wait_ge(sE, E_STEPS * g + n + 1)
                        if h == 0 and c >= RING:
                            act.wait_ge(pv_ps, NC * g + c - RING + 1)
                        w = chunk_cols(c)[1]
                        act.activation(probs[c % RING][:, h, 0:w], banks[:, n % SLOTS, 0:w], ACT.Exp).then_inc(exped, 1)
                        if c == first_half + 1 and h == 0:
                            out(g, 0)
                    out(g, 1)
                    if with_build:
                        turned(g + 2, u)

                act.wait_ge(zeros0, 1)
                turned(0, 0)
                act.wait_ge(zeros, 2)
                turned(1, 1)
                phases(act, phase)

            @block.vector
            def _(dve):
                def turned(g, u):
                    for h, src in enumerate((sm[0], sm[0], turn_k)):
                        dve.wait_ge(t_ps, 4 * g + 2 * (h // 2) + 1)
                        dve.tensor_copy(kT[u][rows(h), h, :], src[rows(h), :]).then_inc(kT_ok, 1)

                def m(g, n):
                    h, i = m_step(n)
                    dve.wait_ge(scores, M_STEPS * g + n + 1)
                    dve.tensor_reduce(nmax[:, h, i:i + 1], sm[n % 2][:, 0:(i + 1) * P], AX.X, ALU.max,
                                      negate=True).then_inc(maxed, 1)

                def maxima(g, first=False):
                    dve.wait_ge(maxed, M_STEPS * (g + 1))
                    dve.tensor_copy(nmax_h[:], nmax[:]).then_inc(nmaxh_ok, 1)
                    dve.wait_ge(nmaxh_ok, g + 1)
                    dve.tensor_copy(nmax_hl[:, 0, :, 0, :], nmax_h[:].bitcast(F32))
                    dve.tensor_tensor(nmax_hl[:, 0, :, 1, :], nmax[:], nmax_h[:].bitcast(F32), ALU.subtract).then_inc(split, 1)
                    if not first:
                        dve.wait_ge(rows_in, ROWS * g)
                    dve.wait_ge(rows_ps, g + 1)
                    dve.tensor_copy(mT[:], banks[0:HG * 2 * ST, 0, 0:P]).then_inc(tr_free, 1)

                def normalise(g):
                    dve.wait_ge(back_ps, g + 1)
                    byhead = turn_q.rearrange("p (j h c) -> p j h c", j=ST, h=HG)
                    dve.reciprocal(rsum[:], byhead[:, :, :, HD1]).then_inc(recip, 1)
                    dve.wait_ge(recip, g + 1)
                    dve.tensor_tensor(cols(keep.attn, g), byhead[:, :, :, 0:HD1],
                                      rsum[:].unsqueeze(3).to_broadcast([P, ST, HG, HD1]), ALU.mult).then_inc(tr_free, 1)

                def phase(g, u, with_m, with_build):
                    if with_m:
                        for n in range(M_STEPS):
                            m(g + 1, n)
                        maxima(g + 1)
                    if with_build:
                        turned(g + 2, u)
                    normalise(g)

                dve.tensor_copy(qx[:, :, :, 32:48], cols(keep.q, 0)).then_inc(built, 1)
                dve.tensor_copy(kx[:, :, :, 48:64], cols(keep.k, 0)).then_inc(built, 1)
                dve.tensor_copy(qx[:, :, :, 16:32], cols(keep.q, 0)).then_inc(built, 1)
                for j in (slice(4, 8), slice(0, 4)):
                    dve.tensor_copy(kx[:, j, :, 16:32], cols(keep.k, 0, j)).then_inc(built, 1)
                dve.wait_ge(built, 2)
                dve.tensor_tensor(qx[:, :, :, 48:64], cols(keep.q, 0), qx[:, :, :, 32:48].bitcast(F32),
                                  ALU.subtract).then_inc(built, 1)
                dve.tensor_tensor(kx[:, :, :, 32:48], cols(keep.k, 0), kx[:, :, :, 48:64].bitcast(F32),
                                  ALU.subtract).then_inc(built, 1)
                dve.memset(kT[0][:].bitcast(F32), 0.0).then_inc(zeros0, 1)
                dve.wait_ge(zeros0, 1)
                turned(0, 0)
                for n in range(M_STEPS):
                    m(0, n)
                dve.wait_ge(zeros, 2)
                maxima(0, first=True)
                turned(1, 1)
                phases(dve, phase)

            @block.gpsimd
            def _(pool):
                def group(g, u):
                    pool.tensor_copy(qx[:, :, :, 32:48], cols(keep.q, g)).then_inc(built, 1)
                    pool.tensor_copy(kx[:, :, :, 48:64], cols(keep.k, g)).then_inc(built, 1)
                    pool.tensor_copy(qx[:, :, :, 16:32], cols(keep.q, g)).then_inc(built, 1)
                    pool.wait_ge(built, BUILT * g + 2)
                    for j in (slice(4, 8), slice(0, 4)):
                        pool.tensor_copy(kx[:, j, :, 16:32], cols(keep.k, g, j)).then_inc(built, 1)
                    pool.tensor_tensor(qx[:, :, :, 48:64], cols(keep.q, g), qx[:, :, :, 32:48].bitcast(F32),
                                       ALU.subtract).then_inc(built, 1)
                    pool.tensor_tensor(kx[:, :, :, 32:48], cols(keep.k, g), kx[:, :, :, 48:64].bitcast(F32),
                                       ALU.subtract).then_inc(built, 1)

                def values(g, u):
                    pool.tensor_copy(vx[u][:, :, :, 0:HD1], cols(keep.v, g)).then_inc(vx_ok, 1)

                pool.memset(kT[1][:].bitcast(F32), 0.0).then_inc(zeros, 1)
                pool.memset(nmax_hl[:], 0.0).then_inc(zeros, 1)
                for u in range(2):
                    pool.memset(vx[u][:], 0.0).then_inc(ones, 1)
                    pool.wait_ge(ones, 2 * u + 1)
                    pool.memset(vx[u][:, :, :, HD1:HD1 + 1], 1.0).then_inc(ones, 1)
                    pool.wait_ge(ones, 2 * u + 2)
                    values(u, u)
                pool.wait_ge(t_ps, 4)
                group(1, 1)
                with pool.Fori(1, GROUPS // 2) as i:
                    for u in range(2):
                        g = i * 2 + u
                        pool.wait_ge(t_ps, 4 * g)
                        group(g, u)
                        pool.wait_ge(pv_ps, NC * (g - 1))
                        values(g, u)




IM = 1792
IT = IM // P


EARLY = (0, 1, IT - 1)


def gated_weight(keep, t, c):
    if isinstance(t, int):
        return keep.gated_early[:, EARLY.index(t), c, :] if t in EARLY else keep.gated_late[:, t - 2, c, :]
    return keep.gated_late[:, bass.ds(t - 2, 1), c, :].rearrange("p o c -> p (o c)")


def gated_load(t):
    return 0 if t in EARLY else min(t // 2, (IT - len(EARLY)) // 2)


def load_gated(sp, io, keep, t):
    r = slice(t * P, (t + 1) * P)
    sp.dma_start(gated_weight(keep, t, 0), io["L1_ffn_gate_w"][r, :]).then_inc(keep.gated_in[gated_load(t)], 16)
    sp.dma_start(gated_weight(keep, t, 1), io["L1_ffn_up_w"][r, :]).then_inc(keep.gated_in[gated_load(t)], 16)
    sp.dma_start(gated_weight(keep, t, 2).rearrange("p (k c) -> p k c", k=DK),
                 io["L1_ffn_down_w"][:, r].rearrange("(k p) c -> p k c", p=P)).then_inc(keep.gated_in[gated_load(t)], 16)


def prefetch_gated(sp, io, keep):
    sp.dma_start(keep.wo_f[:], io["L1_attn_w_out"].rearrange("(t p) n -> p t n", p=P)).then_inc(keep.wo_in, 16)
    for t in EARLY:
        load_gated(sp, io, keep, t)


def stage_gated(nc, io, keep, upto=9):
    with ExitStack() as ctx:
        al = Alloc(nc, ctx)
        xT_h, xT_l = al.sb("x3T_h", [P, DK, S], F32R), al.sb("x3T_l", [P, DK, S], F32R)
        keep.gated_late = al.sb("gated_late", [P, IT - len(EARLY), 3, D])
        lnw = al.sb("lnw", [P, D])
        HT = ST // 2
        n3 = [Norm(al, f"n3{half}", HT) for half in "ab"]
        rms, rms_inv = ([al.sb(f"{n}{half}", [P, HT]) for half in "ab"] for n in ("rms", "rms_inv"))
        n4 = Norm(al, "n4", ST)
        names = "ln_in tr_ps tr_h tr_l wt_ps out_ps out_ev nx"
        ln_in, tr_ps, tr_h, tr_l, wt_ps, out_ps, out_ev, nx = (al.sem("g_" + n) for n in names.split())
        wt_read = [al.sem(f"g_wt_read{i}") for i in range(2)]
        ms_ok, root_ok, rinv_ok = (al.sem("g_" + n) for n in ("ms", "root", "rinv"))

        with ExitStack() as c1:
            a1 = Alloc(nc, c1)
            woT_h, woT_l = a1.sb("woT_h", [P, DK, D], F32R), a1.sb("woT_l", [P, DK, D], F32R)
            tr = [a1.ps(f"g_tr{i}", [P, DK, P]) for i in range(4)]
            po = [a1.ps(f"g_po{i}", [P, D]) for i in range(4)]
            jobs = [([keep.wo_f[:, t, k * P:(k + 1) * P] for k in range(DK)], woT_h, woT_l, slice(t * P, (t + 1) * P))
                    for t in range(DK)]
            jobs += [([keep.attn[:, j, k * P:(k + 1) * P] for k in range(DK)], xT_h, xT_l, slice(j * P, (j + 1) * P)) for j in range(ST)]
            JX = len(jobs)
            jobs += [([keep.attn[:, j, k * P:(k + 1) * P] for k in range(DK)], xT_h, xT_l, slice(j * P, (j + 1) * P)) for j in range(ST)]
            wjobs = [(t, c) for t in list(EARLY) + [t for t in range(IT) if t not in EARLY] for c in range(3)]
            BESIDE = 3 * ST

            def weight_dst(m):
                return gated_weight(keep, *wjobs[m])

            with nc.Block() as block:

                @block.sync
                def _(sp):
                    sp.dma_start(lnw[:], io["L1_ffn_ln_w"].partition_broadcast(P)).then_inc(ln_in, 16)
                    for t in range(IT):
                        if t not in EARLY:
                            load_gated(sp, io, keep, t)

                @block.tensor
                def _(pe):
                    def turn(n):
                        if n >= 2:
                            pe.wait_ge(tr_l, n - 1)
                        for k, src in enumerate(jobs[n][0]):
                            last = pe.transpose(tr[n % 2][:, k, :], src, keep.ident[:])
                        last.then_inc(tr_ps, 1)

                    def turn_weight(m):
                        t, c = wjobs[m]
                        if c == 0:
                            load = gated_load(t)
                            pe.wait_ge(keep.gated_in[load], 48 * sum(gated_load(x) == load for x in range(IT)))
                        if m >= 2:
                            pe.wait_ge(wt_read[m % 2], m // 2)
                        for k in range(DK):
                            last = pe.transpose(tr[2 + m % 2][:, k, :], gated_weight(keep, t, c)[:, k * P:(k + 1) * P], keep.ident[:])
                        last.then_inc(wt_ps, 1)

                    pe.wait_ge(keep.wo_in, 16)
                    for n in range(JX):
                        turn(n)
                    for j in range(ST):
                        pe.wait_ge(tr_l, DK + j + 1)
                        if j >= 4:
                            pe.wait_ge(out_ev, j - 3)
                        rows = slice(j * P, (j + 1) * P)
                        terms = []
                        for k in range(DK):
                            terms += [(xT_h[:, k, rows], woT_h[:, k, :]), (xT_l[:, k, rows], woT_h[:, k, :]),
                                      (xT_h[:, k, rows], woT_l[:, k, :])]
                        three(pe, po[j % 4][:], terms).then_inc(out_ps, 1)
                        for m in range(3 * j, 3 * j + 3):
                            turn_weight(m)
                    for j in range(HT):
                        pe.wait_ge(nx, j + 1)
                        turn(JX + j)
                    for m in range(BESIDE, len(wjobs)):
                        turn_weight(m)
                    for j in range(HT, ST):
                        pe.wait_ge(nx, j + 1)
                        turn(JX + j)

                @block.scalar
                def _(act):
                    def split(n):
                        act.wait_ge(tr_ps, n + 1)
                        act.copy(jobs[n][1][:, :, jobs[n][3]], tr[n % 2][:]).then_inc(tr_h, 1)

                    def weight(m):
                        act.wait_ge(wt_ps, m + 1)
                        act.copy(weight_dst(m), tr[2 + m % 2][:].rearrange("p k c -> p (k c)")).then_inc(wt_read[m % 2], 1)

                    def rms_root(half):
                        act.wait_ge(ms_ok, 3 * half + 3)
                        act.activation(rms[half][:], rms[half][:], ACT.Sqrt).then_inc(root_ok, 1)

                    for n in range(JX):
                        split(n)
                    for m in range(0, BESIDE, 2):
                        weight(m)
                        if m == 12:
                            n3[0].root(act)
                        if m == 16:
                            rms_root(0)
                    n3[1].root(act)
                    for n in range(JX, JX + HT):
                        split(n)
                    for m in range(BESIDE, len(wjobs)):
                        weight(m)
                        if m == BESIDE + 8:
                            rms_root(1)
                    for n in range(JX + HT, len(jobs)):
                        split(n)

                @block.vector
                def _(dve):
                    def split(n):
                        dve.wait_ge(tr_h, n + 1)
                        h, l, cols = jobs[n][1:]
                        dve.tensor_tensor(l[:, :, cols], tr[n % 2][:], h[:, :, cols].bitcast(F32), ALU.subtract).then_inc(tr_l, 1)

                    def project(j):
                        dve.wait_ge(out_ps, j + 1)
                        dve.tensor_tensor(keep.x[:, j, :], po[j % 4][:], keep.x[:, j, :], ALU.add).then_inc(out_ev, 1)
                        dve.wait_ge(out_ev, j + 1)
                        n3[j // HT].stats(dve, j % HT, keep.x[:, j, :])

                    def weight(m):
                        dve.wait_ge(wt_ps, m + 1)
                        dve.tensor_copy(weight_dst(m), tr[2 + m % 2][:].rearrange("p k c -> p (k c)")).then_inc(wt_read[m % 2], 1)

                    def norm(half):
                        n3[half].inverse(dve)
                        for t in range(HT):
                            n3[half].apply(dve, t, keep.x[:, HT * half + t, :])
                        var, rs = n3[half].mv[:, :, 1], n3[half].rs[:]
                        dve.tensor_tensor(rms[half][:], var, rs, ALU.mult).then_inc(ms_ok, 1)
                        dve.wait_ge(ms_ok, 3 * half + 1)
                        dve.tensor_tensor(rms[half][:], rms[half][:], rs, ALU.mult).then_inc(ms_ok, 1)
                        dve.wait_ge(ms_ok, 3 * half + 2)
                        dve.tensor_scalar(rms[half][:], rms[half][:], 1e-5, None, ALU.add).then_inc(ms_ok, 1)

                    def scale(half):
                        dve.wait_ge(root_ok, half + 1)
                        dve.reciprocal(rms_inv[half][:], rms[half][:]).then_inc(rinv_ok, 1)
                        dve.wait_ge(rinv_ok, half + 1)
                        dve.wait_ge(n3[half].x_ok, HT)
                        dve.wait_ge(ln_in, 16)
                        for t in range(HT):
                            j = HT * half + t
                            dve.scalar_tensor_tensor(out=keep.attn[:, j, :], in0=keep.x[:, j, :], scalar=rms_inv[half][:, t:t + 1],
                                                     in1=lnw[:], op0=ALU.mult, op1=ALU.mult).then_inc(nx, 1)

                    for n in range(JX):
                        split(n)
                    for j in range(ST):
                        project(j)
                        if j == HT - 1:
                            n3[0].variance(dve)
                        for m in range(3 * j, 3 * j + 3):
                            if m % 2 == 1:
                                weight(m)
                        if j == HT:
                            norm(0)
                        if j == HT + 1:
                            scale(0)
                    n3[1].variance(dve)
                    for n in range(JX, JX + HT):
                        split(n)
                    norm(1)
                    scale(1)
                    for n in range(JX + HT, len(jobs)):
                        split(n)

        if upto == 3:
            return
        names = "guh gul dh dl gu ex den rec sil a_f a_h a_l down fin"
        guh, gul, dh, dl, gu, ex_ok, den_ok, rec_ok, sil_ok, af_ok, ah_ok, al_ok, down, fin = (al.sem("h_" + n) for n in names.split())
        w_h, w_l = ([[al.sb(f"{n}_{part}{i}", [P, D], F32R) for n in "gud"] for i in range(2)] for part in "hl")
        ex, den = al.sb("ex", [P, BANK]), al.sb("den", [P, BANK])
        act_f = al.sb("act_f", [P, BANK])
        a_h = [al.sb(f"a_h{i}", [P, BANK], F32R) for i in range(2)]
        a_l = [al.sb(f"a_l{i}", [P, BANK], F32R) for i in range(2)]
        pg, pu = ([al.ps(f"h_{n}{i}", [P, BANK]) for i in range(2)] for n in "gu")
        pd = [al.ps(f"h_d{i}", [P, D]) for i in range(4)]
        STEPS = 2 * IT

        with nc.Block() as block:

            def each(eng, step):
                for half in range(2):
                    base = half * IT
                    for t in range(2):
                        step(half, base + t, t, t)
                    with eng.Fori(1, IT // 2 - 1) as i:
                        for u in range(2):
                            step(half, i * 2 + (base + u), i * 2 + u, u)
                    for t in range(IT - 2, IT):
                        step(half, base + t, t, t % 2)

            def tile(t, c):
                return gated_weight(keep, t % IT if isinstance(t, int) else t, c)

            def last_step(n):
                return isinstance(n, int) and n == STEPS - 1

            @block.tensor
            def _(pe):
                def down_part(n, u, first, last):
                    pe.wait_ge(dh, n + 1)
                    pe.wait_ge(dl, n + 1)
                    pe.wait_ge(ah_ok, n + 1)
                    pe.wait_ge(al_ok, n + 1)
                    for j in range(4):
                        rows = slice(j * P, (j + 1) * P)
                        end = three(pe, pd[j][:], [(a_h[u][:, rows], w_h[u][2][:]), (a_l[u][:, rows], w_h[u][2][:]),
                                                   (a_h[u][:, rows], w_l[u][2][:])], start=first, stop=last)
                    end.then_inc(down, 1)

                def step(half, n, t, u):
                    cols = slice(half * BANK, (half + 1) * BANK)
                    pe.wait_ge(guh, 2 * n + 2)
                    pe.wait_ge(gul, 2 * n + 2)
                    if not (isinstance(n, int) and n < 2):
                        pe.wait_ge(af_ok, n - 1)
                    for c, dst in ((0, pg[u]), (1, pu[u])):
                        terms = []
                        for k in range(DK):
                            b = slice(k * P, (k + 1) * P)
                            h, l = w_h[u][c][:, b], w_l[u][c][:, b]
                            terms += [(h, xT_h[:, k, cols]), (h, xT_l[:, k, cols]), (l, xT_h[:, k, cols])]
                        three(pe, dst[:], terms).then_inc(gu, 1)
                    if isinstance(n, int) and n == 0:
                        return
                    if isinstance(n, int) and n == IT + 1:
                        pe.wait_ge(fin, 4)
                    before = t - 1 if isinstance(t, int) else None
                    down_part(n - 1, 1 - u, before == 0, before == -1)

                each(pe, step)
                down_part(STEPS - 1, 1, False, True)

            @block.scalar
            def _(act):
                def upper_gu(n, t, u):
                    for c in range(2):
                        act.copy(w_h[u][c][:], tile(t, c)).then_inc(guh, 1)

                def upper_d(n, t, u):
                    act.copy(w_h[u][2][:], tile(t, 2)).then_inc(dh, 1)

                def step(half, n, t, u):
                    if not last_step(n):
                        if not (isinstance(n, int) and n == 0):
                            act.wait_ge(gu, 2 * n)
                        upper_gu(n + 1, t + 1, 1 - u)
                    act.wait_ge(gu, 2 * n + 1)
                    if not (isinstance(n, int) and n == 0):
                        act.wait_ge(den_ok, n)
                    act.activation(ex[:], pg[u][:], ACT.Exp, scale=-1.0).then_inc(ex_ok, 1)
                    act.wait_ge(af_ok, n + 1)
                    act.copy(a_h[u][:], act_f[:]).then_inc(ah_ok, 1)
                    if not last_step(n):
                        if not (isinstance(n, int) and n == 0):
                            act.wait_ge(down, n)
                        upper_d(n + 1, t + 1, 1 - u)

                upper_gu(0, 0, 0)
                upper_d(0, 0, 0)
                each(act, step)
                n4.root(act)

            @block.gpsimd
            def _(pool):
                def lower_gu(n, t, u):
                    for c in range(2):
                        pool.wait_ge(guh, 2 * n + c + 1)
                        pool.tensor_tensor(w_l[u][c][:], tile(t, c), w_h[u][c][:].bitcast(F32), ALU.subtract).then_inc(gul, 1)

                def lower_d(n, t, u):
                    pool.wait_ge(dh, n + 1)
                    pool.tensor_tensor(w_l[u][2][:], tile(t, 2), w_h[u][2][:].bitcast(F32), ALU.subtract).then_inc(dl, 1)

                def step(half, n, t, u):
                    if not last_step(n):
                        lower_gu(n + 1, t + 1, 1 - u)
                        lower_d(n + 1, t + 1, 1 - u)

                lower_gu(0, 0, 0)
                lower_d(0, 0, 0)
                each(pool, step)

            @block.vector
            def _(dve):
                def finish(half):
                    dve.wait_ge(down, (half + 1) * IT)
                    for j in range(4):
                        x = keep.x[:, 4 * half + j, :]
                        dve.tensor_tensor(x, pd[j][:], x, ALU.add).then_inc(fin, 1)
                        dve.wait_ge(fin, 4 * half + j + 1)
                        n4.stats(dve, 4 * half + j, x)

                def step(half, n, t, u):
                    dve.wait_ge(ex_ok, n + 1)
                    dve.tensor_scalar(den[:], ex[:], 1.0, None, ALU.add).then_inc(den_ok, 1)
                    dve.wait_ge(den_ok, n + 1)
                    dve.reciprocal(den[:], den[:]).then_inc(rec_ok, 1)
                    dve.wait_ge(rec_ok, n + 1)
                    dve.tensor_tensor(act_f[:], pg[u][:], den[:], ALU.mult).then_inc(sil_ok, 1)
                    dve.wait_ge(sil_ok, n + 1)
                    dve.wait_ge(gu, 2 * n + 2)
                    dve.tensor_tensor(act_f[:], pu[u][:], act_f[:], ALU.mult).then_inc(af_ok, 1)
                    dve.wait_ge(ah_ok, n + 1)
                    dve.tensor_tensor(a_l[u][:], act_f[:], a_h[u][:].bitcast(F32), ALU.subtract).then_inc(al_ok, 1)
                    if isinstance(n, int) and n == IT:
                        finish(0)

                each(dve, step)
                finish(1)
                n4.variance(dve)
                n4.inverse(dve)
                for j in range(ST):
                    n4.apply(dve, j, keep.x[:, j, :])


class Kept:
    pass


def program(nc, io, out, upto=9):
    with ExitStack() as ctx:
        al = Alloc(nc, ctx)
        keep = Kept()
        keep.x = al.sb("x_tok", [P, ST, D])
        keep.ident, keep.ident_b = al.sb("ident", [P, P]), al.sb("ident_b", [P, P], BF16)
        keep.mask, keep.mask_t = al.sb("mask", [P, P], BF16), al.sb("mask_t", [P, P], BF16)
        with ExitStack() as layer0:
            a0 = Alloc(nc, layer0)
            keep.cos, keep.sin = a0.sb("cos", [P, S]), a0.sb("sin", [P, S])
            keep.cqa_h, keep.cqa_l = a0.sb("cqa_h", [P, S], F32R), a0.sb("cqa_l", [P, S], F32R)
            keep.cqb_hh, keep.cqb_l = a0.sb("cqb_hh", [P, S], F32R), a0.sb("cqb_l", [64, S], F32R)
            keep.k_h, keep.k_l = a0.sb("k_h", [P, S], F32R), a0.sb("k_l", [P, S], F32R)
            keep.ckv = a0.sb("ckv", [P, ST, KVL])
            stage_latent(nc, io, keep)
            if upto >= 1:
                stage_mla(nc, io, keep)
        with ExitStack() as layer1:
            a1 = Alloc(nc, layer1)
            keep.q = a1.sb("l1_q", [P, ST, D])
            keep.gated_early = a1.sb("gated_early", [P, D // P, 3, D])
            keep.wqkv = keep.gated_early[:].rearrange("p t c d -> p (t c) d")
            keep.gated_in = [a1.sem(f"gated_in{i}") for i in range(1 + (IT - len(EARLY)) // 2)]
            keep.wo_f, keep.wo_in = a1.sb("wo_f", [P, DK, D]), a1.sem("l1_wo_in")
            keep.attn = keep.q
            with ExitStack() as heads:
                a2 = Alloc(nc, heads)
                keep.k, keep.v = (a2.sb("l1_" + n, [P, ST, D]) for n in "kv")
                keep.qx, keep.kx = (a2.sb(n, [P, ST, HG, 64], F32R) for n in ("qx", "kx"))
                keep.alibi_in = a2.sem("alibi_in")
                with ExitStack() as proj:
                    a3 = Alloc(nc, proj)
                    keep.qk_ln = a3.sb("qk_ln", [P, 4, D])
                    keep.wqkv_in, keep.ln_in = a3.sem("wqkv_in"), a3.sem("ln_in")
                    if upto >= 2:
                        stage_route(nc, io, keep)
                    if upto >= 3:
                        stage_qkv(nc, io, keep)
                if upto >= 3:
                    stage_alibi(nc, io, keep)
            if upto >= 3:
                stage_gated(nc, io, keep, upto)
        with ExitStack() as last:
            stored = Alloc(nc, last).sem("stored")
            with nc.Block() as block:

                @block.sync
                def _(sp):
                    sp.dma_start(out.rearrange("b (j p) d -> p (b j) d", p=P), keep.x[:]).then_inc(stored, 16)
                    sp.wait_ge(stored, 16)


_NAMES = {n.split("_", 2)[2] if n.startswith("L0_attn") else n: n for n in [
    "L0_attn_w_q_down", "L0_attn_w_q_up_nope", "L0_attn_w_q_up_rope", "L0_attn_w_kv_down", "L0_attn_w_k_rope",
    "L0_attn_w_uk", "L0_attn_w_uv", "L0_attn_w_out", "L0_ffn_W", "L0_ffn_b", "L0_ffn_A", "L0_ffn_B",
    "L0_ffn_gate_w", "L0_ffn_gate_b", "L1_attn_w_qkv", "L1_attn_q_ln_w", "L1_attn_q_ln_b", "L1_attn_k_ln_w",
    "L1_attn_k_ln_b", "L1_attn_w_out", "L1_ffn_ln_w", "L1_ffn_gate_w", "L1_ffn_up_w", "L1_ffn_down_w"]}


def layout(inputs):
    arrays = {"x": np.ascontiguousarray(inputs["L0_attn_hidden_states"])}
    for short, name in _NAMES.items():
        arrays[short] = np.ascontiguousarray(inputs[name])
    arrays["cos"], arrays["sin"] = rope_tables()
    arrays["alibi_q"], arrays["alibi_k"] = alibi_columns()
    return arrays


def kernel(**inputs):
    import concourse.bacc as bacc
    from concourse.bass_utils import run_bass_kernel_spmd

    nc = bacc.Bacc("TRN2", target_bir_lowering=False, num_devices=1)
    arrays = layout(inputs)
    io = {n: nc.dram_tensor(f"in_{n}", a.shape, mybir.dt.from_np(a.dtype), kind="ExternalInput").ap()
          for n, a in arrays.items()}
    out = nc.dram_tensor("out_0_dram", (1, S, D), F32, kind="ExternalOutput").ap()
    program(nc, io, out)
    r = run_bass_kernel_spmd(nc, [{f"in_{n}": a for n, a in arrays.items()}], core_ids=[0])
    return r.results[0]["out_0_dram"]
```
